# Optimizing a Trainium2 kernel written in Bass

```python
import numpy as np
import jax
import jax.numpy as jnp

def _softmax(x, axis=-1):
    return jax.nn.softmax(x, axis=axis)

def _gelu(x):
    return jax.nn.gelu(x, approximate=True)

def _silu(x):
    return jax.nn.silu(x)

def _sigmoid(x):
    return jax.nn.sigmoid(x)

def _layernorm(x, axis=-1, eps=1e-05):
    m = jnp.mean(x, axis=axis, keepdims=True)
    v = jnp.var(x, axis=axis, keepdims=True)
    return (x - m) / jnp.sqrt(v + eps)

def _scatter_add(tgt, idx, src, axis=0):
    return tgt.at[idx].add(src)

def _segment_sum(src, seg, n):
    return jax.ops.segment_sum(src, seg, n)
kernel_name = 'mk_macaron_d2_jaxref_r8_192c4a'

def setup_inputs(seed: int=0):
    np.random.seed(seed)
    _w = jnp.asarray

    def _L0_attn_setup():
        import jax, jax.numpy as jnp
        import numpy as np
        D_MODEL = 128
        NUM_HEADS = 16
        HEAD_DIM = D_MODEL // NUM_HEADS
        key = jax.random.key(seed)
        ks = jax.random.split(key, 7)
        B, T, C = (4, 256, D_MODEL)
        s = 1.0 / np.sqrt(C)
        return {'x': jax.random.normal(ks[0], (B, T, C), dtype=jnp.float32), 'ln_gamma': jnp.ones((C,), dtype=jnp.float32), 'ln_beta': jnp.zeros((C,), dtype=jnp.float32), 'w_qkv': jax.random.normal(ks[1], (C, 3 * C), dtype=jnp.float32) * s, 'b_qkv': jnp.zeros((3 * C,), dtype=jnp.float32), 'w_out': jax.random.normal(ks[2], (C, C), dtype=jnp.float32) * s, 'b_out': jnp.zeros((C,), dtype=jnp.float32)}
    _L0_attn_in = _L0_attn_setup()

    def _L0_ffn_setup():
        import jax, jax.numpy as jnp
        import numpy as np
        from jax import lax
        H = 128
        E = 8
        E_MLP = E - 4
        TOP_K = 2
        I = 64
        KC = 4
        SHARED_SCALE = 1.0
        key = jax.random.key(seed)
        ks = jax.random.split(key, 8)
        B, S = (4, 512)
        s_h = 1.0 / np.sqrt(H)
        s_i = 1.0 / np.sqrt(I)
        return {'hidden_states': jax.random.normal(ks[0], (B, S, H), dtype=jnp.float32), 'Wr': jax.random.normal(ks[1], (H, E), dtype=jnp.float32) * s_h, 'router_bias': jnp.zeros((E,), dtype=jnp.float32), 'Wg': jax.random.normal(ks[2], (E_MLP, H, I), dtype=jnp.float32) * s_h, 'Wu': jax.random.normal(ks[3], (E_MLP, H, I), dtype=jnp.float32) * s_h, 'Wd': jax.random.normal(ks[4], (E_MLP, I, H), dtype=jnp.float32) * s_i, 'conv_w': jax.random.normal(ks[5], (KC, 1, H), dtype=jnp.float32) * (1.0 / np.sqrt(KC)), 'conv_b': jnp.zeros((H,), dtype=jnp.float32)}
    _L0_ffn_in = _L0_ffn_setup()

    def _L1_attn_setup():
        import jax, jax.numpy as jnp
        import numpy as np
        import math
        D_MODEL, N_HEADS, D_K, D_C, D_HR = (128, 8, 128, 32, 32)
        B, S = (4, 256)
        key = jax.random.key(seed)
        ks = jax.random.split(key, 17)

        def lin(k, fan_in, fan_out):
            lim = 1.0 / math.sqrt(fan_in)
            kw, kb = jax.random.split(k)
            W = jax.random.uniform(kw, (fan_in, fan_out), jnp.float32, -lim, lim)
            b = jax.random.uniform(kb, (fan_out,), jnp.float32, -lim, lim)
            return (W, b)
        W_DQ, b_DQ = lin(ks[0], D_MODEL, D_C)
        W_UQ, b_UQ = lin(ks[1], D_C, N_HEADS * D_K)
        W_DKV, b_DKV = lin(ks[2], D_MODEL, D_C)
        W_UK, b_UK = lin(ks[3], D_C, N_HEADS * D_K)
        W_UV, b_UV = lin(ks[4], D_C, N_HEADS * D_K)
        W_QR, b_QR = lin(ks[5], D_C, N_HEADS * D_HR)
        W_KR, b_KR = lin(ks[6], D_MODEL, D_HR)
        W_O, b_O = lin(ks[7], N_HEADS * D_K, D_MODEL)
        h_t = jax.random.normal(ks[8], (B, S, D_MODEL), jnp.float32)
        return {'h_t': h_t, 'W_DQ': W_DQ, 'b_DQ': b_DQ, 'W_UQ': W_UQ, 'b_UQ': b_UQ, 'W_DKV': W_DKV, 'b_DKV': b_DKV, 'W_UK': W_UK, 'b_UK': b_UK, 'W_UV': W_UV, 'b_UV': b_UV, 'W_QR': W_QR, 'b_QR': b_QR, 'W_KR': W_KR, 'b_KR': b_KR, 'W_O': W_O, 'b_O': b_O}
    _L1_attn_in = _L1_attn_setup()

    def _L1_ffn_setup():
        import jax, jax.numpy as jnp
        import numpy as np
        H = 128
        E = 64
        K = 8
        G = 8
        TOPK_GROUP = 4
        I_MOE = 64
        I_SHARED = 256
        SCALE = 2.5

        def relu2(x):
            return jnp.square(jax.nn.relu(x))

        def _route(xf, router_w, correction_bias):
            T = xf.shape[0]
            logits = xf @ router_w.T
            scores = jax.nn.sigmoid(logits)
            sfc = scores + correction_bias[None, :]
            grp = sfc.reshape(T, G, E // G)
            top2, _ = jax.lax.top_k(grp, 2)
            group_scores = top2.sum(-1)
            _, gidx = jax.lax.top_k(group_scores, TOPK_GROUP)
            gmask = jnp.zeros((T, G), sfc.dtype).at[jnp.arange(T)[:, None], gidx].set(1.0)
            emask = jnp.repeat(gmask, E // G, axis=1)
            masked = jnp.where(emask > 0, sfc, 0.0)
            _, tidx = jax.lax.top_k(masked, K)
            tw = jnp.take_along_axis(scores, tidx, axis=1)
            tw = tw / (tw.sum(-1, keepdims=True) + 1e-20)
            return (tidx, tw * SCALE)
        key = jax.random.key(seed)
        ks = jax.random.split(key, 7)
        x = jax.random.normal(ks[0], (2, 128, H), dtype=jnp.float32)
        router_w = jax.random.normal(ks[1], (E, H), dtype=jnp.float32) * 0.02
        correction_bias = jax.random.normal(ks[2], (E,), dtype=jnp.float32) * 0.01
        up_w = jax.random.normal(ks[3], (E, H, I_MOE), dtype=jnp.float32) * 0.02
        down_w = jax.random.normal(ks[4], (E, I_MOE, H), dtype=jnp.float32) * 0.02
        shared_up_w = jax.random.normal(ks[5], (H, I_SHARED), dtype=jnp.float32) * 0.02
        shared_down_w = jax.random.normal(ks[6], (I_SHARED, H), dtype=jnp.float32) * 0.02
        return {'x': x, 'router_w': router_w, 'correction_bias': correction_bias, 'up_w': up_w, 'down_w': down_w, 'shared_up_w': shared_up_w, 'shared_down_w': shared_down_w}
    _L1_ffn_in = _L1_ffn_setup()
    _d = {'L0_attn_x': _L0_attn_in['x'], 'L0_attn_ln_gamma': _L0_attn_in['ln_gamma'], 'L0_attn_ln_beta': _L0_attn_in['ln_beta'], 'L0_attn_w_qkv': _L0_attn_in['w_qkv'], 'L0_attn_b_qkv': _L0_attn_in['b_qkv'], 'L0_attn_w_out': _L0_attn_in['w_out'], 'L0_attn_b_out': _L0_attn_in['b_out'], 'L0_ffn_Wr': _L0_ffn_in['Wr'], 'L0_ffn_router_bias': _L0_ffn_in['router_bias'], 'L0_ffn_Wg': _L0_ffn_in['Wg'], 'L0_ffn_Wu': _L0_ffn_in['Wu'], 'L0_ffn_Wd': _L0_ffn_in['Wd'], 'L0_ffn_conv_w': _L0_ffn_in['conv_w'], 'L0_ffn_conv_b': _L0_ffn_in['conv_b'], 'L1_attn_W_DQ': _L1_attn_in['W_DQ'], 'L1_attn_b_DQ': _L1_attn_in['b_DQ'], 'L1_attn_W_UQ': _L1_attn_in['W_UQ'], 'L1_attn_b_UQ': _L1_attn_in['b_UQ'], 'L1_attn_W_DKV': _L1_attn_in['W_DKV'], 'L1_attn_b_DKV': _L1_attn_in['b_DKV'], 'L1_attn_W_UK': _L1_attn_in['W_UK'], 'L1_attn_b_UK': _L1_attn_in['b_UK'], 'L1_attn_W_UV': _L1_attn_in['W_UV'], 'L1_attn_b_UV': _L1_attn_in['b_UV'], 'L1_attn_W_QR': _L1_attn_in['W_QR'], 'L1_attn_b_QR': _L1_attn_in['b_QR'], 'L1_attn_W_KR': _L1_attn_in['W_KR'], 'L1_attn_b_KR': _L1_attn_in['b_KR'], 'L1_attn_W_O': _L1_attn_in['W_O'], 'L1_attn_b_O': _L1_attn_in['b_O'], 'L1_ffn_router_w': _L1_ffn_in['router_w'], 'L1_ffn_correction_bias': _L1_ffn_in['correction_bias'], 'L1_ffn_up_w': _L1_ffn_in['up_w'], 'L1_ffn_down_w': _L1_ffn_in['down_w'], 'L1_ffn_shared_up_w': _L1_ffn_in['shared_up_w'], 'L1_ffn_shared_down_w': _L1_ffn_in['shared_down_w']}
    _x0 = _d['L0_attn_x']
    _d['L0_attn_x'] = jax.random.normal(jax.random.fold_in(jax.random.key(seed), 1), (8, 256, 128), dtype=_x0.dtype)
    del _x0
    return _d

def reference(L0_attn_x, L0_attn_ln_gamma, L0_attn_ln_beta, L0_attn_w_qkv, L0_attn_b_qkv, L0_attn_w_out, L0_attn_b_out, L0_ffn_Wr, L0_ffn_router_bias, L0_ffn_Wg, L0_ffn_Wu, L0_ffn_Wd, L0_ffn_conv_w, L0_ffn_conv_b, L1_attn_W_DQ, L1_attn_b_DQ, L1_attn_W_UQ, L1_attn_b_UQ, L1_attn_W_DKV, L1_attn_b_DKV, L1_attn_W_UK, L1_attn_b_UK, L1_attn_W_UV, L1_attn_b_UV, L1_attn_W_QR, L1_attn_b_QR, L1_attn_W_KR, L1_attn_b_KR, L1_attn_W_O, L1_attn_b_O, L1_ffn_router_w, L1_ffn_correction_bias, L1_ffn_up_w, L1_ffn_down_w, L1_ffn_shared_up_w, L1_ffn_shared_down_w):

    def _L0_attn_ref(x, ln_gamma, ln_beta, w_qkv, b_qkv, w_out, b_out):
        import jax, jax.numpy as jnp
        import numpy as np
        D_MODEL = 128
        NUM_HEADS = 16
        HEAD_DIM = D_MODEL // NUM_HEADS
        B, T, C = x.shape
        residual = x
        mu = jnp.mean(x, axis=-1, keepdims=True)
        var = jnp.var(x, axis=-1, keepdims=True)
        h = (x - mu) * jax.lax.rsqrt(var + 1e-05) * ln_gamma + ln_beta
        qkv = (h @ w_qkv + b_qkv).reshape(B, T, 3, NUM_HEADS, HEAD_DIM)
        qkv = jnp.transpose(qkv, (2, 0, 3, 1, 4))
        q, k, v = (qkv[0], qkv[1], qkv[2])
        scores = jnp.einsum('bhqd,bhkd->bhqk', q, k) / np.sqrt(HEAD_DIM)
        attn = jax.nn.softmax(scores, axis=-1)
        out = jnp.einsum('bhqk,bhkd->bhqd', attn, v)
        out = jnp.transpose(out, (0, 2, 1, 3)).reshape(B, T, C)
        out = out @ w_out + b_out
        return residual + out

    def _L0_ffn_ref(hidden_states, Wr, router_bias, Wg, Wu, Wd, conv_w, conv_b):
        import jax, jax.numpy as jnp
        import numpy as np
        from jax import lax
        H = 128
        E = 8
        E_MLP = E - 4
        TOP_K = 2
        I = 64
        KC = 4
        SHARED_SCALE = 1.0
        B, S, Hd = hidden_states.shape
        T = B * S
        x = hidden_states.reshape(T, Hd)
        scores = jax.nn.sigmoid(x @ Wr)
        _, idx = lax.top_k(scores + router_bias, TOP_K)
        w = jnp.take_along_axis(scores, idx, axis=-1)
        w = w / (jnp.sum(w, axis=-1, keepdims=True) + 1e-09)
        cw = jnp.zeros((T, E), dtype=x.dtype).at[jnp.arange(T)[:, None], idx].add(w)
        g = jnp.einsum('th,ehi->tei', x, Wg)
        u = jnp.einsum('th,ehi->tei', x, Wu)
        hid = jax.nn.silu(g) * u
        mlp_out = jnp.einsum('tei,eih->teh', hid, Wd)
        routed = jnp.einsum('te,teh->th', cw[:, :E_MLP], mlp_out)
        routed = routed + cw[:, E_MLP:E_MLP + 1] * x
        routed = routed + cw[:, E_MLP + 2:E_MLP + 3] * x
        routed = routed + cw[:, E_MLP + 3:E_MLP + 4] * jax.nn.relu(x)
        routed = routed.reshape(B, S, Hd)
        shared = lax.conv_general_dilated(hidden_states, conv_w, window_strides=(1,), padding=[(KC - 1, 0)], dimension_numbers=('NHC', 'HIO', 'NHC'), feature_group_count=Hd) + conv_b
        return routed + SHARED_SCALE * shared

    def _L1_attn_ref(h_t, W_DQ, b_DQ, W_UQ, b_UQ, W_DKV, b_DKV, W_UK, b_UK, W_UV, b_UV, W_QR, b_QR, W_KR, b_KR, W_O, b_O):
        import jax, jax.numpy as jnp
        import numpy as np
        import math
        D_MODEL, N_HEADS, D_K, D_C, D_HR = (128, 8, 128, 32, 32)
        B, S = (4, 256)
        b, s, _ = h_t.shape
        c_q = h_t @ W_DQ + b_DQ
        c_kv = h_t @ W_DKV + b_DKV
        q_c = (c_q @ W_UQ + b_UQ).reshape(b, s, N_HEADS, D_K).transpose(0, 2, 1, 3)
        k_c = (c_kv @ W_UK + b_UK).reshape(b, s, N_HEADS, D_K).transpose(0, 2, 1, 3)
        v_c = (c_kv @ W_UV + b_UV).reshape(b, s, N_HEADS, D_K).transpose(0, 2, 1, 3)
        q_r = (c_q @ W_QR + b_QR).reshape(b, s, N_HEADS, D_HR).transpose(0, 2, 1, 3)
        k_r = (h_t @ W_KR + b_KR)[:, None, :, :]
        k_r = jnp.broadcast_to(k_r, (b, N_HEADS, s, D_HR))
        q = jnp.concatenate([q_c, q_r], axis=-1)
        k = jnp.concatenate([k_c, k_r], axis=-1)
        scale = 1.0 / math.sqrt(D_K + D_HR)
        scores = jnp.einsum('bhsd,bhtd->bhst', q, k) * scale
        attn = jax.nn.softmax(scores, axis=-1)
        o = jnp.einsum('bhst,bhtd->bhsd', attn, v_c)
        o = o.transpose(0, 2, 1, 3).reshape(b, s, N_HEADS * D_K)
        return o @ W_O + b_O

    def _L1_ffn_ref(x, router_w, correction_bias, up_w, down_w, shared_up_w, shared_down_w):
        import jax, jax.numpy as jnp
        import numpy as np
        H = 128
        E = 64
        K = 8
        G = 8
        TOPK_GROUP = 4
        I_MOE = 64
        I_SHARED = 256
        SCALE = 2.5

        def relu2(x):
            return jnp.square(jax.nn.relu(x))

        def _route(xf, router_w, correction_bias):
            T = xf.shape[0]
            logits = xf @ router_w.T
            scores = jax.nn.sigmoid(logits)
            sfc = scores + correction_bias[None, :]
            grp = sfc.reshape(T, G, E // G)
            top2, _ = jax.lax.top_k(grp, 2)
            group_scores = top2.sum(-1)
            _, gidx = jax.lax.top_k(group_scores, TOPK_GROUP)
            gmask = jnp.zeros((T, G), sfc.dtype).at[jnp.arange(T)[:, None], gidx].set(1.0)
            emask = jnp.repeat(gmask, E // G, axis=1)
            masked = jnp.where(emask > 0, sfc, 0.0)
            _, tidx = jax.lax.top_k(masked, K)
            tw = jnp.take_along_axis(scores, tidx, axis=1)
            tw = tw / (tw.sum(-1, keepdims=True) + 1e-20)
            return (tidx, tw * SCALE)
        B, S, Hd = x.shape
        xf = x.reshape(-1, Hd)
        T = xf.shape[0]
        tidx, tw = _route(xf.astype(jnp.float32), router_w, correction_bias)
        combine = jnp.zeros((T, E), xf.dtype).at[jnp.arange(T)[:, None], tidx].add(tw.astype(xf.dtype))

        def body(acc, ew):
            wu, wd, c = ew
            return (acc + c[:, None] * (relu2(xf @ wu) @ wd), None)
        routed, _ = jax.lax.scan(body, jnp.zeros_like(xf), (up_w, down_w, combine.T))
        shared = relu2(xf @ shared_up_w) @ shared_down_w
        return (routed + shared).reshape(B, S, Hd)
    x = L0_attn_x
    x = x + 0.5 * _L0_ffn_ref(_layernorm(x, axis=-1), L0_ffn_Wr, L0_ffn_router_bias, L0_ffn_Wg, L0_ffn_Wu, L0_ffn_Wd, L0_ffn_conv_w, L0_ffn_conv_b)
    x = x + _L0_attn_ref(_layernorm(x, axis=-1), L0_attn_ln_gamma, L0_attn_ln_beta, L0_attn_w_qkv, L0_attn_b_qkv, L0_attn_w_out, L0_attn_b_out)
    x = x + 0.5 * _L0_ffn_ref(_layernorm(x, axis=-1), L0_ffn_Wr, L0_ffn_router_bias, L0_ffn_Wg, L0_ffn_Wu, L0_ffn_Wd, L0_ffn_conv_w, L0_ffn_conv_b)
    x = x + 0.5 * _L1_ffn_ref(_layernorm(x, axis=-1), L1_ffn_router_w, L1_ffn_correction_bias, L1_ffn_up_w, L1_ffn_down_w, L1_ffn_shared_up_w, L1_ffn_shared_down_w)
    x = x + _L1_attn_ref(_layernorm(x, axis=-1), L1_attn_W_DQ, L1_attn_b_DQ, L1_attn_W_UQ, L1_attn_b_UQ, L1_attn_W_DKV, L1_attn_b_DKV, L1_attn_W_UK, L1_attn_b_UK, L1_attn_W_UV, L1_attn_b_UV, L1_attn_W_QR, L1_attn_b_QR, L1_attn_W_KR, L1_attn_b_KR, L1_attn_W_O, L1_attn_b_O)
    x = x + 0.5 * _L1_ffn_ref(_layernorm(x, axis=-1), L1_ffn_router_w, L1_ffn_correction_bias, L1_ffn_up_w, L1_ffn_down_w, L1_ffn_shared_up_w, L1_ffn_shared_down_w)
    return x

_drawn_inputs = setup_inputs


def setup_inputs(seed=0):
    import zlib

    import numpy as np

    out = dict(_drawn_inputs(seed))
    spreads = {'L0_attn_ln_gamma': (1.0, 0.539),
     'L0_attn_ln_beta': (0.0, 0.1),
     'L0_attn_b_qkv': (0.0, 0.1),
     'L0_attn_b_out': (0.0, 0.1),
     'L0_ffn_router_bias': (0.0, 0.1),
     'L0_ffn_conv_b': (0.0, 0.1)}
    factors = {'L1_attn_W_DQ': 8.0,
     'L1_attn_b_DQ': 8.0,
     'L1_attn_W_UQ': 8.0,
     'L1_attn_b_UQ': 8.0,
     'L1_attn_W_DKV': 7.654,
     'L1_attn_b_DKV': 8.0,
     'L1_attn_W_UK': 8.0,
     'L1_attn_b_UK': 64.0,
     'L1_attn_W_UV': 6.144,
     'L1_attn_W_QR': 8.0,
     'L1_attn_b_QR': 8.0,
     'L1_attn_W_KR': 8.0,
     'L1_attn_b_KR': 64.0,
     'L1_attn_b_O': 8.0,
     'L1_ffn_router_w': 8.0,
     'L1_ffn_correction_bias': 8.0,
     'L1_ffn_up_w': 8.0,
     'L1_ffn_down_w': 8.0,
     'L1_ffn_shared_up_w': 8.0,
     'L1_ffn_shared_down_w': 8.0,
     'L1_attn_b_UV': 3.699}
    for name, (base, spread) in spreads.items():
        noise = np.random.default_rng([zlib.crc32(name.encode()), seed]).standard_normal(out[name].shape)
        drawn = base * np.exp(spread * noise) if base else spread * noise
        out[name] = jnp.asarray(drawn.astype(out[name].dtype))
    for name, factor in factors.items():
        out[name] = (out[name] * factor).astype(out[name].dtype)
    return out
```

```python
from contextlib import ExitStack

import concourse.bass as bass
from concourse import mybir

ALU = mybir.AluOpType
ACT = mybir.ActivationFunctionType
AX = mybir.AxisListType
F32 = mybir.dt.float32
F32R = mybir.dt.float32r

P = 128
D = 128
LN_EPS = 1e-5
PAD_LOW = -3e38
TAKEN = -2e38
LOW = -1e30
LAST_STAGE = 6
WIDE = 96


class Count:

    def __init__(self, sem, per, base=0):
        self.sem, self.per, self.base = sem, per, base

    def at(self, base):
        return Count(self.sem, self.per, base)

    def wait(self, eng, b, k):
        k = k + self.base * self.per
        if isinstance(b, int):
            if b * self.per + k > 0:
                eng.wait_ge(self.sem, b * self.per + k)
        else:
            assert self.per + k > 0
            eng.wait_ge(self.sem, b * self.per + k)

    def up(self, ins):
        return ins.then_inc(self.sem, 1)


def macaron_kernel(nc, I, out):
    B, T, _ = I["L0_attn_x"].shape
    NT = T // P
    E0, IM0 = I["L0_ffn_Wg"].shape[0], I["L0_ffn_Wg"].shape[2]
    R0 = I["L0_ffn_Wr"].shape[1]
    TAPS = I["L0_ffn_conv_w"].shape[0]
    NC0 = E0 * IM0 // P
    E1, _, IM1 = I["L1_ffn_up_w"].shape
    NG1, TOPG, TOPK = 8, 4, 8
    NC1 = E1 * IM1 // P
    NSH = I["L1_ffn_shared_up_w"].shape[1] // P
    PAIRS = NC1 // 2
    SLOTS = PAIRS + NSH
    H0, DH0 = 16, 8
    H1, DC, DR = 8, 32, 32
    DK = 128
    assert T == 256 and NT == 2 and SLOTS % 6 == 0 and H0 * DH0 == D and NC0 == 2 and TAPS == 4

    with ExitStack() as ctx:
        def sb(name, shape, dt=F32):
            return ctx.enter_context(nc.sbuf_tensor(name, shape, dt))

        def sem(name):
            return ctx.enter_context(nc.semaphore(name))

        def count(name, per=1):
            return Count(sem(name), per)

        bank = [ctx.enter_context(nc.psum_tensor(f"bank{i}", [P, 512], F32)) for i in range(8)]

        ident = sb("ident", [P, P])
        neghalf = sb("neghalf", [P, NT])
        eps2 = sb("eps2", [P, NT])
        cell = sb("cell", [P, 1])
        cell_pool = sb("cell_pool", [P, 2, NT])
        head_mask = sb("head_mask", [P, 4])
        sel_small = sb("sel_small", [P, 64])
        sel_exp = sb("sel_exp", [P, 64, 64], F32R)
        sel_row = sb("sel_row", [P, 4, P], F32R)

        x = sb("x", [P, B, NT, D])
        xt = sb("xt", [P, B, TAPS - 1 + T])
        xts = sb("xts", [P, T])
        xn = sb("xn", [P, NT, D])
        xh = sb("xh", [P, NT, D])
        st = sb("st", [P, NT, 6])
        mv = sb("mv", [P, NT, 2])
        veps = sb("veps", [P, NT])
        rstd = sb("rstd", [P, NT])
        st2 = sb("st2", [P, NT, 6])
        mv2 = sb("mv2", [P, NT, 2])
        veps2 = sb("veps2", [P, NT])
        rstd2 = sb("rstd2", [P, NT])

        area = sb("area", [P, 4096])

        def part(at, *shape, rows=P):
            n = 1
            for k in shape:
                n *= k
            names = "abcd"[:len(shape)]
            return area[0:rows, at:at + n].rearrange(f"p ({' '.join(names)}) -> p {' '.join(names)}",
                                                     **dict(zip(names, shape)))

        wr0 = sb("wr0", [P, R0])
        rb0 = sb("rb0", [P, R0])
        wg0 = sb("wg0", [P, E0, IM0])
        wu0 = sb("wu0", [P, E0, IM0])
        wd0 = sb("wd0", [P, NC0, D])
        cw0 = sb("cw0", [P, TAPS])
        cb0 = sb("cb0", [P, 1])
        gam = sb("gam", [P, 1])
        bet = sb("bet", [P, 1])
        wqkv = sb("wqkv", [P, 3 * D])
        wq4 = sb("wq4", [P, 4, 4, 32])
        wk4 = sb("wk4", [P, 4, 4, 32])
        bq4 = sb("bq4", [P, 4])
        bk4 = sb("bk4", [P, 4])
        bvr = sb("bvr", [P, D])
        wo0 = sb("wo0", [P, D])
        bo0 = sb("bo0", [P, D])
        wr1 = sb("wr1", [P, E1])
        wr1t = sb("wr1t", [E1, D])
        cb1 = sb("cb1", [P, E1])
        wup = sb("wup", [P, E1, IM1])
        wdn = sb("wdn", [P, NC1, D])
        wsu = sb("wsu", [P, NSH * P])
        wsd = sb("wsd", [P, NSH, D])
        uq, uk, uv = (part(i * H1 * DK, H1 * DK, rows=DC + 1) for i in range(3))
        qr = sb("qr", [DC + 1, H1, DR])
        uqt = sb("uqt", [P, H1, DC + 1])
        ukt = sb("ukt", [P, H1, DC + 1])
        uvt = sb("uvt", [P, H1, DC + 1])
        wo1 = sb("wo1", [P, H1, D])
        wdq = sb("wdq", [P, DC])
        bdq = sb("bdq", [DC, 1])
        wkk = sb("wkk", [P, 2, DC + DR])
        bkk = sb("bkk", [P, 1])
        bdkvr = sb("bdkvr", [P, DC])
        bo1r = sb("bo1r", [P, D])
        a1 = sb("a1", [P, H1, 2, DC + DR])
        acol = sb("acol", [P, H1])
        vo1 = sb("vo1", [P, 2, D])
        bvb = part(3 * H1 * DK, H1, P)
        bo1 = sb("bo1", [P, D])

        sc = sb("sc", [P, NT, E1])
        sfc = sb("sfc", [P, NT, E1])
        pad16 = sb("pad16", [P, NT, 16])
        top8 = sb("top8", [P, NT, 8])
        want8 = sb("want8", [P, NT, 8])
        want8g = sb("want8g", [P, NT, 8])
        hit16 = sb("hit16", [P, NT, 16])
        wsel = sb("wsel", [P, NT, E1])
        wsum = sb("wsum", [P, NT])
        wrec = sb("wrec", [P, NT])
        cwt = sb("cwt", [P, NT, E1])
        cc = sb("cc", [P, NT, P], F32R)
        k1 = sb("k1", [P, B, 2, T], F32R)
        ct = k1[:, :, 0, :]
        s46 = sb("s46", [P, NT])
        s46h = sb("s46h", [P, NT])
        c7h = sb("c7h", [P, NT])
        skip_u = sb("skip_u", [P, NT, D])
        skip_v = sb("skip_v", [P, NT, D])
        g_max = sb("g_max", [P, NT * NG1])
        g_eq = sb("g_eq", [P, NT, E1])
        g_cnt = sb("g_cnt", [P, NT * NG1])
        g_rest = sb("g_rest", [P, NT, E1])
        g_m2 = sb("g_m2", [P, NT * NG1])
        g_d = sb("g_d", [P, NT * NG1])
        g_d2 = sb("g_d2", [P, NT * NG1])
        g_m2b = sb("g_m2b", [P, NT * NG1])
        gmask = sb("gmask", [P, NT, NG1])
        masked = sb("masked", [P, NT, E1])
        hit64 = sb("hit64", [P, NT, E1])
        relu_h = part(0, 3, 512)
        hid = part(1536, 3, 512)
        relu_c = part(3072, 2, 512)
        outT = sb("outT", [P, T])
        silu_g = sb("silu_g", [P, 512])
        gu = sb("gu", [P, 512])
        hid0 = sb("hid0", [P, 512])
        conv = part(0, 4, T)

        q0 = sb("q0", [P, 4, T], F32R)
        k0 = sb("k0", [P, T], F32R)
        k0m = sb("k0m", [P, 2, 4, T], F32R)
        v0 = sb("v0", [P, B, NT, H0 * (DH0 + 1) + WIDE])
        v0h = v0[:, :, :, 0:H0 * (DH0 + 1)].rearrange("p b t (h d) -> p b t h d", h=H0)
        q1 = sb("q1", [P, 2, 4, T], F32R)
        k1s = sb("k1s", [P, 2, 2, T], F32R)
        cq = sb("cq", [P, B, T])
        cqs = sb("cqs", [P, T])
        v1 = sb("v1", [P, B, NT, WIDE])
        cst = sb("cst", [P, B, NT, H1])
        nm = sb("nm", [P, 2, NT, 4])
        msum = sb("msum", [P, NT, 4])
        shift = sb("shift", [P, 2, NT, 4])
        mt = sb("mt", [P, T], F32R)
        probs = part(0, 4, 512)
        rz = sb("rz", [P, 8])
        on = sb("on", [P, NT, H1 * DC])
        ots = sb("ots", [P, 512])

        x_in, w0_in, att0_in, pre1_in, moe_in = (sem(n) for n in ("x_in", "w0_in", "att0_in", "pre1_in", "moe_in"))
        stored = sem("stored")
        const_pool, const_dve = sem("const_pool"), sem("const_dve")
        pre_tr, pre_ev, pre_mm, pre_done = sem("pre_tr"), sem("pre_ev"), sem("pre_mm"), sem("pre_done")
        stats_c = count("stats", NT)
        mv_c = count("mean_var", NT)
        veps_c = count("var_eps")
        rstd_c = count("rstd")
        xn_c = count("xn", NT)
        xT_c = count("xT_psum")
        xts_c = count("xT_stage")
        xt_c = count("xT_all")
        x_done = count("x_done")
        logit_c = count("logits")
        score_c = count("scores")
        R_OPS0, R_OPS1 = 21, 29
        route0_c = count("route0", R_OPS0)
        route1_c = count("route1", R_OPS1)
        ccT_c = count("ccT_psum")
        ct_c = count("ct_all")
        gate_c, up0_c, cb0_c = count("gate_psum"), count("up_psum"), count("comb0_psum")
        silu_c, gu_c, hid0_c = count("silu"), count("gate_up"), count("hid0")
        conv_c = count("conv", 4)
        down0_c, outT0_c, back0_c = count("down0_psum"), count("outT0"), count("back0_psum")
        up1_c = count("up1_psum", SLOTS)
        cb1_c = count("comb1_psum", PAIRS)
        relu_c_ = count("relu1", SLOTS)
        rc_c = count("relu_comb", PAIRS)
        hid1_c = count("hid1", SLOTS)
        down1_c = count("down1_psum", SLOTS)
        outT1_c, back1_c = count("outT1"), count("back1_psum")

        def make_attention_counts(tag, ng):
            c = {}
            for name, per in (("q_mm", 1), ("k_mm", 1), ("q_hi", 1), ("q_hi2", 1), ("k_hi", 1), ("q_lo", 1), ("q_lo2", 1),
                              ("k_lo", 2), ("k_mask", 4), ("s_mm", 4), ("row_max", 4), ("shift", 2), ("mT", 1),
                              ("mt_rows", 2), ("t_mm", 4), ("exp", 4), ("pv", 4), ("recip", 1), ("norm", 1)):
                c[name] = count(f"{tag}_{name}", per * ng)
            return c

        A0C = make_attention_counts("a0", 4)
        A1C = make_attention_counts("a1", 2)
        for c, tag in ((A0C, "a0"), (A1C, "a1")):
            for name in ("v_mm", "v_ev", "onT", "ots", "out_mm", "x_add"):
                c[name] = count(f"{tag}_{name}")
        stats2_c = count("stats2", NT)
        mv2_c = count("mean_var2", NT)
        veps2_c = count("var_eps2")
        rstd2_c = count("rstd2")
        xh_c = count("xh", NT)
        x_xn_c = count("x_plus_xn")
        kk_mm_c, kk_hi_c, kk_lo_c, cq_c, cqs_c = (count(n) for n in ("kk_mm", "kk_hi", "kk_lo", "cq_ev", "cq_stage"))
        cst_c = count("cst_ev")

        block = ctx.enter_context(nc.Block())

        def batches(eng, body, lead):
            body(0)
            with eng.Fori(1, B - lead) as b:
                body(b)
            for b in range(B - lead, B):
                body(b)

        def hold(v, b, *waits):
            for c, k in waits:
                c.wait(v, b, k)
            if not isinstance(b, int):
                v.memset(cell[:], 0.0)

        def hold_pool(g, b, c, k, which=0):
            c.wait(g, b, k)
            if not isinstance(b, int):
                nc.gpsimd.tensor_tensor(cell_pool[:, which], neghalf[:], eps2[:], ALU.add)

        def exists(b):
            return not isinstance(b, int) or 0 <= b < B

        def ln_stats(v, b, ph):
            for t in range(NT):
                stats_c.up(v.bn_stats(st[:, t, :], x[:, b, t, :]))
            for t in range(NT):
                if t == 0:
                    hold(v, b, (stats_c.at(B * ph), NT), (rstd_c.at(B * ph), 0))
                mv_c.up(v.bn_aggr(mv[:, t, :], st[:, t, :]))

        def ln_rstd(g, b, ph):
            mv_c.at(B * ph).wait(g, b, NT)
            xn_c.at(B * ph).wait(g, b, 0)
            veps_c.up(nc.gpsimd.tensor_tensor(veps[:], mv[:, :, 1], eps2[:], ALU.add))
            veps_c.at(B * ph).wait(g, b, 1)
            rstd_c.up(nc.gpsimd.tensor_tensor(rstd[:], veps[:], neghalf[:], ALU.pow))

        def ln_xn(v, b, ph):
            rstd_c.at(B * ph).wait(v, b, 1)
            for t in range(NT):
                xn_c.up(v.tensor_scalar(xn[:, t, :], x[:, b, t, :], mv[:, t, 0:1], rstd[:, t:t + 1],
                                        ALU.subtract, ALU.mult))

        def x_transpose(pe, b, ph, src, ready):
            ready(pe, b)
            for t in range(NT):
                ins = pe.transpose(bank[7][:, t * P:(t + 1) * P], src[:, t, :], ident[:])
            xT_c.up(ins)

        def x_evacuate(a, b, ph, **affine):
            xT_c.at(B * ph).wait(a, b, 1)
            fn = ACT.Identity if affine else ACT.Copy
            xts_c.up(nc.scalar.activation(xts[:], bank[7][:, 0:T], fn, **affine))
            xt_c.up(nc.scalar.activation(xt[:, b, TAPS - 1:], bank[7][:, 0:T], fn, **affine))

        def ffn_pe_xT(pe, b, ph, fo):
            ct_c.at(B * fo).wait(pe, b, 0)
            x_transpose(pe, b, ph, xn, lambda e, i: xn_c.at(B * ph).wait(e, i, NT))

        def ffn_pe_router(pe, b, ph, fo, w, ne):
            xts_c.at(B * ph).wait(pe, b, 1)
            xt_c.at(B * ph).wait(pe, b, 1)
            for t in range(NT):
                ins = pe.matmul(bank[7][:, T + t * E1:T + t * E1 + ne], xts[:, t * P:(t + 1) * P], w[:, 0:ne],
                                start=True, stop=True)
            logit_c.up(ins)

        def ffn_pe_ccT(pe, b, fo, route, n_route):
            route.wait(pe, b, n_route)
            for t in range(NT):
                ins = pe.transpose(bank[7][:, t * P:(t + 1) * P], cc[:, t, :].bitcast(F32), ident[:])
            ccT_c.up(ins)

        def ffn_act_xT(a, b, ph, fo):
            logit_c.at(B * fo).wait(a, b, 0)
            x_evacuate(a, b, ph)

        def ffn_act_scores(a, b, fo, ne, route, n_route):
            logit_c.at(B * fo).wait(a, b, 1)
            route.wait(a, b, 0)
            lg = bank[7][:, T:T + NT * E1].rearrange("p (t e) -> p t e", t=NT)[:, :, 0:ne]
            score_c.up(nc.scalar.activation(sc[:, :, 0:ne], lg, ACT.Sigmoid))

        def ffn_act_ct(a, b, fo):
            ccT_c.at(B * fo).wait(a, b, 1)
            ct_c.up(nc.scalar.activation(ct[:, b, :], bank[7][:, 0:T], ACT.Copy))

        def chain(v, c, b):
            k = [0]

            def do(make, lone=False):
                if k[0]:
                    if lone:
                        hold(v, b, (c, k[0]))
                    else:
                        c.wait(v, b, k[0])
                k[0] += 1
                c.up(make())
            return do, k

        def scale_and_split(v, do, ne, eps, scale):
            do(lambda: v.reduce_sum(wsum[:], wsel[:, :, 0:ne], AX.X))
            do(lambda: v.tensor_scalar(wsum[:], wsum[:], eps, None, ALU.add))
            do(lambda: v.reciprocal(wrec[:], wsum[:]))
            if scale != 1.0:
                do(lambda: v.tensor_scalar(wrec[:], wrec[:], scale, None, ALU.mult))
            do(lambda: v.tensor_tensor(cwt[:, :, 0:ne], wsel[:, :, 0:ne], wrec[:].unsqueeze(2).broadcast_to([P, NT, ne]),
                                       ALU.mult))
            do(lambda: v.tensor_copy(cc[:, :, 0:ne], cwt[:, :, 0:ne]))
            do(lambda: v.tensor_tensor(cc[:, :, 64:64 + ne], cwt[:, :, 0:ne], cc[:, :, 0:ne].bitcast(F32), ALU.subtract))

        def route0(v, b, fo):
            c = route0_c.at(B * fo)
            do, k = chain(v, c, b)
            score_c.at(B * (2 * fo if fo < 0 else FO_ALL[("f0", fo)])).wait(v, b, 1)
            ccT_c.at(B * FO_ALL[("f0", fo)]).wait(v, b, 0)
            do(lambda: v.tensor_tensor(pad16[:, :, 0:R0], sc[:, :, 0:R0], rb0[:].unsqueeze(1).broadcast_to([P, NT, R0]),
                                       ALU.add))
            do(lambda: v.max(top8[:, 0, :], pad16[:, 0, :]), True)
            do(lambda: v.max(top8[:, 1, :], pad16[:, 1, :]), True)
            do(lambda: v.tensor_copy(want8[:, :, 0:2], top8[:, :, 0:2]))
            do(lambda: v.match_replace(hit16[:, 0, :], want8[:, 0, :], pad16[:, 0, :], TAKEN), True)
            do(lambda: v.match_replace(hit16[:, 1, :], want8[:, 1, :], pad16[:, 1, :], TAKEN), True)
            do(lambda: v.scalar_tensor_tensor(wsel[:, :, 0:R0], hit16[:, :, 0:R0], TAKEN, sc[:, :, 0:R0],
                                              ALU.is_equal, ALU.mult))
            scale_and_split(v, do, R0, 1e-9, 1.0)
            do(lambda: v.tensor_tensor(s46[:], cwt[:, :, 4], cwt[:, :, 6], ALU.add))
            do(lambda: v.tensor_scalar(s46h[:], s46[:], 0.5, None, ALU.mult))
            do(lambda: v.tensor_scalar(c7h[:], cwt[:, :, 7], 0.5, None, ALU.mult))
            for t in range(NT):
                do(lambda: v.tensor_scalar(skip_u[:, t, :], xn[:, t, :], 0.0, c7h[:, t:t + 1], ALU.max, ALU.mult))
            for t in range(NT):
                do(lambda: v.scalar_tensor_tensor(skip_v[:, t, :], xn[:, t, :], s46h[:, t:t + 1], skip_u[:, t, :],
                                                  ALU.mult, ALU.add))
            do(lambda: v.tensor_tensor(x[:, b, :, :], x[:, b, :, :], skip_v[:], ALU.add))
            assert k[0] == R_OPS0, k

        def route1(v, b, fo):
            c = route1_c.at(B * fo)
            do, k = chain(v, c, b)
            grp = lambda a: a[:].rearrange("p t (g e) -> p (t g) e", e=E1 // NG1)
            spread = lambda a: a[:].unsqueeze(2).broadcast_to([P, NT * NG1, E1 // NG1])
            steps = []

            def first():
                score_c.at(B * FO_ALL[("f1", fo)]).wait(v, b, 1)
                ccT_c.at(B * FO_ALL[("f1", fo)]).wait(v, b, 0)
                do(lambda: v.tensor_tensor(sfc[:], sc[:], cb1[:].unsqueeze(1).broadcast_to([P, NT, E1]), ALU.add))
            steps.append(first)
            add = lambda make, lone=False: steps.append(lambda: do(make, lone))
            add(lambda: v.reduce_max(g_max[:], grp(sfc), AX.X))
            add(lambda: v.tensor_tensor(grp(g_eq), grp(sfc), spread(g_max), ALU.is_equal))
            add(lambda: v.reduce_sum(g_cnt[:], grp(g_eq), AX.X))
            add(lambda: v.scalar_tensor_tensor(g_rest[:], g_eq[:], LOW, sfc[:], ALU.mult, ALU.add))
            add(lambda: v.reduce_max(g_m2[:], grp(g_rest), AX.X))
            add(lambda: v.tensor_scalar(g_d[:], g_cnt[:], 1.5, LOW, ALU.is_lt, ALU.mult))
            add(lambda: v.tensor_tensor(g_d2[:], g_d[:], g_max[:], ALU.add))
            add(lambda: v.tensor_tensor(g_m2b[:], g_m2[:], g_d2[:], ALU.max))
            add(lambda: v.tensor_tensor(pad16[:, :, 0:NG1], g_max[:].rearrange("p (t g) -> p t g", t=NT),
                                        g_m2b[:].rearrange("p (t g) -> p t g", t=NT), ALU.add))
            for t in range(NT):
                add(lambda t=t: v.max(top8[:, t, :], pad16[:, t, :]), True)
            add(lambda: v.tensor_copy(want8g[:, :, 0:TOPG], top8[:, :, 0:TOPG]))
            for t in range(NT):
                add(lambda t=t: v.match_replace(hit16[:, t, :], want8g[:, t, :], pad16[:, t, :], TAKEN), True)
            add(lambda: v.tensor_scalar(gmask[:], hit16[:, :, 0:NG1], TAKEN, None, ALU.is_equal))
            add(lambda: v.tensor_tensor(grp(masked), grp(sfc),
                                        gmask[:].rearrange("p t g -> p (t g)").unsqueeze(2)
                                        .broadcast_to([P, NT * NG1, E1 // NG1]), ALU.mult))
            for t in range(NT):
                add(lambda t=t: v.max(top8[:, t, :], masked[:, t, :]), True)
            for t in range(NT):
                add(lambda t=t: v.match_replace(hit64[:, t, :], top8[:, t, :], masked[:, t, :], TAKEN), True)
            add(lambda: v.scalar_tensor_tensor(wsel[:], hit64[:], TAKEN, sc[:], ALU.is_equal, ALU.mult))
            add(lambda: v.reduce_sum(wsum[:], wsel[:], AX.X))
            add(lambda: v.tensor_scalar(wsum[:], wsum[:], 1e-20, None, ALU.add))
            add(lambda: v.reciprocal(wrec[:], wsum[:]))
            add(lambda: v.tensor_scalar(wrec[:], wrec[:], 2.5, None, ALU.mult))
            add(lambda: v.tensor_tensor(cwt[:], wsel[:], wrec[:].unsqueeze(2).broadcast_to([P, NT, E1]), ALU.mult))
            add(lambda: v.tensor_copy(cc[:, :, 0:E1], cwt[:]))
            add(lambda: v.tensor_tensor(cc[:, :, 64:64 + E1], cwt[:], cc[:, :, 0:E1].bitcast(F32), ALU.subtract))
            assert len(steps) == R_OPS1, len(steps)
            return steps

        FO_ALL = {("f0", 0): 0, ("f0", 1): 1, ("f1", 0): 2, ("f1", 1): 3}

        GB, UB, CB, ACC, BT = bank[0], bank[1], bank[2], bank[4], bank[5]

        def f0_pe(pe, ph, fo):
            fa = FO_ALL[("f0", fo)]
            x_done.wait(pe, ph, 0) if ph == 0 else pe.wait_ge(x_done.sem, B * ph)

            def prep(b):
                ffn_pe_xT(pe, b, ph, fa)
                ffn_pe_router(pe, b, ph, fa, wr0, R0)
                ffn_pe_ccT(pe, b, fa, route0_c.at(B * fo), R_OPS0)

            def body(b):
                xt_c.at(B * ph).wait(pe, b, 1)
                silu_c.at(B * fo).wait(pe, b, 0)
                for bk, w, c in ((GB, wg0, gate_c), (UB, wu0, up0_c)):
                    if c is up0_c:
                        gu_c.at(B * fo).wait(pe, b, 0)
                    for j in range(NC0):
                        ins = pe.matmul(bk[:, j * T:(j + 1) * T], w[:].rearrange("p e i -> p (e i)")[:, j * P:(j + 1) * P],
                                        xt[:, b, TAPS - 1:], start=True, stop=True)
                    c.up(ins)
                ct_c.at(B * fa).wait(pe, b, 1)
                hid0_c.at(B * fo).wait(pe, b, 0)
                for j in range(NC0):
                    ins = pe.matmul(CB[:, j * T:(j + 1) * T], sel_exp[:, 2 * j:2 * j + 2, :].rearrange("p e i -> p (e i)"),
                                    ct[:, b, :], start=True, stop=True)
                cb0_c.up(ins)
                hid0_c.at(B * fo).wait(pe, b, 1)
                outT0_c.at(B * fo).wait(pe, b, 0)
                for j in range(NC0):
                    ins = pe.matmul(ACC[:, 0:T], wd0[:, j, :], hid0[:, j * T:(j + 1) * T], start=(j == 0), stop=(j == NC0 - 1))
                down0_c.up(ins)
                outT0_c.at(B * fo).wait(pe, b, 1)
                x_done.at(B * ph).wait(pe, b, 0)
                for t in range(NT):
                    ins = pe.transpose(BT[:, t * P:(t + 1) * P], outT[:, t * P:(t + 1) * P], ident[:])
                back0_c.up(ins)
                if exists(b + 1):
                    prep(b + 1)

            prep(0)
            batches(pe, body, 1)

        def f0_act(a, ph, fo):
            fa = FO_ALL[("f0", fo)]
            if ph:
                a.wait_ge(x_done.sem, B * ph)

            def prep(b):
                ffn_act_xT(a, b, ph, fa)
                ffn_act_scores(a, b, fa, R0, route0_c.at(B * fo), 0)
                ffn_act_ct(a, b, fa)

            def body(b):
                gate_c.at(B * fo).wait(a, b, 1)
                gu_c.at(B * fo).wait(a, b, 0)
                silu_c.up(nc.scalar.activation(silu_g[:], GB[:], ACT.Silu))
                if exists(b + 1):
                    prep(b + 1)

            prep(0)
            batches(a, body, 1)

        def f0_dve(v, ph, fo):
            fa = FO_ALL[("f0", fo)]
            if ph:
                v.wait_ge(x_done.sem, B * ph)

            def body(b):
                xt_c.at(B * ph).wait(v, b, 1)
                outT0_c.at(B * fo).wait(v, b, 0)
                conv_c.up(v.tensor_scalar(conv[:, 0, :], xt[:, b, 0:T], cw0[:, 0:1], cb0[:, 0:1], ALU.mult, ALU.add))
                for k in range(1, TAPS):
                    conv_c.at(B * fo).wait(v, b, k)
                    conv_c.up(v.scalar_tensor_tensor(conv[:, k, :], xt[:, b, k:k + T], cw0[:, k:k + 1], conv[:, k - 1, :],
                                                     ALU.mult, ALU.add))
                silu_c.at(B * fo).wait(v, b, 1)
                up0_c.at(B * fo).wait(v, b, 1)
                hid0_c.at(B * fo).wait(v, b, 0)
                gu_c.up(v.tensor_tensor(gu[:], silu_g[:], UB[:], ALU.mult))
                gu_c.at(B * fo).wait(v, b, 1)
                cb0_c.at(B * fo).wait(v, b, 1)
                down0_c.at(B * fo).wait(v, b, 0)
                hid0_c.up(v.tensor_tensor(hid0[:], gu[:], CB[:], ALU.mult))
                if exists(b + 1):
                    ln_stats(v, b + 1, ph)
                down0_c.at(B * fo).wait(v, b, 1)
                conv_c.at(B * fo).wait(v, b, TAPS)
                back0_c.at(B * fo).wait(v, b, 0)
                outT0_c.up(v.tensor_tensor(outT[:], conv[:, TAPS - 1, :], ACC[:, 0:T], ALU.add))
                if exists(b + 1):
                    ccT_c.at(B * fa).wait(v, b + 1, 0)
                    ln_xn(v, b + 1, ph)
                back0_c.at(B * fo).wait(v, b, 1)
                route0_c.at(B * fo).wait(v, b, R_OPS0)
                x_done.up(v.scalar_tensor_tensor(x[:, b, :, :].rearrange("p t d -> p (t d)"), BT[:, 0:T], 0.5,
                                                 x[:, b, :, :].rearrange("p t d -> p (t d)"), ALU.mult, ALU.add))
                if exists(b + 1):
                    route0(v, b + 1, fo)

            ln_stats(v, 0, ph)
            ln_xn(v, 0, ph)
            route0(v, 0, fo)
            batches(v, body, 1)

        HB, CB1 = (bank[0], bank[1]), (bank[2], bank[3])

        def up_weight(slot):
            if slot < PAIRS:
                w = wup[:].rearrange("p e i -> p (e i)")
                return [w[:, (2 * slot + c) * P:(2 * slot + c + 1) * P] for c in range(2)]
            return [wsu[:, (slot - PAIRS) * P:(slot - PAIRS + 1) * P]]

        def down_weight(slot):
            if slot < PAIRS:
                return [wdn[:, 2 * slot + c, :] for c in range(2)]
            return [wsd[:, slot - PAIRS, :]]

        def width(slot):
            return 512 if slot < PAIRS else T

        def f1_pe(pe, ph, fo):
            fa = FO_ALL[("f1", fo)]
            pe.wait_ge(x_done.sem, B * ph)
            r1 = route1_c.at(B * fo)

            def down(b, s):
                if s < 0:
                    b, s = b - 1, s + SLOTS
                if not exists(b):
                    return
                hid1_c.at(B * fo).wait(pe, b, s + 1)
                if s == 0:
                    outT1_c.at(B * fo).wait(pe, b, 0)
                ws = down_weight(s)
                for c, w in enumerate(ws):
                    ins = pe.matmul(ACC[:, 0:T], w, hid[:, s % 3, c * T:(c + 1) * T], start=(s == 0 and c == 0),
                                    stop=(s == SLOTS - 1))
                down1_c.up(ins)

            def back(b):
                outT1_c.at(B * fo).wait(pe, b, 1)
                x_done.at(B * ph).wait(pe, b, 0)
                for t in range(NT):
                    ins = pe.transpose(BT[:, t * P:(t + 1) * P], outT[:, t * P:(t + 1) * P], ident[:])
                back1_c.up(ins)

            def body(b):
                xt_c.at(B * ph).wait(pe, b, 1)
                ct_c.at(B * fa).wait(pe, b, 1)
                for s in range(SLOTS):
                    relu_c_.at(B * fo).wait(pe, b, s - 1)
                    for c, w in enumerate(up_weight(s)):
                        ins = pe.matmul(HB[s % 2][:, c * T:(c + 1) * T], w, xt[:, b, TAPS - 1:], start=True, stop=True)
                    up1_c.up(ins)
                    if s < PAIRS:
                        rc_c.at(B * fo).wait(pe, b, s - 1)
                        for c in range(2):
                            e = 4 * s + 2 * c
                            ins = pe.matmul(CB1[s % 2][:, c * T:(c + 1) * T],
                                            sel_exp[:, e:e + 2, :].rearrange("p e i -> p (e i)"), ct[:, b, :],
                                            start=True, stop=True)
                        cb1_c.up(ins)
                    down(b, s - 2)
                    if s == 3 and exists(b + 1):
                        ffn_pe_xT(pe, b + 1, ph, fa)
                    if s == 4 and exists(b - 1):
                        back(b - 1)
                    if s == 5 and exists(b + 1):
                        ffn_pe_router(pe, b + 1, ph, fa, wr1, E1)
                    if s == SLOTS - 2 and exists(b + 1):
                        ffn_pe_ccT(pe, b + 1, fa, r1, R_OPS1)

            ffn_pe_xT(pe, 0, ph, fa)
            ffn_pe_router(pe, 0, ph, fa, wr1, E1)
            ffn_pe_ccT(pe, 0, fa, r1, R_OPS1)
            batches(pe, body, 1)
            down(B, -2)
            down(B, -1)
            back(B - 1)

        def f1_act(a, ph, fo):
            fa = FO_ALL[("f1", fo)]
            a.wait_ge(x_done.sem, B * ph)
            r1 = route1_c.at(B * fo)

            def evacuate(b):
                down1_c.at(B * fo).wait(a, b, SLOTS)
                back1_c.at(B * fo).wait(a, b, 0)
                outT1_c.up(nc.scalar.activation(outT[:], ACC[:, 0:T], ACT.Copy))

            def body(b):
                for s in range(SLOTS):
                    up1_c.at(B * fo).wait(a, b, s + 1)
                    hid1_c.at(B * fo).wait(a, b, s - 2)
                    relu_c_.up(nc.scalar.activation(relu_h[:, s % 3, 0:width(s)], HB[s % 2][:, 0:width(s)], ACT.Relu))
                    if s == 1 and exists(b - 1):
                        evacuate(b - 1)
                    if s == 3 and exists(b + 1):
                        ffn_act_xT(a, b + 1, ph, fa)
                    if s == 5 and exists(b + 1):
                        ffn_act_scores(a, b + 1, fa, E1, r1, 0)
                    if s == SLOTS - 2 and exists(b + 1):
                        ffn_act_ct(a, b + 1, fa)

            ffn_act_xT(a, 0, ph, fa)
            ffn_act_scores(a, 0, fa, E1, r1, 0)
            ffn_act_ct(a, 0, fa)
            batches(a, body, 1)
            evacuate(B - 1)

        def f1_dve(v, ph, fo):
            fa = FO_ALL[("f1", fo)]
            v.wait_ge(x_done.sem, B * ph)

            def hidden(b, s):
                if s < 0:
                    b, s = b - 1, s + SLOTS
                if not exists(b):
                    return
                down1_c.at(B * fo).wait(v, b, s - 2)
                if s < PAIRS:
                    rc_c.at(B * fo).wait(v, b, s + 1)
                    ins = v.tensor_tensor(hid[:, s % 3, :], relu_c[:, s % 2, :], relu_h[:, s % 3, :], ALU.mult)
                else:
                    relu_c_.at(B * fo).wait(v, b, s + 1)
                    ins = v.tensor_tensor(hid[:, s % 3, 0:T], relu_h[:, s % 3, 0:T], relu_h[:, s % 3, 0:T], ALU.mult)
                hid1_c.up(ins)

            def add_out(b):
                back1_c.at(B * fo).wait(v, b, 1)
                x_done.up(v.scalar_tensor_tensor(x[:, b, :, :].rearrange("p t d -> p (t d)"), BT[:, 0:T], 0.5,
                                                 x[:, b, :, :].rearrange("p t d -> p (t d)"), ALU.mult, ALU.add))

            def body(b):
                steps = route1(v, b + 1, fo) if exists(b + 1) else []
                for s in range(SLOTS):
                    if s < PAIRS:
                        relu_c_.at(B * fo).wait(v, b, s + 1)
                        cb1_c.at(B * fo).wait(v, b, s + 1)
                        hid1_c.at(B * fo).wait(v, b, s - 1)
                        rc_c.up(v.tensor_tensor(relu_c[:, s % 2, :], relu_h[:, s % 3, :], CB1[s % 2][:], ALU.mult))
                    hidden(b, s - 1)
                    if exists(b + 1):
                        if s == 0:
                            ln_stats(v, b + 1, ph)
                        if s == 2:
                            xT_c.at(B * ph).wait(v, b + 1, 0)
                            ln_xn(v, b + 1, ph)
                    if s == 4 and exists(b - 1):
                        add_out(b - 1)
                    if 6 <= s <= SLOTS - 3:
                        n = -(-R_OPS1 // (SLOTS - 8))
                        for step in steps[(s - 6) * n:(s - 5) * n]:
                            step()

            ln_stats(v, 0, ph)
            ln_xn(v, 0, ph)
            for step in route1(v, 0, fo):
                step()
            batches(v, body, 1)
            hidden(B, -1)
            add_out(B - 1)

        SA, TA, OB, MQ, MK = (bank[0], bank[1]), (bank[2], bank[3]), bank[4], bank[5], bank[6]

        class Att:
            def __init__(self, kind):
                self.kind = kind
                self.ng = 4 if kind == 0 else 2
                self.c = A0C if kind == 0 else A1C
                self.ph = 1 if kind == 0 else 4
                self.lead = 2
                self.dv = DH0 if kind == 0 else DC
                self.scale = float(DH0) ** -0.5 if kind == 0 else float(DK + DR) ** -0.5

            def norm(self, b, g):
                return (b + 1, g - self.ng) if g >= self.ng else (b - 1, g + self.ng) if g < 0 else (b, g)

            def wait(self, eng, name, b, g, k):
                per = self.c[name].per // self.ng
                self.c[name].wait(eng, b, g * per + k)

            def pe_project(self, pe, b, g, half):
                b, g = self.norm(b, g)
                if not exists(b):
                    return
                bk, lo, mm = ((MQ, "q_lo", "q_mm"), (MK, "k_lo" if self.kind == 0 else "q_lo2", "k_mm"))[half]
                self.wait(pe, lo, b, g, 0)
                if self.kind == 0:
                    xt_c.at(B * self.ph).wait(pe, b, 1)
                    ins = pe.matmul(bk[:, 0:T], (wq4, wk4)[half][:, g].rearrange("p c r -> p (c r)"), xt[:, b, TAPS - 1:],
                                    start=True, stop=True)
                else:
                    cq_c.wait(pe, b, 1)
                    for i in range(2):
                        ins = pe.matmul(bk[:, i * T:(i + 1) * T], a1[:, 4 * g + 2 * half + i].rearrange("p c r -> p (c r)"),
                                        cq[:, b, :], start=True, stop=True)
                self.c[mm].up(ins)

            def pe_scores(self, pe, b, g, i):
                b, g = self.norm(b, g)
                if not exists(b):
                    return
                par, qt, pr = g % 2, i // 2, i % 2
                if i == 0:
                    self.wait(pe, "q_lo", b, g, 1)
                    if self.kind == 1:
                        kk_lo_c.wait(pe, b, 1)
                if self.kind == 0 and i < 2:
                    self.wait(pe, "k_mask", b, g, 2 * pr + 2)
                if self.kind == 1 and i == 1:
                    self.wait(pe, "q_lo2", b, g, 1)
                self.wait(pe, "row_max", b, g, i - 1)
                bk = SA[i % 2]
                if self.kind == 0:
                    ins = pe.matmul(bk[:], q0[:, g, qt * P:(qt + 1) * P],
                                    k0m[:, par, 2 * pr:2 * pr + 2, :].rearrange("p j t -> p (j t)"), start=True, stop=True)
                else:
                    for j in range(2):
                        for part in range(2):
                            ins = pe.matmul(bk[:, j * T:(j + 1) * T], q1[:, par, 2 * pr + j, qt * P:(qt + 1) * P],
                                            k1[:, b, part, :], start=(part == 0), stop=(part == 1))
                self.c["s_mm"].up(ins)

            def pe_max_transpose(self, pe, b, g):
                src, name, n = (nm, "row_max", 4) if self.kind == 0 else (shift, "shift", 2)
                self.wait(pe, name, b, g, n)
                self.wait(pe, "exp", b, g, 0)
                for qt in range(NT):
                    ins = pe.transpose(TA[1][0:4, qt * P:(qt + 1) * P], src[:, g % 2, qt, :], ident[:])
                self.c["mT"].up(ins)

            def pe_probs(self, pe, b, g, j):
                par = g % 2
                if j == 0:
                    self.wait(pe, "mt_rows", b, g, 2)
                if self.kind == 1 and j == 0:
                    self.wait(pe, "k_mask", b, g, 1)
                self.wait(pe, "exp", b, g, j - 1)
                bk = TA[j % 2]
                pe.matmul(bk[:].rearrange("p (k t) -> p k t", k=2), sel_row[:, j, :],
                          mt[:].unsqueeze(1).broadcast_to([P, 2, T]), start=True, stop=False)
                for kt in range(NT):
                    o = bk[:, kt * T:(kt + 1) * T]
                    if self.kind == 0:
                        ins = pe.matmul(o, k0m[:, par, j, kt * P:(kt + 1) * P], q0[:, g, :], start=False, stop=(kt == 1))
                    else:
                        for part in range(2):
                            ins = pe.matmul(o, k1s[:, par, part, kt * P:(kt + 1) * P], q1[:, par, j, :], start=False,
                                            stop=(kt == 1 and part == 1))
                self.c["t_mm"].up(ins)

            def pe_values(self, pe, b, g, j):
                b, g = self.norm(b, g)
                if not exists(b):
                    return
                w = self.dv + 1
                self.wait(pe, "exp", b, g, j + 1)
                if j == 0:
                    self.wait(pe, "norm", b, g, 0)
                v_all, at = (v0, (4 * g + j) * w) if self.kind == 0 else (v1, 0)
                for qt in range(NT):
                    for kt in range(NT):
                        rhs = v_all[:, b, kt, at:at + WIDE]
                        o = (j * NT + qt) * w
                        ins = pe.matmul(OB[:, o:o + WIDE], probs[:, j, kt * T + qt * P:kt * T + (qt + 1) * P], rhs,
                                        start=(kt == 0), stop=(kt == 1))
                self.c["pv"].up(ins)

            def pe_out_transpose(self, pe, b):
                if not exists(b):
                    return
                self.wait(pe, "norm", b, self.ng - 1, 1)
                if exists(b + 2):
                    (self.c["v_ev"] if self.kind == 0 else cst_c).wait(pe, b, 3)
                nb = H0 * DH0 // P if self.kind == 0 else H1 * DC // P
                for blk in range(nb):
                    for qt in range(NT):
                        ins = pe.transpose(bank[7][:, (blk * NT + qt) * P:(blk * NT + qt + 1) * P],
                                           on[:, qt, blk * P:(blk + 1) * P], ident[:])
                self.c["onT"].up(ins)

            def pe_out(self, pe, b):
                if not exists(b):
                    return
                self.c["ots"].wait(pe, b, 1)
                nb = 1 if self.kind == 0 else 2
                for qt in range(NT):
                    for blk in range(nb):
                        w = wo0[:] if self.kind == 0 else vo1[:, blk, :]
                        ins = pe.matmul(bank[7][:, qt * P:(qt + 1) * P], ots[:, (blk * NT + qt) * P:(blk * NT + qt + 1) * P],
                                        w, start=(blk == 0), stop=(blk == nb - 1))
                self.c["out_mm"].up(ins)

            def pe_prep_xT(self, pe, b, prev):
                if not exists(b):
                    return
                if exists(prev):
                    x_done.at(B * self.ph).wait(pe, prev, 1)
                ready = ((lambda e, i: xh_c.wait(e, i, NT)) if self.kind == 0 else
                         (lambda e, i: xn_c.at(B * self.ph).wait(e, i, NT)))
                (self.c["v_ev"] if self.kind == 0 else cst_c).wait(pe, b, 0)
                x_transpose(pe, b, self.ph, xh if self.kind == 0 else xn, ready)

            def pe_prep_values(self, pe, b):
                if not exists(b):
                    return
                xts_c.at(B * self.ph).wait(pe, b, 1)
                xt_c.at(B * self.ph).wait(pe, b, 1)
                if self.kind == 0:
                    for t in range(NT):
                        ins = pe.matmul(bank[7][:, t * P:(t + 1) * P], xts[:, t * P:(t + 1) * P], wqkv[:, 2 * D:3 * D],
                                        start=True, stop=True)
                    self.c["v_mm"].up(ins)
                    return
                pe.matmul(bank[7][:, 0:T], wkk[:].rearrange("p c r -> p (c r)"), xt[:, b, TAPS - 1:], start=True, stop=True)
                kk_mm_c.up(pe.matmul(bank[7][0:DC, T:2 * T], wdq[:], xt[:, b, TAPS - 1:], start=True, stop=True))

            def pe_prep_latent(self, pe, b):
                if self.kind == 0 or not exists(b):
                    return
                kk_lo_c.wait(pe, b, 1)
                for t in range(NT):
                    pe.matmul(bank[7][:, t * DC:(t + 1) * DC], xts[:, t * P:(t + 1) * P], wkk[:, 0, 0:DC], start=True, stop=True)
                cqs_c.wait(pe, b, 1)
                for t in range(NT):
                    ins = pe.matmul(bank[7][:, P + t * H1:P + (t + 1) * H1], cqs[:, t * P:(t + 1) * P], acol[:],
                                    start=True, stop=True)
                self.c["v_mm"].up(ins)

            def pe(self, pe):
                pe.wait_ge(x_done.sem, B * self.ph)
                for b in range(2):
                    self.pe_prep_xT(pe, b, -1)
                    self.pe_prep_values(pe, b)
                    if b == 0:
                        self.pe_prep_latent(pe, b)
                for g in range(2):
                    for half in range(2):
                        self.pe_project(pe, 0, g, half)
                for i in range(4):
                    self.pe_scores(pe, 0, 0, i)

                last = self.ng - 1

                def body(b):
                    for g in range(self.ng):
                        self.pe_max_transpose(pe, b, g)
                        self.pe_project(pe, b, g + 2, 0)
                        self.pe_values(pe, b, g - 1, 3)
                        self.pe_scores(pe, b, g + 1, 0)
                        if self.kind == 0:
                            self.pe_project(pe, b, g + 2, 1)
                        self.pe_scores(pe, b, g + 1, 1)
                        if self.kind == 1:
                            self.pe_project(pe, b, g + 2, 1)
                        self.pe_probs(pe, b, g, 0)
                        self.pe_scores(pe, b, g + 1, 2)
                        self.pe_probs(pe, b, g, 1)
                        if g == 0:
                            self.pe_prep_latent(pe, b + 1)
                        if g == last and self.kind == 1:
                            self.pe_prep_xT(pe, b + 2, b - 1)
                        if g == last and self.kind == 0:
                            self.pe_prep_values(pe, b + 2)
                        self.pe_values(pe, b, g, 0)
                        self.pe_scores(pe, b, g + 1, 3)
                        self.pe_probs(pe, b, g, 2)
                        if g == 0:
                            self.pe_out_transpose(pe, b - 1)
                        self.pe_values(pe, b, g, 1)
                        self.pe_probs(pe, b, g, 3)
                        if g == last and self.kind == 1:
                            self.pe_prep_values(pe, b + 2)
                        if g == 2:
                            self.pe_prep_xT(pe, b + 2, b - 1)
                        self.pe_values(pe, b, g, 2)
                        if g == 0:
                            self.pe_out(pe, b - 1)

                batches(pe, body, self.lead)
                self.pe_values(pe, B - 1, last, 3)
                self.pe_out_transpose(pe, B - 1)
                self.pe_out(pe, B - 1)

            def act_split(self, a, b, g, half):
                b, g = self.norm(b, g)
                if not exists(b):
                    return
                c = self.c
                self.wait(a, ("q_mm", "k_mm")[half], b, g, 1)
                if self.kind == 1:
                    self.wait(a, "t_mm", b, g - 2, 2 * half + 2)
                    c[("q_hi", "q_hi2")[half]].up(nc.scalar.activation(
                        q1[:, g % 2, 2 * half:2 * half + 2, :].rearrange("p j t -> p (j t)"), (MQ, MK)[half][:], ACT.Copy))
                elif half == 0:
                    self.wait(a, "t_mm", b, g - 4, 4)
                    c["q_hi"].up(nc.scalar.activation(q0[:, g, :], MQ[:, 0:T], ACT.Identity, bias=bq4[:, g:g + 1]))
                else:
                    self.wait(a, "k_mask", b, g, 0)
                    c["k_hi"].up(nc.scalar.activation(k0[:], MK[:, 0:T], ACT.Identity, bias=bk4[:, g:g + 1]))

            def act_mask(self, a, b, g, j):
                b, g = self.norm(b, g)
                if not exists(b):
                    return
                self.wait(a, "k_lo", b, g, 2)
                self.wait(a, "t_mm", b, g - 2, j + 1)
                self.c["k_mask"].up(nc.scalar.activation(k0m[:, g % 2, j, :], k0[:].bitcast(F32), ACT.Copy,
                                                         scale=head_mask[:, j:j + 1]))

            def act_exp(self, a, b, g, j):
                self.wait(a, "t_mm", b, g, j + 1)
                self.wait(a, "pv", b, g, j + 1 - 4)
                self.c["exp"].up(nc.scalar.activation(probs[:, j, :], TA[j % 2][:], ACT.Exp, scale=self.scale))

            def act_out(self, a, b):
                if not exists(b):
                    return
                self.c["onT"].wait(a, b, 1)
                self.c["out_mm"].wait(a, b, 0)
                n = T if self.kind == 0 else 2 * T
                self.c["ots"].up(nc.scalar.activation(ots[:, 0:n], bank[7][:, 0:n], ACT.Copy))

            def act_prep(self, a, b):
                if not exists(b):
                    return
                self.c["v_mm"].wait(a, b, 0)
                if self.kind == 0:
                    x_evacuate(a, b, self.ph, bias=bet[:, 0:1], scale=gam[:, 0:1])
                else:
                    x_evacuate(a, b, self.ph)

            def act_prep_keys(self, a, b):
                if self.kind == 0 or not exists(b):
                    return
                kk_mm_c.wait(a, b, 1)
                kk_hi_c.up(nc.scalar.activation(k1[:, b, 0, :], bank[7][:, 0:T], ACT.Identity, bias=bkk[:, 0:1]))
                cq_c.up(nc.scalar.activation(cq[0:DC, b, :], bank[7][0:DC, T:2 * T], ACT.Identity, bias=bdq[:, 0:1]))
                cqs_c.up(nc.scalar.activation(cqs[0:DC, :], bank[7][0:DC, T:2 * T], ACT.Identity, bias=bdq[:, 0:1]))

            def act(self, a):
                a.wait_ge(x_done.sem, B * self.ph)
                for b in range(2):
                    self.act_prep(a, b)
                    self.act_prep_keys(a, b)
                for g in range(2):
                    for half in range(2):
                        self.act_split(a, 0, g, half)
                    if self.kind == 0:
                        for j in range(4):
                            self.act_mask(a, 0, g, j)

                last = self.ng - 1

                def body(b):
                    for g in range(self.ng):
                        if self.kind == 0:
                            self.act_split(a, b, g + 2, 0)
                            self.act_split(a, b, g + 2, 1)
                            self.act_exp(a, b, g, 0)
                            self.act_exp(a, b, g, 1)
                            self.act_mask(a, b, g + 2, 0)
                            self.act_exp(a, b, g, 2)
                            self.act_mask(a, b, g + 2, 1)
                            if g == 0:
                                self.act_out(a, b - 1)
                            self.act_exp(a, b, g, 3)
                            self.act_mask(a, b, g + 2, 2)
                            self.act_mask(a, b, g + 2, 3)
                            if g == 2:
                                self.act_prep(a, b + 2)
                        else:
                            self.act_exp(a, b, g, 0)
                            self.act_exp(a, b, g, 1)
                            self.act_split(a, b, g + 2, 0)
                            if g == 1:
                                self.act_prep(a, b + 2)
                            self.act_exp(a, b, g, 2)
                            if g == 0:
                                self.act_out(a, b - 1)
                            self.act_exp(a, b, g, 3)
                            self.act_split(a, b, g + 2, 1)
                            if g == 1:
                                self.act_prep_keys(a, b + 2)

                batches(a, body, self.lead)
                self.act_out(a, B - 1)

            def dve_split(self, v, b, g, half):
                b, g = self.norm(b, g)
                if not exists(b):
                    return
                c, hi = self.c, slice(64, P)
                if self.kind == 1:
                    bk, name, src = ((MQ, "q_lo", "q_hi"), (MK, "q_lo2", "q_hi2"))[half]
                    self.wait(v, src, b, g, 1)
                    q = q1[hi, g % 2, 2 * half:2 * half + 2, :].rearrange("p j t -> p (j t)")
                    c[name].up(v.tensor_tensor(q, bk[hi, :], q.bitcast(F32), ALU.subtract))
                elif half == 0:
                    self.wait(v, "q_hi", b, g, 1)
                    c["q_lo"].up(v.scalar_tensor_tensor(q0[hi, g, :], MQ[hi, 0:T], bq4[hi, g:g + 1],
                                                        q0[hi, g, :].bitcast(F32), ALU.add, ALU.subtract))
                else:
                    self.wait(v, "k_hi", b, g, 1)
                    for r in (slice(32, 64), slice(96, 128)):
                        c["k_lo"].up(v.scalar_tensor_tensor(k0[r, :], MK[r, 0:T], bk4[r, g:g + 1], k0[r, :].bitcast(F32),
                                                            ALU.add, ALU.subtract))

            def dve_rows(self, v, b, g):
                self.wait(v, "mT", b, g, 1)
                self.wait(v, "t_mm", b, g, 0)
                self.c["mt_rows"].up(v.tensor_copy(mt[0:4, :], TA[1][0:4, 0:T]))
                self.wait(v, "mt_rows", b, g, 1)
                self.c["mt_rows"].up(v.tensor_tensor(mt[32:36, :], TA[1][0:4, 0:T], mt[0:4, :].bitcast(F32), ALU.subtract))

            def dve_normalise(self, v, b, g):
                b, g = self.norm(b, g)
                if not exists(b):
                    return
                w = self.dv + 1
                self.wait(v, "pv", b, g, 4)
                o8 = OB[:, 0:8 * w].rearrange("p (r w) -> p r w", w=w)
                self.c["recip"].up(v.reciprocal(rz[:], o8[:, :, self.dv]))
                self.wait(v, "recip", b, g, 1)
                if g == 0:
                    self.c["onT"].wait(v, b, 0)
                o4 = OB[:, 0:8 * w].rearrange("p (j q w) -> p q j w", q=NT, j=4)
                dst = on[:, :, g * 4 * self.dv:(g + 1) * 4 * self.dv].rearrange("p q (j d) -> p q j d", j=4)
                rzb = rz[:].rearrange("p (j q) -> p q j", q=NT).unsqueeze(3).broadcast_to([P, NT, 4, self.dv])
                self.c["norm"].up(v.tensor_tensor(dst, o4[:, :, :, 0:self.dv], rzb, ALU.mult))

            def dve_max(self, v, b, g, i):
                b, g = self.norm(b, g)
                if not exists(b):
                    return
                qt, pr = i // 2, i % 2
                self.wait(v, "s_mm", b, g, i + 1)
                if i == 0:
                    self.wait(v, "mT", b, g - 2, 1)
                self.c["row_max"].up(v.tensor_reduce(nm[:, g % 2, qt, 2 * pr:2 * pr + 2],
                                                     SA[i % 2][:].rearrange("p (j t) -> p j t", j=2), AX.X, ALU.max,
                                                     negate=True))

            def dve_shift(self, v, b, g):
                b, g = self.norm(b, g)
                if self.kind == 0 or not exists(b):
                    return
                cs = cst[:, b, :, 4 * g:4 * g + 4]
                self.wait(v, "row_max", b, g, 4)
                if isinstance(b, int) or True:
                    cst_c.wait(v, b, 1)
                self.c["shift"].up(v.tensor_tensor(msum[:], cs, nm[:, g % 2], ALU.subtract))
                self.wait(v, "shift", b, g, 1)
                self.c["shift"].up(v.tensor_tensor(shift[:, g % 2], cs, msum[:], ALU.subtract))

            def dve_add_out(self, v, b):
                if not exists(b):
                    return
                self.c["out_mm"].wait(v, b, 1)
                self.c["x_add"].wait(v, b, 1)
                xb = x[:, b, :, :].rearrange("p t d -> p (t d)")
                x_done.up(v.tensor_tensor(xb, xb, bank[7][:, 0:T], ALU.add))

            def dve_prep_a(self, v, b):
                if not exists(b):
                    return
                ln_stats(v, b, self.ph)

            def dve_prep_b(self, v, b):
                if not exists(b):
                    return
                if self.kind == 0:
                    x_xn_c.wait(v, b, 0)
                    xh_c.wait(v, b, 0)
                else:
                    xT_c.at(B * self.ph).wait(v, b, 0)
                ln_xn(v, b, self.ph)

            def dve_prep_h(self, v, b, part):
                if self.kind == 1 or not exists(b):
                    return
                if part == 0:
                    xn_c.at(B * self.ph).wait(v, b, NT)
                    for t in range(NT):
                        stats2_c.up(v.bn_stats(st2[:, t, :], xn[:, t, :]))
                    for t in range(NT):
                        if t == 0:
                            hold(v, b, (stats2_c, NT))
                        mv2_c.up(v.bn_aggr(mv2[:, t, :], st2[:, t, :]))
                    return
                rstd2_c.wait(v, b, 1)
                xT_c.at(B * self.ph).wait(v, b, 0)
                for t in range(NT):
                    xh_c.up(v.tensor_scalar(xh[:, t, :], xn[:, t, :], mv2[:, t, 0:1], rstd2[:, t:t + 1],
                                            ALU.subtract, ALU.mult))

            def dve_prep_keys(self, v, b):
                if self.kind == 0 or not exists(b):
                    return
                kk_hi_c.wait(v, b, 1)
                cq_c.wait(v, b, 1)
                cqs_c.wait(v, b, 1)
                kk_lo_c.up(v.scalar_tensor_tensor(k1[:, b, 1, :], bank[7][:, 0:T], bkk[:, 0:1],
                                                  k1[:, b, 0, :].bitcast(F32), ALU.add, ALU.subtract))

            def dve_prep_values(self, v, b):
                if not exists(b):
                    return
                self.c["v_mm"].wait(v, b, 1)
                if self.kind == 0:
                    for t in range(NT):
                        ins = v.tensor_tensor(v0h[:, b, t, :, 0:DH0],
                                              bank[7][:, t * P:(t + 1) * P].rearrange("p (h d) -> p h d", h=H0),
                                              bvr[:].rearrange("p (h d) -> p h d", h=H0), ALU.add)
                    self.c["v_ev"].up(ins)
                else:
                    self.c["v_ev"].up(v.tensor_tensor(v1[:, b, :, 0:DC],
                                                      bank[7][:, 0:NT * DC].rearrange("p (t d) -> p t d", t=NT),
                                                      bdkvr[:].unsqueeze(1).broadcast_to([P, NT, DC]), ALU.add))
                    cst_c.up(v.tensor_copy(cst[:, b, :, :],
                                           bank[7][:, P:P + NT * H1].rearrange("p (t h) -> p t h", t=NT)))

            def dve(self, v):
                v.wait_ge(x_done.sem, B * self.ph)
                for b in range(2):
                    self.dve_prep_a(v, b)
                    self.dve_prep_b(v, b)
                    self.dve_prep_h(v, b, 0)
                    self.dve_prep_h(v, b, 1)
                    self.dve_prep_keys(v, b)
                    if b == 0 or self.kind == 0:
                        self.dve_prep_values(v, b)
                for g in range(2):
                    for half in range(2):
                        self.dve_split(v, 0, g, half)
                for i in range(4):
                    self.dve_max(v, 0, 0, i)
                self.dve_shift(v, 0, 0)

                last = self.ng - 1

                def body(b):
                    for g in range(self.ng):
                        self.dve_rows(v, b, g)
                        self.dve_normalise(v, b, g - 1)
                        self.dve_max(v, b, g + 1, 0)
                        if self.kind == 0:
                            self.dve_split(v, b, g + 2, 0)
                            if g == 2:
                                self.dve_prep_h(v, b + 2, 1)
                        self.dve_max(v, b, g + 1, 1)
                        if self.kind == 0:
                            self.dve_split(v, b, g + 2, 1)
                        if g == 0 and self.kind == 1:
                            self.dve_prep_values(v, b + 1)
                        self.dve_max(v, b, g + 1, 2)
                        if self.kind == 1:
                            self.dve_split(v, b, g + 2, 0)
                        if g == 0:
                            self.dve_prep_a(v, b + 2)
                        if g == 1 and self.kind == 0:
                            self.dve_prep_b(v, b + 2)
                        self.dve_max(v, b, g + 1, 3)
                        self.dve_shift(v, b, g + 1)
                        if self.kind == 1:
                            self.dve_split(v, b, g + 2, 1)
                        if g == 0:
                            self.dve_add_out(v, b - 1)
                            if self.kind == 1:
                                self.dve_prep_b(v, b + 2)
                        if g == 1:
                            self.dve_prep_h(v, b + 2, 0)
                        if g == last:
                            if self.kind == 1:
                                self.dve_prep_keys(v, b + 2)
                            else:
                                self.dve_prep_values(v, b + 2)

                batches(v, body, self.lead)
                self.dve_normalise(v, B, -1)
                self.dve_add_out(v, B - 1)

            def pool_prep(self, g_, b):
                if not exists(b):
                    return
                ln_rstd(g_, b, self.ph)
                if self.kind == 0:
                    xn_c.at(B * self.ph).wait(g_, b, NT)
                    mv2_c.wait(g_, b, NT)
                    xh_c.wait(g_, b, 0)
                    veps2_c.up(nc.gpsimd.tensor_tensor(veps2[:], mv2[:, :, 1], eps2[:], ALU.add))
                    veps2_c.wait(g_, b, 1)
                    rstd2_c.up(nc.gpsimd.tensor_tensor(rstd2[:], veps2[:], neghalf[:], ALU.pow))
                    x_xn_c.up(nc.gpsimd.tensor_tensor(x[:, b], x[:, b], xn[:], ALU.add))
                    hold_pool(g_, b, x_xn_c, 1)
                else:
                    hold_pool(g_, b, xn_c.at(B * self.ph), NT)
                bias = bo0 if self.kind == 0 else bo1
                self.c["x_add"].up(nc.gpsimd.tensor_tensor(x[:, b], x[:, b], bias[:].unsqueeze(1).broadcast_to([P, NT, D]),
                                                           ALU.add))

            def pool_keys(self, g_, b, g):
                b, g = self.norm(b, g)
                if self.kind == 0 or not exists(b):
                    return
                kk_lo_c.wait(g_, b, 1)
                self.wait(g_, "k_mask", b, g, 0)
                hold_pool(g_, b, self.c["t_mm"], (g - 2) * 4 + 4, 1)
                self.c["k_mask"].up(nc.gpsimd.tensor_copy(k1s[:, g % 2], k1[:, b].bitcast(F32)))

            def pool(self, g_):
                g_.wait_ge(x_done.sem, B * self.ph)
                for b in range(self.lead):
                    self.pool_prep(g_, b)
                self.pool_keys(g_, 0, 0)
                self.pool_keys(g_, 0, 1)

                def body(b):
                    for g in range(self.ng):
                        self.pool_keys(g_, b, g + 2)
                        if g == 0:
                            self.pool_prep(g_, b + self.lead)

                batches(g_, body, self.lead)

        if True:
            A1C["k_mask"].per = 2
        att0, att1 = Att(0), Att(1)

        row = lambda ap, n: ap.rearrange("(a n) -> a n", a=1).partition_broadcast(P) if False else ap.partition_broadcast(P)
        col = lambda ap: ap.rearrange("(p a) -> p a", a=1)

        N_X, N_W0, N_ATT0, N_PRE1, N_MOE = 2, 8, 16, 18, 6

        @block.sync
        def _(sp):
            def load(dst, src, s, scattered=False):
                sp.dma_start(dst, src, allow_slow_non_contiguous=scattered).then_inc(s, 16)

            xin = I["L0_attn_x"].rearrange("b (t p) d -> p (b t) d", p=P)
            xf = x[:].rearrange("p b t d -> p (b t) d")
            load(xf[:, 0:4], xin[:, 0:4], x_in)
            load(xf[:, 4:], xin[:, 4:], x_in)
            load(wr0[:], I["L0_ffn_Wr"], w0_in)
            load(rb0[:], I["L0_ffn_router_bias"].partition_broadcast(P), w0_in)
            load(wg0[:], I["L0_ffn_Wg"].rearrange("e h i -> h e i"), w0_in)
            load(wu0[:], I["L0_ffn_Wu"].rearrange("e h i -> h e i"), w0_in)
            load(cw0[:], I["L0_ffn_conv_w"].rearrange("k a h -> h (k a)"), w0_in, True)
            load(cb0[:], col(I["L0_ffn_conv_b"]), w0_in)
            for e in range(2):
                load(wd0[e * IM0:(e + 1) * IM0], I["L0_ffn_Wd"].rearrange("(j e) i h -> e i j h", e=2)[e], w0_in)
            load(wqkv[:], I["L0_attn_w_qkv"], att0_in)
            load(gam[:], col(I["L0_attn_ln_gamma"]), att0_in)
            load(bet[:], col(I["L0_attn_ln_beta"]), att0_in)
            bqkv = I["L0_attn_b_qkv"].rearrange("(s g r) -> s r g", s=3, g=4)
            for c in range(4):
                load(bq4[32 * c:32 * c + 32], bqkv[0], att0_in, True)
                load(bk4[32 * c:32 * c + 32], bqkv[1], att0_in, True)
            load(bvr[:], I["L0_attn_b_qkv"][2 * D:3 * D].partition_broadcast(P), att0_in)
            load(wo0[:], I["L0_attn_w_out"], att0_in)
            load(bo0[:], I["L0_attn_b_out"].partition_broadcast(P), att0_in)
            load(wr1t[:], I["L1_ffn_router_w"], att0_in)
            load(cb1[:], I["L1_ffn_correction_bias"].partition_broadcast(P), att0_in)
            for dst, w, bias in ((uq, "W_UQ", "b_UQ"), (uk, "W_UK", "b_UK"), (uv, "W_UV", "b_UV")):
                load(dst[0:DC], I[f"L1_attn_{w}"], pre1_in)
                load(dst[DC:DC + 1], I[f"L1_attn_{bias}"].rearrange("(a n) -> a n", a=1), pre1_in)
            load(qr[0:DC], I["L1_attn_W_QR"].rearrange("c (h r) -> c h r", h=H1), pre1_in)
            load(qr[DC:DC + 1], I["L1_attn_b_QR"].rearrange("(a h r) -> a h r", a=1, h=H1), pre1_in)
            load(wo1[:], I["L1_attn_W_O"].rearrange("(h d) n -> d h n", h=H1), pre1_in)
            load(wdq[:], I["L1_attn_W_DQ"], pre1_in)
            load(bdq[:], col(I["L1_attn_b_DQ"]), pre1_in)
            for c in range(2):
                load(wkk[:, c, 0:DC], I["L1_attn_W_DKV"], pre1_in)
                load(wkk[:, c, DC:], I["L1_attn_W_KR"], pre1_in)
                load(bkk[64 * c:64 * c + DC], col(I["L1_attn_b_DKV"]), pre1_in)
                load(bkk[64 * c + DC:64 * c + 64], col(I["L1_attn_b_KR"]), pre1_in)
            load(bdkvr[:], I["L1_attn_b_DKV"].partition_broadcast(P), pre1_in)
            load(bo1r[:], I["L1_attn_b_O"].partition_broadcast(P), pre1_in)
            load(wup[:], I["L1_ffn_up_w"].rearrange("e h i -> h e i"), moe_in)
            for e in range(2):
                load(wdn[e * IM1:(e + 1) * IM1], I["L1_ffn_down_w"].rearrange("(j e) i h -> e i j h", e=2)[e], moe_in)
            load(wsu[:], I["L1_ffn_shared_up_w"], moe_in)
            load(wsd[:], I["L1_ffn_shared_down_w"].rearrange("(s p) h -> p s h", p=P), moe_in)
            outv = out.rearrange("b (t p) d -> b p t d", p=P)
            with sp.Fori(0, B) as b:
                sp.wait_ge(x_done.sem, b + (B * (LAST_STAGE - 1) + 1))
                sp.dma_start(outv[b], x[:, b]).then_inc(stored, 16)
            sp.wait_ge(stored, 16 * B)

        LOADS = {"w0": 8, "att0": 3 + 8 + 5, "pre1": 6 + 2 + 3 + 8 + 2, "moe": 5}

        @block.gpsimd
        def _(g):
            g.memset(ident[:], 0.0).then_inc(const_pool, 1)
            g.wait_ge(const_pool, 1)
            g.affine_select(out=ident[:], in_=ident[:], compare_op=ALU.not_equal, fill=1.0, base=0,
                            pattern=[[-1, P]], channel_multiplier=1).then_inc(const_pool, 1)
            g.memset(neghalf[:], -0.5).then_inc(const_pool, 1)
            g.memset(eps2[:], LN_EPS).then_inc(const_pool, 1)
            g.memset(a1[:], 0.0).then_inc(const_pool, 1)
            g.memset(acol[:], 0.0).then_inc(const_pool, 1)
            g.memset(v0[:], 1.0).then_inc(const_pool, 1)
            g.memset(v1[:], 1.0).then_inc(const_pool, 1)
            g.memset(cq[:], 0.0).then_inc(const_pool, 1)
            g.memset(cqs[:], 0.0).then_inc(const_pool, 1)
            g.wait_ge(const_pool, 10)
            g.memset(cq[DC:DC + 1], 1.0).then_inc(const_pool, 1)
            g.memset(cqs[DC:DC + 1], 1.0).then_inc(const_pool, 1)
            g.wait_ge(const_pool, 12)

            def rstd_loop(ph):
                if ph:
                    g.wait_ge(x_done.sem, B * ph)
                ln_rstd(g, 0, ph)
                with g.Fori(1, B) as b:
                    ln_rstd(g, b, ph)

            stages = [lambda: rstd_loop(0), lambda: att0.pool(g), lambda: rstd_loop(2), lambda: rstd_loop(3),
                      lambda: (g.wait_ge(pre_done, 1), att1.pool(g)), lambda: rstd_loop(5)]
            for stage in stages[:LAST_STAGE]:
                stage()

        @block.tensor
        def _(pe):
            pe.wait_ge(const_pool, 2)
            pe.wait_ge(pre1_in, 16 * LOADS["pre1"])
            pe.wait_ge(att0_in, 16 * LOADS["att0"])
            for i, w in enumerate((uq, uk, uv)):
                for h in range(H1):
                    ins = pe.transpose(bank[i][:, h * (DC + 1):(h + 1) * (DC + 1)], w[:, h * DK:(h + 1) * DK],
                                       ident[0:DC + 1, 0:DC + 1])
                ins.then_inc(pre_tr, 1)
            pe.transpose(bank[6][:, 0:E1], wr1t[:], ident[0:E1, 0:E1]).then_inc(pre_tr, 1)
            pe.wait_ge(pre_ev, 4)
            for h in range(H1):
                ins = pe.matmul(bank[3][0:DC + 1, h * (DC + 1):(h + 1) * (DC + 1)], uqt[:, h, :], ukt[:, h, :],
                                start=True, stop=True)
            ins.then_inc(pre_mm, 1)
            for h in range(H1):
                blk, j = h // 4, h % 4
                ins = pe.matmul(bank[4][32 * j:32 * j + 32, blk * D:(blk + 1) * D], uvt[:, h, 0:DC], wo1[:, h, :],
                                start=True, stop=True, tile_position=(0, 32 * j))
            ins.then_inc(pre_mm, 1)
            for h in range(H1):
                ins = pe.matmul(bank[5][:, 0:D], bvb[:, h, :], wo1[:, h, :], start=(h == 0), stop=(h == H1 - 1))
            ins.then_inc(pre_mm, 1)
            pe.wait_ge(pre_done, 1)
            pe.wait_ge(w0_in, 16 * LOADS["w0"])
            pe.wait_ge(moe_in, 16 * LOADS["moe"])
            stages = [lambda: f0_pe(pe, 0, 0), lambda: att0.pe(pe), lambda: f0_pe(pe, 2, 1), lambda: f1_pe(pe, 3, 0),
                      lambda: att1.pe(pe), lambda: f1_pe(pe, 5, 1)]
            for stage in stages[:LAST_STAGE]:
                stage()

        @block.scalar
        def _(a):
            a.wait_ge(pre_done, 1)
            stages = [lambda: f0_act(a, 0, 0), lambda: att0.act(a), lambda: f0_act(a, 2, 1), lambda: f1_act(a, 3, 0),
                      lambda: att1.act(a), lambda: f1_act(a, 5, 1)]
            for stage in stages[:LAST_STAGE]:
                stage()

        @block.vector
        def _(v):
            for t, s in ((xt, None), (pad16, None)):
                pass
            v.memset(xt[:, :, 0:TAPS - 1], 0.0).then_inc(const_dve, 1)
            v.memset(pad16[:], PAD_LOW).then_inc(const_dve, 1)
            v.memset(want8[:], PAD_LOW).then_inc(const_dve, 1)
            v.memset(want8g[:], PAD_LOW).then_inc(const_dve, 1)
            v.memset(cc[:].bitcast(F32), 0.0).then_inc(const_dve, 1)
            v.memset(mt[:].bitcast(F32), 0.0).then_inc(const_dve, 1)
            v.wait_ge(const_pool, 12)
            v.tensor_reduce(head_mask[:], ident[:].rearrange("p (c j d) -> p j c d", c=4, j=4), AX.XY,
                            ALU.add).then_inc(const_dve, 1)
            v.tensor_tensor(sel_small[:], ident[:, 0:64], ident[:, 64:128], ALU.add).then_inc(const_dve, 1)
            v.tensor_tensor(rz[:, 0:4], ident[:, 0:4], ident[:, 32:36], ALU.add).then_inc(const_dve, 1)
            v.wait_ge(const_dve, 9)
            v.tensor_copy(sel_exp[:], sel_small[:].unsqueeze(2).broadcast_to([P, 64, 64])).then_inc(const_dve, 1)
            v.tensor_copy(sel_row[:], rz[:, 0:4].unsqueeze(2).broadcast_to([P, 4, P])).then_inc(const_dve, 1)
            v.wait_ge(att0_in, 16 * LOADS["att0"])
            for dst, o in ((wq4, 0), (wk4, D)):
                v.tensor_copy(dst[:], wqkv[:, o:o + D].rearrange("p (g r) -> p g r", g=4).unsqueeze(2)
                              .broadcast_to([P, 4, 4, 32])).then_inc(const_dve, 1)
            v.wait_ge(pre1_in, 16 * LOADS["pre1"])
            v.wait_ge(pre_tr, 4)
            for i, dst in enumerate((uqt, ukt, uvt)):
                v.tensor_copy(dst[:], bank[i][:, 0:H1 * (DC + 1)].rearrange("p (h c) -> p h c", h=H1)).then_inc(const_dve, 1)
            v.tensor_copy(wr1[:], bank[6][:, 0:E1]).then_inc(const_dve, 1)
            v.wait_ge(const_dve, 17)
            v.tensor_copy(bvb, uvt[:, :, DC:DC + 1].broadcast_to([P, H1, P])).then_inc(pre_ev, 4)
            v.wait_ge(pre_mm, 1)
            m = bank[3][0:DC + 1, 0:H1 * (DC + 1)].rearrange("p (h c) -> p h c", h=H1)
            for c in range(2):
                v.tensor_copy(a1[0:DC + 1, :, c, 0:DC], m[:, :, 0:DC]).then_inc(const_dve, 1)
                v.tensor_copy(a1[0:DC + 1, :, c, DC:], qr[:]).then_inc(const_dve, 1)
            v.tensor_copy(acol[0:DC + 1, :], m[:, :, DC]).then_inc(const_dve, 1)
            v.wait_ge(pre_mm, 2)
            v.tensor_copy(vo1[:], bank[4][:, 0:2 * D].rearrange("p (b n) -> p b n", b=2)).then_inc(const_dve, 1)
            v.wait_ge(pre_mm, 3)
            v.tensor_tensor(bo1[:], bank[5][:, 0:D], bo1r[:], ALU.add).then_inc(const_dve, 1)
            v.wait_ge(w0_in, 16 * LOADS["w0"])
            v.wait_ge(x_in, 32)
            v.wait_ge(const_dve, 24)
            v.memset(rz[:], 0.0).then_inc(pre_done, 1)
            v.wait_ge(pre_done, 1)
            stages = [lambda: f0_dve(v, 0, 0), lambda: att0.dve(v), lambda: f0_dve(v, 2, 1), lambda: f1_dve(v, 3, 0),
                      lambda: att1.dve(v), lambda: f1_dve(v, 5, 1)]
            for stage in stages[:LAST_STAGE]:
                stage()


_INS = ['L0_attn_x', 'L0_attn_ln_gamma', 'L0_attn_ln_beta', 'L0_attn_w_qkv', 'L0_attn_b_qkv', 'L0_attn_w_out',
        'L0_attn_b_out', 'L0_ffn_Wr', 'L0_ffn_router_bias', 'L0_ffn_Wg', 'L0_ffn_Wu', 'L0_ffn_Wd', 'L0_ffn_conv_w',
        'L0_ffn_conv_b', 'L1_attn_W_DQ', 'L1_attn_b_DQ', 'L1_attn_W_UQ', 'L1_attn_b_UQ', 'L1_attn_W_DKV',
        'L1_attn_b_DKV', 'L1_attn_W_UK', 'L1_attn_b_UK', 'L1_attn_W_UV', 'L1_attn_b_UV', 'L1_attn_W_QR',
        'L1_attn_b_QR', 'L1_attn_W_KR', 'L1_attn_b_KR', 'L1_attn_W_O', 'L1_attn_b_O', 'L1_ffn_router_w',
        'L1_ffn_correction_bias', 'L1_ffn_up_w', 'L1_ffn_down_w', 'L1_ffn_shared_up_w', 'L1_ffn_shared_down_w']


def kernel(**inputs):
    import numpy as _np
    import concourse.bacc as _bacc
    from concourse import mybir as _mybir
    from concourse.bass_utils import run_bass_kernel_spmd as _run

    nc = _bacc.Bacc("TRN2", target_bir_lowering=False, num_devices=1)
    arrays, aps = {}, {}
    for name in _INS:
        a = _np.ascontiguousarray(inputs[name])
        arrays[f"in_{name}"] = a
        aps[name] = nc.dram_tensor(f"in_{name}", a.shape, _mybir.dt.from_np(a.dtype), kind="ExternalInput").ap()
    shape = inputs["L0_attn_x"].shape
    out = nc.dram_tensor("out_0", shape, _mybir.dt.from_np(_np.dtype("float32")), kind="ExternalOutput").ap()
    macaron_kernel(nc, aps, out)
    r = _run(nc, [arrays], core_ids=[0])
    return r.results[0]["out_0"]
```

```python
from contextlib import ExitStack

import concourse.bass as bass
from concourse import mybir

ALU = mybir.AluOpType
ACT = mybir.ActivationFunctionType
AX = mybir.AxisListType
F32 = mybir.dt.float32
F32R = mybir.dt.float32r

P = 128
D = 128
LN_EPS = 1e-5
PAD_LOW = -3e38
TAKEN = -2e38
LOW = -1e30
LAST_STAGE = 6


class Count:

    def __init__(self, sem, per, base=0):
        self.sem, self.per, self.base = sem, per, base

    def at(self, base):
        return Count(self.sem, self.per, base)

    def wait(self, eng, b, k):
        k = k + self.base * self.per
        if isinstance(b, int):
            if b * self.per + k > 0:
                eng.wait_ge(self.sem, b * self.per + k)
        else:
            assert self.per + k > 0
            eng.wait_ge(self.sem, b * self.per + k)

    def up(self, ins):
        return ins.then_inc(self.sem, 1)


def macaron_kernel(nc, I, out):
    B, T, _ = I["L0_attn_x"].shape
    NT = T // P
    E0, IM0 = I["L0_ffn_Wg"].shape[0], I["L0_ffn_Wg"].shape[2]
    R0 = I["L0_ffn_Wr"].shape[1]
    TAPS = I["L0_ffn_conv_w"].shape[0]
    NC0 = E0 * IM0 // P
    E1, _, IM1 = I["L1_ffn_up_w"].shape
    NG1, TOPG, TOPK = 8, 4, 8
    NC1 = E1 * IM1 // P
    NSH = I["L1_ffn_shared_up_w"].shape[1] // P
    PAIRS = NC1 // 2
    SLOTS = PAIRS + NSH
    H0, DH0 = 16, 8
    H1, DC, DR = 8, 32, 32
    DK = 128
    assert T == 256 and NT == 2 and SLOTS % 6 == 0 and H0 * DH0 == D and NC0 == 2 and TAPS == 4

    with ExitStack() as ctx:
        def sb(name, shape, dt=F32):
            return ctx.enter_context(nc.sbuf_tensor(name, shape, dt))

        def sem(name):
            return ctx.enter_context(nc.semaphore(name))

        def count(name, per=1):
            return Count(sem(name), per)

        bank = [ctx.enter_context(nc.psum_tensor(f"bank{i}", [P, 512], F32)) for i in range(8)]

        ident = sb("ident", [P, P])
        neghalf = sb("neghalf", [P, NT])
        eps2 = sb("eps2", [P, NT])
        cell = sb("cell", [P, 2])
        cell_pool = sb("cell_pool", [P, 2, NT])
        head_mask = sb("head_mask", [P, 4])
        sel_small = sb("sel_small", [P, 64])
        sel_exp = sb("sel_exp", [P, 64, 64], F32R)
        sel_row = sb("sel_row", [P, 4, P], F32R)

        x = sb("x", [P, B, NT, D])
        xt = sb("xt", [P, B, TAPS - 1 + T])
        xts = sb("xts", [P, T])
        xn = sb("xn", [P, NT, D])
        xh = sb("xh", [P, NT, D])
        st = sb("st", [P, NT, 6])
        mv = sb("mv", [P, NT, 2])
        veps = sb("veps", [P, NT])
        rstd = sb("rstd", [P, NT])
        st2 = sb("st2", [P, NT, 6])
        mv2 = sb("mv2", [P, NT, 2])
        veps2 = sb("veps2", [P, NT])
        rstd2 = sb("rstd2", [P, NT])

        area = sb("area", [P, 4096])

        def part(at, *shape, rows=P):
            n = 1
            for k in shape:
                n *= k
            names = "abcd"[:len(shape)]
            return area[0:rows, at:at + n].rearrange(f"p ({' '.join(names)}) -> p {' '.join(names)}",
                                                     **dict(zip(names, shape)))

        wr0 = sb("wr0", [P, R0])
        rb0 = sb("rb0", [P, R0])
        wg0 = sb("wg0", [P, E0, IM0])
        wu0 = sb("wu0", [P, E0, IM0])
        wd0 = sb("wd0", [P, NC0, D])
        cw0 = sb("cw0", [P, TAPS])
        cb0 = sb("cb0", [P, 1])
        gam = sb("gam", [P, 1])
        bet = sb("bet", [P, 1])
        wqkv = sb("wqkv", [P, 3 * D])
        wq4 = sb("wq4", [P, 4, 4, 32])
        wk4 = sb("wk4", [P, 4, 4, 32])
        bq4 = sb("bq4", [P, 4])
        bk4 = sb("bk4", [P, 4])
        bvr = sb("bvr", [P, D])
        wo0 = sb("wo0", [P, D])
        bo0 = sb("bo0", [P, D])
        wr1 = sb("wr1", [P, E1])
        wr1t = sb("wr1t", [E1, D])
        cb1 = sb("cb1", [P, E1])
        wup = sb("wup", [P, E1, IM1])
        wdn = sb("wdn", [P, NC1, D])
        wsu = sb("wsu", [P, NSH * P])
        wsd = sb("wsd", [P, NSH, D])
        uq, uk, uv = (part(i * H1 * DK, H1 * DK, rows=DC + 1) for i in range(3))
        qr = sb("qr", [DC + 1, H1, DR])
        uqt = sb("uqt", [P, H1, DC + 1])
        ukt = sb("ukt", [P, H1, DC + 1])
        uvt = sb("uvt", [P, H1, DC + 1])
        wo1 = sb("wo1", [P, H1, D])
        wdq = sb("wdq", [P, DC])
        bdq = sb("bdq", [DC, 1])
        wkk = sb("wkk", [P, 2, DC + DR])
        bkk = sb("bkk", [P, 1])
        bdkvr = sb("bdkvr", [P, DC])
        bo1r = sb("bo1r", [P, D])
        a1 = sb("a1", [P, H1, 2, DC + DR])
        acol = sb("acol", [P, H1])
        vo1 = sb("vo1", [P, 2, D])
        bvb = part(3 * H1 * DK, H1, P)
        bo1 = sb("bo1", [P, D])

        k0m = sb("k0m", [P, 2, 4, T], F32R)
        cq = sb("cq", [P, B, T])
        xn_all = cq[:].rearrange("p b (t d) -> p b t d", t=NT)
        sc = sb("sc", [P, NT, E1])
        sfc = sb("sfc", [P, NT, E1])
        pad16 = sb("pad16", [P, NT, 16])
        top8 = sb("top8", [P, NT, 8])
        want8 = sb("want8", [P, NT, 8])
        want8g = sb("want8g", [P, NT, 8])
        hit16 = sb("hit16", [P, NT, 16])
        wsel = sb("wsel", [P, NT, E1])
        wsum = sb("wsum", [P, NT])
        wrec = sb("wrec", [P, NT])
        cwt = sb("cwt", [P, NT, E1])
        cc = sb("cc", [P, NT, P], F32R)
        k1 = sb("k1", [P, B, 2, T], F32R)
        ct = k1[:, :, 0, :]
        s46 = sb("s46", [P, NT])
        s46h = sb("s46h", [P, NT])
        c7h = sb("c7h", [P, NT])
        skip_u = sb("skip_u", [P, NT, D])
        skip_v = sb("skip_v", [P, NT, D])
        g_max = sb("g_max", [P, NT * NG1])
        g_eq = sb("g_eq", [P, NT, E1])
        g_cnt = sb("g_cnt", [P, NT * NG1])
        g_rest = sb("g_rest", [P, NT, E1])
        g_m2 = sb("g_m2", [P, NT * NG1])
        g_d = sb("g_d", [P, NT * NG1])
        g_d2 = sb("g_d2", [P, NT * NG1])
        g_m2b = sb("g_m2b", [P, NT * NG1])
        gmask = sb("gmask", [P, NT, NG1])
        masked = sb("masked", [P, NT, E1])
        hit64 = sb("hit64", [P, NT, E1])
        relu_h = part(0, 3, 512)
        hid = part(1536, 3, 512)
        relu_c = part(3072, 2, 512)
        outT = sb("outT", [P, T])
        silu_g = sb("silu_g", [P, 512])
        gu = sb("gu", [P, 512])
        hid0 = sb("hid0", [P, 512])
        conv = part(3072, 4, T)

        q0 = sb("q0", [P, 4, T], F32R)
        k0 = sb("k0", [P, T], F32R)
        v0 = sb("v0", [P, B, NT, H0, DH0 + 1])
        q1 = sb("q1", [P, 2, 4, T], F32R)
        k1s = sb("k1s", [P, 2, 2, T], F32R)
        cqs = sb("cqs", [P, T])
        v1 = sb("v1", [P, B, NT, DC + 1])
        cst = sb("cst", [P, B, NT, H1])
        nm = sb("nm", [P, 2, NT, 4])
        msum = sb("msum", [P, NT, 4])
        shift = sb("shift", [P, 2, NT, 4])
        mt = sb("mt", [P, T], F32R)
        probs = part(0, 4, 512)
        rz = sb("rz", [P, 8])
        on = sb("on", [P, NT, H1 * DC])
        ots = sb("ots", [P, 512])

        x_in, w0_in, att0_in, pre1_in, moe_in = (sem(n) for n in ("x_in", "w0_in", "att0_in", "pre1_in", "moe_in"))
        stored = sem("stored")
        cq_one = sem("cq_one")
        const_pool, const_dve = sem("const_pool"), sem("const_dve")
        pre_tr, pre_ev, pre_mm, pre_done = sem("pre_tr"), sem("pre_ev"), sem("pre_mm"), sem("pre_done")
        ready0 = sem("ready0")
        stats_c = count("stats", NT)
        mv_c = count("mean_var", NT)
        veps_c = count("var_eps")
        rstd_c = count("rstd")
        xn_c = count("xn", NT)
        xT_c = count("xT_psum")
        xts_c = count("xT_stage")
        xt_c = count("xT_all")
        x_done = count("x_done")
        logit_c = count("logits")
        score_c = count("scores")
        R_OPS0, R_OPS1 = 21, 29
        route0_c = count("route0", R_OPS0)
        route1_c = count("route1", R_OPS1)
        ccT_c = count("ccT_psum")
        ct_c = count("ct_all")
        xn_kept_c = count("xn_kept")
        gate_c, up0_c, cb0_c = count("gate_psum"), count("up_psum"), count("comb0_psum")
        silu_c, gu_c, hid0_c = count("silu"), count("gate_up"), count("hid0")
        conv_c = count("conv", 4)
        down0_c, outT0_c, back0_c = count("down0_psum"), count("outT0"), count("back0_psum")
        up1_c = count("up1_psum", SLOTS)
        cb1_c = count("comb1_psum", PAIRS)
        relu_c_ = count("relu1", SLOTS)
        rc_c = count("relu_comb", PAIRS)
        hid1_c = count("hid1", SLOTS)
        down1_c = count("down1_psum", SLOTS)
        outT1_c, back1_c = count("outT1"), count("back1_psum")

        def make_attention_counts(tag, ng):
            c = {}
            for name, per in (("q_mm", 1), ("k_mm", 1), ("q_hi", 1), ("q_hi2", 1), ("k_hi", 1), ("q_lo", 1), ("q_lo2", 1),
                              ("k_lo", 2), ("k_mask", 4), ("s_mm", 4), ("row_max", 4), ("shift", 2), ("mT", 1),
                              ("mt_rows", 2), ("t_mm", 4), ("exp", 4), ("pv", 4), ("recip", 1), ("norm", 1)):
                c[name] = count(f"{tag}_{name}", per * ng)
            return c

        A0C = make_attention_counts("a0", 4)
        A1C = make_attention_counts("a1", 2)
        for c, tag in ((A0C, "a0"), (A1C, "a1")):
            for name in ("v_mm", "v_ev", "onT", "ots", "out_mm", "x_add"):
                c[name] = count(f"{tag}_{name}")
        stats2_c = count("stats2", NT)
        mv2_c = count("mean_var2", NT)
        veps2_c = count("var_eps2")
        rstd2_c = count("rstd2")
        xh_c = count("xh", NT)
        x_xn_c = count("x_plus_xn")
        kk_mm_c, kk_hi_c, kk_lo_c, cq_c, cqs_c = (count(n) for n in ("kk_mm", "kk_hi", "kk_lo", "cq_ev", "cq_stage"))
        cst_c = count("cst_ev")

        block = ctx.enter_context(nc.Block())

        def batches(eng, body, lead):
            body(0)
            with eng.Fori(1, B - lead) as b:
                body(b)
            for b in range(B - lead, B):
                body(b)

        def hold(v, b, *waits, which=0):
            for c, k in waits:
                c.wait(v, b, k)
            if not isinstance(b, int):
                v.memset(cell[:, which:which + 1], 0.0)

        def hold_pool(g, b, c, k, which=0):
            c.wait(g, b, k)
            if not isinstance(b, int):
                nc.gpsimd.tensor_tensor(cell_pool[:, which], neghalf[:], eps2[:], ALU.add)

        def is_batch(b, k):
            return isinstance(b, int) and b == k

        def exists(b):
            return not isinstance(b, int) or 0 <= b < B

        def ln_stats(v, b, ph):
            if ph and isinstance(b, int):
                x_done.at(B * (ph - 1)).wait(v, b, 1)
            for t in range(NT):
                stats_c.up(v.bn_stats(st[:, t, :], x[:, b, t, :]))
            for t in range(NT):
                if t == 0:
                    hold(v, b, (stats_c.at(B * ph), NT), (rstd_c.at(B * ph), 0))
                mv_c.up(v.bn_aggr(mv[:, t, :], st[:, t, :]))

        def ln_rstd(g, b, ph):
            mv_c.at(B * ph).wait(g, b, NT)
            xn_c.at(B * ph).wait(g, b, 0)
            veps_c.up(nc.gpsimd.tensor_tensor(veps[:], mv[:, :, 1], eps2[:], ALU.add))
            veps_c.at(B * ph).wait(g, b, 1)
            rstd_c.up(nc.gpsimd.tensor_tensor(rstd[:], veps[:], neghalf[:], ALU.pow))

        def ln_xn(v, b, ph):
            rstd_c.at(B * ph).wait(v, b, 1)
            for t in range(NT):
                xn_c.up(v.tensor_scalar(xn[:, t, :], x[:, b, t, :], mv[:, t, 0:1], rstd[:, t:t + 1],
                                        ALU.subtract, ALU.mult))

        def x_transpose(pe, b, ph, src, ready):
            ready(pe, b)
            for t in range(NT):
                ins = pe.transpose(bank[7][:, t * P:(t + 1) * P], src[:, t, :], ident[:])
            xT_c.up(ins)

        def x_evacuate(a, b, ph, **affine):
            xT_c.at(B * ph).wait(a, b, 1)
            fn = ACT.Identity if affine else ACT.Copy
            xts_c.up(nc.scalar.activation(xts[:], bank[7][:, 0:T], fn, **affine))
            xt_c.up(nc.scalar.activation(xt[:, b, TAPS - 1:], bank[7][:, 0:T], fn, **affine))

        def ffn_pe_xT(pe, b, ph, fo, shared_bank=True):
            if shared_bank:
                ct_c.at(B * fo).wait(pe, b, 0)
            else:
                xt_c.at(B * ph).wait(pe, b, 0)
            x_transpose(pe, b, ph, xn, lambda e, i: xn_c.at(B * ph).wait(e, i, NT))

        def ffn_pe_router(pe, b, ph, fo, w, ne, bk=None):
            xts_c.at(B * ph).wait(pe, b, 1)
            xt_c.at(B * ph).wait(pe, b, 1)
            if bk is not None:
                score_c.at(B * fo).wait(pe, b, 0)
            o = bank[7] if bk is None else bk
            for t in range(NT):
                ins = pe.matmul(o[:, T + t * E1:T + t * E1 + ne], xts[:, t * P:(t + 1) * P], w[:, 0:ne],
                                start=True, stop=True)
            logit_c.up(ins)

        def ffn_pe_ccT(pe, b, fo, route, n_route, bk=None):
            route.wait(pe, b, n_route)
            if bk is not None:
                ct_c.at(B * fo).wait(pe, b, 0)
            o = bank[7] if bk is None else bk
            for t in range(NT):
                ins = pe.transpose(o[:, t * P:(t + 1) * P], cc[:, t, :].bitcast(F32), ident[:])
            ccT_c.up(ins)

        def ffn_act_xT(a, b, ph, fo):
            logit_c.at(B * fo).wait(a, b, 0)
            x_evacuate(a, b, ph)

        def ffn_act_scores(a, b, fo, ne, route, n_route, bk=None):
            logit_c.at(B * fo).wait(a, b, 1)
            route.wait(a, b, n_route)
            o = bank[7] if bk is None else bk
            lg = o[:, T:T + NT * E1].rearrange("p (t e) -> p t e", t=NT)[:, :, 0:ne]
            score_c.up(nc.scalar.activation(sc[:, :, 0:ne], lg, ACT.Sigmoid))

        def ffn_act_ct(a, b, fo, bk=None):
            ccT_c.at(B * fo).wait(a, b, 1)
            o = bank[7] if bk is None else bk
            ct_c.up(nc.scalar.activation(ct[:, b, :], o[:, 0:T], ACT.Copy))

        def chain(v, c, b):
            k = [0]

            def do(make, lone=False):
                if k[0]:
                    if lone:
                        hold(v, b, (c, k[0]), which=1)
                    else:
                        c.wait(v, b, k[0])
                k[0] += 1
                c.up(make())
            return do, k

        def route0(v, b, fo):
            do, _ = chain(v, route0_c.at(B * fo), b)
            steps = []

            def first():
                score_c.at(B * FO_ALL[("f0", fo)]).wait(v, b, 1)
                do(lambda: v.tensor_tensor(pad16[:, :, 0:R0], sc[:, :, 0:R0],
                                           rb0[:].unsqueeze(1).broadcast_to([P, NT, R0]), ALU.add))
            steps.append(first)
            add = lambda make, lone=False: steps.append(lambda: do(make, lone))
            for t in range(NT):
                add(lambda t=t: v.max(top8[:, t, :], pad16[:, t, :]), True)
            add(lambda: v.tensor_copy(want8[:, :, 0:2], top8[:, :, 0:2]))
            for t in range(NT):
                add(lambda t=t: v.match_replace(hit16[:, t, :], want8[:, t, :], pad16[:, t, :], TAKEN), True)
            add(lambda: v.scalar_tensor_tensor(wsel[:, :, 0:R0], hit16[:, :, 0:R0], TAKEN, sc[:, :, 0:R0],
                                               ALU.is_equal, ALU.mult))
            add(lambda: v.reduce_sum(wsum[:], wsel[:, :, 0:R0], AX.X))
            add(lambda: v.tensor_scalar(wsum[:], wsum[:], 1e-9, None, ALU.add))
            add(lambda: v.reciprocal(wrec[:], wsum[:]))
            add(lambda: v.tensor_tensor(cwt[:, :, 0:R0], wsel[:, :, 0:R0], wrec[:].unsqueeze(2).broadcast_to([P, NT, R0]),
                                        ALU.mult))
            steps.append(lambda: (ccT_c.at(B * FO_ALL[("f0", fo)]).wait(v, b, 0),
                                  do(lambda: v.tensor_copy(cc[:, :, 0:R0], cwt[:, :, 0:R0]))))
            add(lambda: v.tensor_tensor(cc[:, :, 64:64 + R0], cwt[:, :, 0:R0], cc[:, :, 0:R0].bitcast(F32), ALU.subtract))
            add(lambda: v.tensor_tensor(s46[:], cwt[:, :, 4], cwt[:, :, 6], ALU.add))
            add(lambda: v.tensor_scalar(s46h[:], s46[:], 0.5, None, ALU.mult))
            add(lambda: v.tensor_scalar(c7h[:], cwt[:, :, 7], 0.5, None, ALU.mult))
            for t in range(NT):
                if t == 0:
                    steps.append(lambda: (xn_kept_c.at(B * fo).wait(v, b, 1), do(lambda: v.tensor_scalar(
                        skip_u[:, 0, :], xn_all[:, b, 0, :], 0.0, c7h[:, 0:1], ALU.max, ALU.mult))))
                    continue
                add(lambda t=t: v.tensor_scalar(skip_u[:, t, :], xn_all[:, b, t, :], 0.0, c7h[:, t:t + 1], ALU.max, ALU.mult))
            for t in range(NT):
                add(lambda t=t: v.scalar_tensor_tensor(skip_v[:, t, :], xn_all[:, b, t, :], s46h[:, t:t + 1],
                                                       skip_u[:, t, :], ALU.mult, ALU.add))
            add(lambda: v.tensor_tensor(x[:, b, :, :], x[:, b, :, :], skip_v[:], ALU.add))
            assert len(steps) == R_OPS0, len(steps)
            return steps

        def route1(v, b, fo):
            c = route1_c.at(B * fo)
            do, k = chain(v, c, b)
            grp = lambda a: a[:].rearrange("p t (g e) -> p (t g) e", e=E1 // NG1)
            spread = lambda a: a[:].unsqueeze(2).broadcast_to([P, NT * NG1, E1 // NG1])
            steps = []

            def first():
                score_c.at(B * FO_ALL[("f1", fo)]).wait(v, b, 1)
                ccT_c.at(B * FO_ALL[("f1", fo)]).wait(v, b, 0)
                do(lambda: v.tensor_tensor(sfc[:], sc[:], cb1[:].unsqueeze(1).broadcast_to([P, NT, E1]), ALU.add))
            steps.append(first)
            add = lambda make, lone=False: steps.append(lambda: do(make, lone))
            add(lambda: v.reduce_max(g_max[:], grp(sfc), AX.X))
            add(lambda: v.tensor_tensor(grp(g_eq), grp(sfc), spread(g_max), ALU.is_equal))
            add(lambda: v.reduce_sum(g_cnt[:], grp(g_eq), AX.X))
            add(lambda: v.scalar_tensor_tensor(g_rest[:], g_eq[:], LOW, sfc[:], ALU.mult, ALU.add))
            add(lambda: v.reduce_max(g_m2[:], grp(g_rest), AX.X))
            add(lambda: v.tensor_scalar(g_d[:], g_cnt[:], 1.5, LOW, ALU.is_lt, ALU.mult))
            add(lambda: v.tensor_tensor(g_d2[:], g_d[:], g_max[:], ALU.add))
            add(lambda: v.tensor_tensor(g_m2b[:], g_m2[:], g_d2[:], ALU.max))
            add(lambda: v.tensor_tensor(pad16[:, :, 0:NG1], g_max[:].rearrange("p (t g) -> p t g", t=NT),
                                        g_m2b[:].rearrange("p (t g) -> p t g", t=NT), ALU.add))
            for t in range(NT):
                add(lambda t=t: v.max(top8[:, t, :], pad16[:, t, :]), True)
            add(lambda: v.tensor_copy(want8g[:, :, 0:TOPG], top8[:, :, 0:TOPG]))
            for t in range(NT):
                add(lambda t=t: v.match_replace(hit16[:, t, :], want8g[:, t, :], pad16[:, t, :], TAKEN), True)
            add(lambda: v.tensor_scalar(gmask[:], hit16[:, :, 0:NG1], TAKEN, None, ALU.is_equal))
            add(lambda: v.tensor_tensor(grp(masked), grp(sfc),
                                        gmask[:].rearrange("p t g -> p (t g)").unsqueeze(2)
                                        .broadcast_to([P, NT * NG1, E1 // NG1]), ALU.mult))
            for t in range(NT):
                add(lambda t=t: v.max(top8[:, t, :], masked[:, t, :]), True)
            for t in range(NT):
                add(lambda t=t: v.match_replace(hit64[:, t, :], top8[:, t, :], masked[:, t, :], TAKEN), True)
            add(lambda: v.scalar_tensor_tensor(wsel[:], hit64[:], TAKEN, sc[:], ALU.is_equal, ALU.mult))
            add(lambda: v.reduce_sum(wsum[:], wsel[:], AX.X))
            add(lambda: v.tensor_scalar(wsum[:], wsum[:], 1e-20, None, ALU.add))
            add(lambda: v.reciprocal(wrec[:], wsum[:]))
            add(lambda: v.tensor_scalar(wrec[:], wrec[:], 2.5, None, ALU.mult))
            add(lambda: v.tensor_tensor(cwt[:], wsel[:], wrec[:].unsqueeze(2).broadcast_to([P, NT, E1]), ALU.mult))
            add(lambda: v.tensor_copy(cc[:, :, 0:E1], cwt[:]))
            add(lambda: v.tensor_tensor(cc[:, :, 64:64 + E1], cwt[:], cc[:, :, 0:E1].bitcast(F32), ALU.subtract))
            assert len(steps) == R_OPS1, len(steps)
            return steps

        FO_ALL = {("f0", 0): 0, ("f0", 1): 1, ("f1", 0): 2, ("f1", 1): 3}
        F1, F1_FIRST = "f1", FO_ALL[("f1", 0)]

        GB, UB, CB, ACC, BT = bank[0], bank[1], bank[2], bank[4], bank[5]
        TB, LB = bank[3], bank[6]
        CC_STEP, SEL_STEP = 13, 7

        def f0_pe(pe, ph, fo, nxt):
            fa = FO_ALL[("f0", fo)]
            if ph:
                pe.wait_ge(x_done.sem, B * ph)

            def gate_up(b):
                if not exists(b):
                    return
                xt_c.at(B * ph).wait(pe, b, 1)
                for bk, w, c, read in ((GB, wg0, gate_c, silu_c), (UB, wu0, up0_c, gu_c)):
                    read.at(B * fo).wait(pe, b, 0)
                    for j in range(NC0):
                        ins = pe.matmul(bk[:, j * T:(j + 1) * T], w[:].rearrange("p e i -> p (e i)")[:, j * P:(j + 1) * P],
                                        xt[:, b, TAPS - 1:], start=True, stop=True)
                    c.up(ins)

            def transposed(b):
                if exists(b):
                    ffn_pe_xT(pe, b, ph, fa, False)
                elif nxt is F1 and b == B:
                    ffn_pe_xT(pe, 0, ph + 1, F1_FIRST, False)

            def logits(b):
                if exists(b):
                    ffn_pe_router(pe, b, ph, fa, wr0, R0, LB)
                elif nxt is F1 and b == B:
                    ffn_pe_router(pe, 0, ph + 1, F1_FIRST, wr1, E1, LB)

            def weights_T(b):
                if exists(b):
                    ffn_pe_ccT(pe, b, fa, route0_c.at(B * fo), CC_STEP, TB)
                elif nxt is F1:
                    ffn_pe_ccT(pe, 0, F1_FIRST, route1_c, R_OPS1, TB)

            def attention_first(b):
                if not exists(b) and nxt is not F1:
                    if b == B:
                        pe.wait_ge(att0_in, 16 * LOADS["att0"])
                    nxt.pe_prep_xT(pe, b - B, -1)
                    nxt.pe_prep_values(pe, b - B)

            def weights(b):
                if not exists(b):
                    return
                ct_c.at(B * fa).wait(pe, b, 1)
                hid0_c.at(B * fo).wait(pe, b, 0)
                for j in range(NC0):
                    ins = pe.matmul(CB[:, j * T:(j + 1) * T], sel_exp[:, 2 * j:2 * j + 2, :].rearrange("p e i -> p (e i)"),
                                    ct[:, b, :], start=True, stop=True)
                cb0_c.up(ins)

            def body(b):
                gate_up(b + 1)
                transposed(b + 2)
                hid0_c.at(B * fo).wait(pe, b, 1)
                outT0_c.at(B * fo).wait(pe, b, 0)
                for j in range(NC0):
                    ins = pe.matmul(ACC[:, 0:T], wd0[:, j, :], hid0[:, j * T:(j + 1) * T], start=(j == 0), stop=(j == NC0 - 1))
                down0_c.up(ins)
                outT0_c.at(B * fo).wait(pe, b, 1)
                x_done.at(B * ph).wait(pe, b, 0)
                for t in range(NT):
                    ins = pe.transpose(BT[:, t * P:(t + 1) * P], outT[:, t * P:(t + 1) * P], ident[:])
                back0_c.up(ins)
                weights_T(b + 1)
                logits(b + 2)
                weights(b + 1)
                attention_first(b + 2)

            if ph == 0:
                transposed(0)
                logits(0)
                transposed(1)
            gate_up(0)
            if ph == 0:
                logits(1)
            weights_T(0)
            weights(0)
            batches(pe, body, 2)

        def f0_act_xT(a, b, ph, fo):
            ffn_act_xT(a, b, ph, FO_ALL[("f0", fo)])
            xn_c.at(B * ph).wait(a, b, NT)
            xn_kept_c.at(B * fo).up(nc.scalar.activation(xn_all[:, b], xn[:], ACT.Copy))

        def f0_dve_normal(v, b, ph, fo):
            xT_c.at(B * ph).wait(v, b, 0)
            xn_kept_c.at(B * fo).wait(v, b, 0)
            ln_xn(v, b, ph)

        def f0_act(a, ph, fo, nxt):
            fa = FO_ALL[("f0", fo)]
            if ph:
                a.wait_ge(x_done.sem, B * ph)
            r0 = route0_c.at(B * fo)

            def silu(b):
                if not exists(b):
                    return
                gate_c.at(B * fo).wait(a, b, 1)
                gu_c.at(B * fo).wait(a, b, 0)
                silu_c.up(nc.scalar.activation(silu_g[:], GB[:], ACT.Silu))

            def transposed(b):
                if exists(b):
                    f0_act_xT(a, b, ph, fo)
                elif nxt is F1 and b == B:
                    ffn_act_xT(a, 0, ph + 1, F1_FIRST)

            def scores(b):
                if exists(b):
                    ffn_act_scores(a, b, fa, R0, r0, SEL_STEP - R_OPS0, LB)
                elif nxt is F1 and b == B:
                    r0.wait(a, B - 1, SEL_STEP)
                    ffn_act_scores(a, 0, F1_FIRST, E1, route1_c, 0, LB)

            def weights(b):
                if exists(b):
                    ffn_act_ct(a, b, fa, TB)
                elif nxt is F1:
                    ffn_act_ct(a, 0, F1_FIRST, TB)

            def body(b):
                silu(b + 1)
                transposed(b + 2)
                weights(b + 1)
                scores(b + 2)
                if not exists(b + 2) and nxt is not F1:
                    if b + 2 == B:
                        a.wait_ge(att0_in, 16 * LOADS["att0"])
                    nxt.act_prep(a, b + 2 - B)

            if ph == 0:
                transposed(0)
                scores(0)
                transposed(1)
            silu(0)
            if ph == 0:
                scores(1)
            weights(0)
            batches(a, body, 2)

        def f0_dve(v, ph, fo, nxt):
            fa = FO_ALL[("f0", fo)]
            if ph:
                v.wait_ge(x_done.sem, B * ph)

            def stats(b):
                if exists(b):
                    ln_stats(v, b, ph)
                elif nxt is not F1:
                    nxt.dve_prep_a(v, b - B)
                elif b == B:
                    ln_stats(v, 0, ph + 1)

            def normal(b):
                if exists(b):
                    f0_dve_normal(v, b, ph, fo)
                elif nxt is not F1:
                    if b == B:
                        xn_kept_c.at(B * fo).wait(v, B - 1, 1)
                        xT_c.at(B * ph).wait(v, B - 1, 1)
                    nxt.dve_prep_b(v, b - B)
                    nxt.dve_prep_h(v, b - B, 0)
                elif b == B:
                    xn_kept_c.at(B * fo).wait(v, B - 1, 1)
                    xT_c.at(B * ph).wait(v, B - 1, 1)
                    ln_xn(v, 0, ph + 1)

            def convolve(b, k):
                if k == 0:
                    xt_c.at(B * ph).wait(v, b, 1)
                    outT0_c.at(B * fo).wait(v, b, 0)
                    conv_c.up(v.tensor_scalar(conv[:, 0, :], xt[:, b, 0:T], cw0[:, 0:1], cb0[:, 0:1], ALU.mult, ALU.add))
                else:
                    conv_c.at(B * fo).wait(v, b, k)
                    conv_c.up(v.scalar_tensor_tensor(conv[:, k, :], xt[:, b, k:k + T], cw0[:, k:k + 1], conv[:, k - 1, :],
                                                     ALU.mult, ALU.add))

            def gate_up(b):
                silu_c.at(B * fo).wait(v, b, 1)
                up0_c.at(B * fo).wait(v, b, 1)
                hid0_c.at(B * fo).wait(v, b, 0)
                gu_c.up(v.tensor_tensor(gu[:], silu_g[:], UB[:], ALU.mult))

            def hidden(b):
                gu_c.at(B * fo).wait(v, b, 1)
                cb0_c.at(B * fo).wait(v, b, 1)
                down0_c.at(B * fo).wait(v, b, 0)
                hid0_c.up(v.tensor_tensor(hid0[:], gu[:], CB[:], ALU.mult))

            def out_T(b):
                down0_c.at(B * fo).wait(v, b, 1)
                conv_c.at(B * fo).wait(v, b, TAPS)
                back0_c.at(B * fo).wait(v, b, 0)
                outT0_c.up(v.tensor_tensor(outT[:], conv[:, TAPS - 1, :], ACC[:, 0:T], ALU.add))

            def add_out(b):
                back0_c.at(B * fo).wait(v, b, 1)
                route0_c.at(B * fo).wait(v, b, R_OPS0)
                x_done.up(v.scalar_tensor_tensor(x[:, b, :, :].rearrange("p t d -> p (t d)"), BT[:, 0:T], 0.5,
                                                 x[:, b, :, :].rearrange("p t d -> p (t d)"), ALU.mult, ALU.add))

            def body(b):
                route = route0(v, b + 1, fo) if exists(b + 1) else route1(v, 0, 0) if nxt is F1 else []

                def routed(n):
                    for _ in range(min(n, len(route))):
                        route.pop(0)()

                routed(1)
                stats(b + 2)
                routed(1)
                gate_up(b)
                routed(1)
                convolve(b, 0)
                routed(1)
                hidden(b)
                routed(1)
                normal(b + 2)
                for k in range(1, TAPS):
                    routed(1)
                    convolve(b, k)
                routed(2)
                out_T(b)
                routed(7)
                add_out(b)
                routed(R_OPS1)
                if not exists(b + 2) and nxt is not F1:
                    if b + 2 == B:
                        v.wait_ge(att0_in, 16 * LOADS["att0"])
                    nxt.dve_prep_h(v, b + 2 - B, 1)
                    nxt.dve_prep_values(v, b + 2 - B)

            if ph == 0:
                stats(0)
                normal(0)
                stats(1)
                normal(1)
                for step in route0(v, 0, fo):
                    step()
            batches(v, body, 2)

        HB, CB1 = (bank[0], bank[1]), (bank[2], bank[3])

        def up_weight(slot):
            if slot < PAIRS:
                w = wup[:].rearrange("p e i -> p (e i)")
                return [w[:, (2 * slot + c) * P:(2 * slot + c + 1) * P] for c in range(2)]
            return [wsu[:, (slot - PAIRS) * P:(slot - PAIRS + 1) * P]]

        def down_weight(slot):
            if slot < PAIRS:
                return [wdn[:, 2 * slot + c, :] for c in range(2)]
            return [wsd[:, slot - PAIRS, :]]

        def width(slot):
            return 512 if slot < PAIRS else T

        def f1_pe(pe, ph, fo, nxt):
            fa = FO_ALL[("f1", fo)]
            pe.wait_ge(x_done.sem, B * ph)
            r1 = route1_c.at(B * fo)

            def down(b, s):
                if s < 0:
                    b, s = b - 1, s + SLOTS
                if not exists(b):
                    return
                hid1_c.at(B * fo).wait(pe, b, s + 1)
                if s == 0:
                    outT1_c.at(B * fo).wait(pe, b, 0)
                ws = down_weight(s)
                for c, w in enumerate(ws):
                    ins = pe.matmul(ACC[:, 0:T], w, hid[:, s % 3, c * T:(c + 1) * T], start=(s == 0 and c == 0),
                                    stop=(s == SLOTS - 1))
                down1_c.up(ins)

            def back(b):
                outT1_c.at(B * fo).wait(pe, b, 1)
                x_done.at(B * ph).wait(pe, b, 0)
                for t in range(NT):
                    ins = pe.transpose(BT[:, t * P:(t + 1) * P], outT[:, t * P:(t + 1) * P], ident[:])
                back1_c.up(ins)

            def body(b):
                xt_c.at(B * ph).wait(pe, b, 1)
                ct_c.at(B * fa).wait(pe, b, 1)
                for s in range(SLOTS):
                    relu_c_.at(B * fo).wait(pe, b, s - 1)
                    for c, w in enumerate(up_weight(s)):
                        ins = pe.matmul(HB[s % 2][:, c * T:(c + 1) * T], w, xt[:, b, TAPS - 1:], start=True, stop=True)
                    up1_c.up(ins)
                    if s < PAIRS:
                        rc_c.at(B * fo).wait(pe, b, s - 1)
                        for c in range(2):
                            e = 4 * s + 2 * c
                            ins = pe.matmul(CB1[s % 2][:, c * T:(c + 1) * T],
                                            sel_exp[:, e:e + 2, :].rearrange("p e i -> p (e i)"), ct[:, b, :],
                                            start=True, stop=True)
                        cb1_c.up(ins)
                    down(b, s - 2)
                    if s == 3 and exists(b + 1):
                        ffn_pe_xT(pe, b + 1, ph, fa)
                    if s == 4 and exists(b - 1):
                        back(b - 1)
                    if s == 5 and exists(b + 1):
                        ffn_pe_router(pe, b + 1, ph, fa, wr1, E1)
                    if s == SLOTS - 2 and exists(b + 1):
                        ffn_pe_ccT(pe, b + 1, fa, r1, R_OPS1)
                    if not exists(b + 1) and nxt:
                        i, k = s // 9, s % 9
                        if k == 4:
                            if i == 0:
                                ct_c.at(B * fa).wait(pe, B - 1, 1)
                            nxt.pe_prep_xT(pe, i, -1)
                        if k == 6:
                            nxt.pe_prep_values(pe, i)
                        if k == 8 and i == 0:
                            nxt.pe_prep_latent(pe, 0)

            batches(pe, body, 1)
            down(B, -2)
            down(B, -1)
            back(B - 1)

        def f1_act(a, ph, fo, nxt):
            fa = FO_ALL[("f1", fo)]
            a.wait_ge(x_done.sem, B * ph)
            r1 = route1_c.at(B * fo)

            def evacuate(b):
                down1_c.at(B * fo).wait(a, b, SLOTS)
                back1_c.at(B * fo).wait(a, b, 0)
                outT1_c.up(nc.scalar.activation(outT[:], ACC[:, 0:T], ACT.Copy))

            def body(b):
                for s in range(SLOTS):
                    up1_c.at(B * fo).wait(a, b, s + 1)
                    hid1_c.at(B * fo).wait(a, b, s - 2)
                    relu_c_.up(nc.scalar.activation(relu_h[:, s % 3, 0:width(s)], HB[s % 2][:, 0:width(s)], ACT.Relu))
                    if s == 1 and exists(b - 1):
                        evacuate(b - 1)
                    if s == 3 and exists(b + 1):
                        ffn_act_xT(a, b + 1, ph, fa)
                    if s == 5 and exists(b + 1):
                        ffn_act_scores(a, b + 1, fa, E1, r1, 0)
                    if s == SLOTS - 2 and exists(b + 1):
                        ffn_act_ct(a, b + 1, fa)
                    if not exists(b + 1) and nxt:
                        if s % 9 == 4:
                            nxt.act_prep(a, s // 9)
                        if s % 9 == 6:
                            nxt.act_prep_keys(a, s // 9)

            batches(a, body, 1)
            evacuate(B - 1)

        def f1_dve(v, ph, fo, nxt):
            fa = FO_ALL[("f1", fo)]
            v.wait_ge(x_done.sem, B * ph)

            def hidden(b, s):
                if s < 0:
                    b, s = b - 1, s + SLOTS
                if not exists(b):
                    return
                down1_c.at(B * fo).wait(v, b, s - 2)
                if s < PAIRS:
                    rc_c.at(B * fo).wait(v, b, s + 1)
                    ins = v.tensor_tensor(hid[:, s % 3, :], relu_c[:, s % 2, :], relu_h[:, s % 3, :], ALU.mult)
                else:
                    relu_c_.at(B * fo).wait(v, b, s + 1)
                    ins = v.tensor_tensor(hid[:, s % 3, 0:T], relu_h[:, s % 3, 0:T], relu_h[:, s % 3, 0:T], ALU.mult)
                hid1_c.up(ins)

            def add_out(b):
                back1_c.at(B * fo).wait(v, b, 1)
                x_done.up(v.scalar_tensor_tensor(x[:, b, :, :].rearrange("p t d -> p (t d)"), BT[:, 0:T], 0.5,
                                                 x[:, b, :, :].rearrange("p t d -> p (t d)"), ALU.mult, ALU.add))

            def body(b):
                steps = route1(v, b + 1, fo) if exists(b + 1) else []
                for s in range(SLOTS):
                    hidden(b, s - 1)
                    if s < PAIRS:
                        relu_c_.at(B * fo).wait(v, b, s + 1)
                        cb1_c.at(B * fo).wait(v, b, s + 1)
                        hid1_c.at(B * fo).wait(v, b, s - 1)
                        rc_c.up(v.tensor_tensor(relu_c[:, s % 2, :], relu_h[:, s % 3, :], CB1[s % 2][:], ALU.mult))
                    if exists(b + 1):
                        if s == 0:
                            ln_stats(v, b + 1, ph)
                        if s == 2:
                            xT_c.at(B * ph).wait(v, b + 1, 0)
                            ln_xn(v, b + 1, ph)
                    if s == 4 and exists(b - 1):
                        add_out(b - 1)
                    if 6 <= s <= SLOTS - 3:
                        n = -(-R_OPS1 // (SLOTS - 8))
                        for step in steps[(s - 6) * n:(s - 5) * n]:
                            step()
                    if not exists(b + 1) and nxt:
                        i, k = s // 9, s % 9
                        if k == 0:
                            nxt.dve_prep_a(v, i)
                        if k == 2:
                            if i == 0:
                                xT_c.at(B * ph).wait(v, B - 1, 1)
                            nxt.dve_prep_b(v, i)
                        if k == 7:
                            nxt.dve_prep_keys(v, i)
                        if s == 9:
                            nxt.dve_prep_values(v, 0)

            batches(v, body, 1)
            hidden(B, -1)
            add_out(B - 1)

        SA, TA, OB, MQ, MK = (bank[0], bank[1]), (bank[2], bank[3]), bank[4], bank[5], bank[6]

        class Att:
            def __init__(self, kind):
                self.kind = kind
                self.ng = 4 if kind == 0 else 2
                self.c = A0C if kind == 0 else A1C
                self.ph = 1 if kind == 0 else 4
                self.lead = 2
                self.next = (2, 1) if kind == 0 else (5, 1)
                self.next_all = FO_ALL[("f0" if kind == 0 else "f1", 1)]
                self.dv = DH0 if kind == 0 else DC
                self.scale = float(DH0) ** -0.5 if kind == 0 else float(DK + DR) ** -0.5

            def norm(self, b, g):
                return (b + 1, g - self.ng) if g >= self.ng else (b - 1, g + self.ng) if g < 0 else (b, g)

            def wait(self, eng, name, b, g, k):
                per = self.c[name].per // self.ng
                self.c[name].wait(eng, b, g * per + k)

            def pe_project(self, pe, b, g, half):
                b, g = self.norm(b, g)
                if not exists(b):
                    return
                bk, lo, mm = ((MQ, "q_lo", "q_mm"), (MK, "k_lo" if self.kind == 0 else "q_lo2", "k_mm"))[half]
                self.wait(pe, lo, b, g, 0)
                if self.kind == 0:
                    xt_c.at(B * self.ph).wait(pe, b, 1)
                    ins = pe.matmul(bk[:, 0:T], (wq4, wk4)[half][:, g].rearrange("p c r -> p (c r)"), xt[:, b, TAPS - 1:],
                                    start=True, stop=True)
                else:
                    if isinstance(b, int):
                        pe.wait_ge(cq_one, 1)
                    cq_c.wait(pe, b, 1)
                    for i in range(2):
                        ins = pe.matmul(bk[:, i * T:(i + 1) * T], a1[:, 4 * g + 2 * half + i].rearrange("p c r -> p (c r)"),
                                        cq[:, b, :], start=True, stop=True)
                self.c[mm].up(ins)

            def pe_scores(self, pe, b, g, i):
                b, g = self.norm(b, g)
                if not exists(b):
                    return
                par, qt, pr = g % 2, i // 2, i % 2
                if i == 0:
                    self.wait(pe, "q_lo", b, g, 1)
                    if self.kind == 1:
                        kk_lo_c.wait(pe, b, 1)
                if self.kind == 0 and i < 2:
                    self.wait(pe, "k_mask", b, g, 2 * pr + 2)
                if self.kind == 1 and i == 1:
                    self.wait(pe, "q_lo2", b, g, 1)
                self.wait(pe, "row_max", b, g, i - 1)
                bk = SA[i % 2]
                if self.kind == 0:
                    ins = pe.matmul(bk[:], q0[:, g, qt * P:(qt + 1) * P],
                                    k0m[:, par, 2 * pr:2 * pr + 2, :].rearrange("p j t -> p (j t)"), start=True, stop=True)
                else:
                    for j in range(2):
                        for part in range(2):
                            ins = pe.matmul(bk[:, j * T:(j + 1) * T], q1[:, par, 2 * pr + j, qt * P:(qt + 1) * P],
                                            k1[:, b, part, :], start=(part == 0), stop=(part == 1))
                self.c["s_mm"].up(ins)

            def pe_max_transpose(self, pe, b, g):
                src, name, n = (nm, "row_max", 4) if self.kind == 0 else (shift, "shift", 2)
                self.wait(pe, name, b, g, n)
                self.wait(pe, "exp", b, g, 0)
                for qt in range(NT):
                    ins = pe.transpose(TA[1][0:4, qt * P:(qt + 1) * P], src[:, g % 2, qt, :], ident[:])
                self.c["mT"].up(ins)

            def pe_probs(self, pe, b, g, j):
                par = g % 2
                if j == 0:
                    self.wait(pe, "mt_rows", b, g, 2)
                if self.kind == 1 and j == 0:
                    self.wait(pe, "k_mask", b, g, 1)
                self.wait(pe, "exp", b, g, j - 1)
                bk = TA[j % 2]
                pe.matmul(bk[:].rearrange("p (k t) -> p k t", k=2), sel_row[:, j, :],
                          mt[:].unsqueeze(1).broadcast_to([P, 2, T]), start=True, stop=False)
                for kt in range(NT):
                    o = bk[:, kt * T:(kt + 1) * T]
                    if self.kind == 0:
                        ins = pe.matmul(o, k0m[:, par, j, kt * P:(kt + 1) * P], q0[:, g, :], start=False, stop=(kt == 1))
                    else:
                        for part in range(2):
                            ins = pe.matmul(o, k1s[:, par, part, kt * P:(kt + 1) * P], q1[:, par, j, :], start=False,
                                            stop=(kt == 1 and part == 1))
                self.c["t_mm"].up(ins)

            def pe_values(self, pe, b, g, j):
                b, g = self.norm(b, g)
                if not exists(b):
                    return
                w = self.dv + 1
                self.wait(pe, "exp", b, g, j + 1)
                if j == 0:
                    self.wait(pe, "norm", b, g, 0)
                for qt in range(NT):
                    for kt in range(NT):
                        rhs = v0[:, b, kt, 4 * g + j, :] if self.kind == 0 else v1[:, b, kt, :]
                        o = (j * NT + qt) * w
                        ins = pe.matmul(OB[:, o:o + w], probs[:, j, kt * T + qt * P:kt * T + (qt + 1) * P], rhs,
                                        start=(kt == 0), stop=(kt == 1))
                self.c["pv"].up(ins)

            def pe_out_transpose(self, pe, b):
                if not exists(b):
                    return
                self.wait(pe, "norm", b, self.ng - 1, 1)
                if exists(b + 2):
                    (self.c["v_ev"] if self.kind == 0 else cst_c).wait(pe, b, 3)
                elif is_batch(b, B - 2):
                    score_c.at(B * self.next_all).wait(pe, 0, 1)
                nb = H0 * DH0 // P if self.kind == 0 else H1 * DC // P
                for blk in range(nb):
                    for qt in range(NT):
                        ins = pe.transpose(bank[7][:, (blk * NT + qt) * P:(blk * NT + qt + 1) * P],
                                           on[:, qt, blk * P:(blk + 1) * P], ident[:])
                self.c["onT"].up(ins)

            def pe_out(self, pe, b):
                if not exists(b):
                    return
                self.c["ots"].wait(pe, b, 1)
                nb = 1 if self.kind == 0 else 2
                for qt in range(NT):
                    for blk in range(nb):
                        w = wo0[:] if self.kind == 0 else vo1[:, blk, :]
                        ins = pe.matmul(bank[7][:, qt * P:(qt + 1) * P], ots[:, (blk * NT + qt) * P:(blk * NT + qt + 1) * P],
                                        w, start=(blk == 0), stop=(blk == nb - 1))
                self.c["out_mm"].up(ins)

            def pe_prep_xT(self, pe, b, prev):
                if not exists(b):
                    return
                if exists(prev):
                    x_done.at(B * self.ph).wait(pe, prev, 1)
                ready = ((lambda e, i: xh_c.wait(e, i, NT)) if self.kind == 0 else
                         (lambda e, i: xn_c.at(B * self.ph).wait(e, i, NT)))
                (self.c["v_ev"] if self.kind == 0 else cst_c).wait(pe, b, 0)
                x_transpose(pe, b, self.ph, xh if self.kind == 0 else xn, ready)

            def pe_prep_values(self, pe, b):
                if not exists(b):
                    return
                xts_c.at(B * self.ph).wait(pe, b, 1)
                xt_c.at(B * self.ph).wait(pe, b, 1)
                if self.kind == 0:
                    for t in range(NT):
                        ins = pe.matmul(bank[7][:, t * P:(t + 1) * P], xts[:, t * P:(t + 1) * P], wqkv[:, 2 * D:3 * D],
                                        start=True, stop=True)
                    self.c["v_mm"].up(ins)
                    return
                pe.matmul(bank[7][:, 0:T], wkk[:].rearrange("p c r -> p (c r)"), xt[:, b, TAPS - 1:], start=True, stop=True)
                kk_mm_c.up(pe.matmul(bank[7][0:DC, T:2 * T], wdq[:], xt[:, b, TAPS - 1:], start=True, stop=True))

            def pe_prep_latent(self, pe, b):
                if self.kind == 0 or not exists(b):
                    return
                kk_lo_c.wait(pe, b, 1)
                for t in range(NT):
                    pe.matmul(bank[7][:, t * DC:(t + 1) * DC], xts[:, t * P:(t + 1) * P], wkk[:, 0, 0:DC], start=True, stop=True)
                cqs_c.wait(pe, b, 1)
                for t in range(NT):
                    ins = pe.matmul(bank[7][:, P + t * H1:P + (t + 1) * H1], cqs[:, t * P:(t + 1) * P], acol[:],
                                    start=True, stop=True)
                self.c["v_mm"].up(ins)

            def next_exists(self, b):
                return isinstance(b, int) and b >= B and (self.kind == 0 or b == B)

            def pe_next_xT(self, pe, b):
                if self.next_exists(b):
                    x_done.at(B * self.ph).wait(pe, b - 3, 1)
                    if b > B:
                        score_c.at(B * self.next_all).wait(pe, b - B, 0)
                    ffn_pe_xT(pe, b - B, self.next[0], self.next_all, b == B)

            def pe_next_logits(self, pe, b):
                if self.next_exists(b):
                    w, ne = (wr0, R0) if self.kind == 0 else (wr1, E1)
                    ffn_pe_router(pe, b - B, self.next[0], self.next_all, w, ne)

            def pe_next_ccT(self, pe, b):
                if self.kind == 1 and is_batch(b, B - 1):
                    x_done.at(B * self.ph).wait(pe, B - 2, 1)
                    ffn_pe_ccT(pe, 0, self.next_all, route1_c.at(B * self.next[1]), R_OPS1)

            def act_next_xT(self, a, b):
                if self.next_exists(b):
                    if self.kind == 0:
                        f0_act_xT(a, b - B, *self.next)
                    else:
                        ffn_act_xT(a, 0, self.next[0], self.next_all)

            def act_next_scores(self, a, b):
                if self.next_exists(b):
                    if self.kind == 0:
                        ffn_act_scores(a, b - B, self.next_all, R0, route0_c.at(B * self.next[1]), SEL_STEP - R_OPS0)
                    else:
                        ffn_act_scores(a, 0, self.next_all, E1, route1_c.at(B * self.next[1]), 0)

            def dve_next_stats(self, v, b):
                if self.next_exists(b):
                    ln_stats(v, b - B, self.next[0])

            def dve_next_normal(self, v, b):
                if self.next_exists(b):
                    if self.kind == 0:
                        f0_dve_normal(v, b - B, *self.next)
                    else:
                        ln_xn(v, 0, self.next[0])

            def pe(self, pe):
                pe.wait_ge(x_done.sem, B * self.ph)
                for g in range(2):
                    for half in range(2):
                        self.pe_project(pe, 0, g, half)
                for i in range(4):
                    self.pe_scores(pe, 0, 0, i)

                last = self.ng - 1

                def body(b):
                    for g in range(self.ng):
                        self.pe_max_transpose(pe, b, g)
                        self.pe_project(pe, b, g + 2, 0)
                        self.pe_values(pe, b, g - 1, 3)
                        self.pe_scores(pe, b, g + 1, 0)
                        if self.kind == 0:
                            self.pe_project(pe, b, g + 2, 1)
                        self.pe_scores(pe, b, g + 1, 1)
                        if self.kind == 1:
                            self.pe_project(pe, b, g + 2, 1)
                        self.pe_probs(pe, b, g, 0)
                        self.pe_scores(pe, b, g + 1, 2)
                        self.pe_probs(pe, b, g, 1)
                        if g == 0:
                            self.pe_prep_latent(pe, b + 1)
                        if g == last and self.kind == 1:
                            self.pe_prep_xT(pe, b + 2, b - 1)
                            self.pe_next_xT(pe, b + 2)
                            self.pe_next_ccT(pe, b)
                        if g == last and self.kind == 0:
                            self.pe_prep_values(pe, b + 2)
                            self.pe_next_logits(pe, b + 2)
                        self.pe_values(pe, b, g, 0)
                        self.pe_scores(pe, b, g + 1, 3)
                        self.pe_probs(pe, b, g, 2)
                        if g == 0:
                            self.pe_out_transpose(pe, b - 1)
                        self.pe_values(pe, b, g, 1)
                        self.pe_probs(pe, b, g, 3)
                        if g == last and self.kind == 1:
                            self.pe_prep_values(pe, b + 2)
                            self.pe_next_logits(pe, b + 2)
                        if g == 2:
                            self.pe_prep_xT(pe, b + 2, b - 1)
                            self.pe_next_xT(pe, b + 2)
                        self.pe_values(pe, b, g, 2)
                        if g == 0:
                            self.pe_out(pe, b - 1)

                batches(pe, body, self.lead)
                self.pe_values(pe, B - 1, last, 3)
                if self.kind == 0:
                    score_c.at(B * self.next_all).wait(pe, 1, 1)
                else:
                    ct_c.at(B * self.next_all).wait(pe, 0, 1)
                self.pe_out_transpose(pe, B - 1)
                self.pe_out(pe, B - 1)

            def act_split(self, a, b, g, half):
                b, g = self.norm(b, g)
                if not exists(b):
                    return
                c = self.c
                self.wait(a, ("q_mm", "k_mm")[half], b, g, 1)
                if self.kind == 1:
                    self.wait(a, "t_mm", b, g - 2, 2 * half + 2)
                    c[("q_hi", "q_hi2")[half]].up(nc.scalar.activation(
                        q1[:, g % 2, 2 * half:2 * half + 2, :].rearrange("p j t -> p (j t)"), (MQ, MK)[half][:], ACT.Copy))
                elif half == 0:
                    self.wait(a, "t_mm", b, g - 4, 4)
                    c["q_hi"].up(nc.scalar.activation(q0[:, g, :], MQ[:, 0:T], ACT.Identity, bias=bq4[:, g:g + 1]))
                else:
                    self.wait(a, "k_mask", b, g, 0)
                    c["k_hi"].up(nc.scalar.activation(k0[:], MK[:, 0:T], ACT.Identity, bias=bk4[:, g:g + 1]))

            def act_mask(self, a, b, g, j):
                b, g = self.norm(b, g)
                if not exists(b):
                    return
                self.wait(a, "k_lo", b, g, 2)
                self.wait(a, "t_mm", b, g - 2, j + 1)
                self.c["k_mask"].up(nc.scalar.activation(k0m[:, g % 2, j, :], k0[:].bitcast(F32), ACT.Copy,
                                                         scale=head_mask[:, j:j + 1]))

            def act_exp(self, a, b, g, j):
                self.wait(a, "t_mm", b, g, j + 1)
                self.wait(a, "pv", b, g, j + 1 - 4)
                self.c["exp"].up(nc.scalar.activation(probs[:, j, :], TA[j % 2][:], ACT.Exp, scale=self.scale))

            def act_out(self, a, b):
                if not exists(b):
                    return
                self.c["onT"].wait(a, b, 1)
                self.c["out_mm"].wait(a, b, 0)
                n = T if self.kind == 0 else 2 * T
                self.c["ots"].up(nc.scalar.activation(ots[:, 0:n], bank[7][:, 0:n], ACT.Copy))

            def act_prep(self, a, b):
                if not exists(b):
                    return
                self.c["v_mm"].wait(a, b, 0)
                if self.kind == 0:
                    x_evacuate(a, b, self.ph, bias=bet[:, 0:1], scale=gam[:, 0:1])
                else:
                    x_evacuate(a, b, self.ph)

            def act_prep_keys(self, a, b):
                if self.kind == 0 or not exists(b):
                    return
                kk_mm_c.wait(a, b, 1)
                kk_hi_c.up(nc.scalar.activation(k1[:, b, 0, :], bank[7][:, 0:T], ACT.Identity, bias=bkk[:, 0:1]))
                cq_c.up(nc.scalar.activation(cq[0:DC, b, :], bank[7][0:DC, T:2 * T], ACT.Identity, bias=bdq[:, 0:1]))
                cqs_c.up(nc.scalar.activation(cqs[0:DC, :], bank[7][0:DC, T:2 * T], ACT.Identity, bias=bdq[:, 0:1]))

            def act(self, a):
                a.wait_ge(x_done.sem, B * self.ph)
                for g in range(2):
                    for half in range(2):
                        self.act_split(a, 0, g, half)
                    if self.kind == 0:
                        for j in range(4):
                            self.act_mask(a, 0, g, j)

                last = self.ng - 1

                def body(b):
                    for g in range(self.ng):
                        if self.kind == 0:
                            self.act_split(a, b, g + 2, 0)
                            self.act_split(a, b, g + 2, 1)
                            self.act_exp(a, b, g, 0)
                            self.act_exp(a, b, g, 1)
                            self.act_mask(a, b, g + 2, 0)
                            self.act_exp(a, b, g, 2)
                            self.act_mask(a, b, g + 2, 1)
                            if g == 0:
                                self.act_out(a, b - 1)
                            self.act_exp(a, b, g, 3)
                            self.act_mask(a, b, g + 2, 2)
                            self.act_mask(a, b, g + 2, 3)
                            if g == 2:
                                self.act_prep(a, b + 2)
                                self.act_next_xT(a, b + 2)
                            if g == 3:
                                self.act_next_scores(a, b + 2)
                        else:
                            self.act_exp(a, b, g, 0)
                            self.act_exp(a, b, g, 1)
                            self.act_split(a, b, g + 2, 0)
                            if g == 1:
                                self.act_prep(a, b + 2)
                                self.act_next_xT(a, b + 2)
                                if self.kind == 1 and is_batch(b, B - 1):
                                    ffn_act_ct(a, 0, self.next_all)
                            self.act_exp(a, b, g, 2)
                            if g == 0:
                                self.act_out(a, b - 1)
                            self.act_exp(a, b, g, 3)
                            self.act_split(a, b, g + 2, 1)
                            if g == 1:
                                self.act_prep_keys(a, b + 2)
                                self.act_next_scores(a, b + 2)

                batches(a, body, self.lead)
                self.act_out(a, B - 1)

            def dve_split(self, v, b, g, half):
                b, g = self.norm(b, g)
                if not exists(b):
                    return
                c, hi = self.c, slice(64, P)
                if self.kind == 1:
                    bk, name, src = ((MQ, "q_lo", "q_hi"), (MK, "q_lo2", "q_hi2"))[half]
                    self.wait(v, src, b, g, 1)
                    q = q1[hi, g % 2, 2 * half:2 * half + 2, :].rearrange("p j t -> p (j t)")
                    c[name].up(v.tensor_tensor(q, bk[hi, :], q.bitcast(F32), ALU.subtract))
                elif half == 0:
                    self.wait(v, "q_hi", b, g, 1)
                    c["q_lo"].up(v.scalar_tensor_tensor(q0[hi, g, :], MQ[hi, 0:T], bq4[hi, g:g + 1],
                                                        q0[hi, g, :].bitcast(F32), ALU.add, ALU.subtract))
                else:
                    self.wait(v, "k_hi", b, g, 1)
                    for r in (slice(32, 64), slice(96, 128)):
                        c["k_lo"].up(v.scalar_tensor_tensor(k0[r, :], MK[r, 0:T], bk4[r, g:g + 1], k0[r, :].bitcast(F32),
                                                            ALU.add, ALU.subtract))

            def dve_rows(self, v, b, g):
                self.wait(v, "mT", b, g, 1)
                self.wait(v, "t_mm", b, g, 0)
                self.c["mt_rows"].up(v.tensor_copy(mt[0:4, :], TA[1][0:4, 0:T]))
                self.wait(v, "mt_rows", b, g, 1)
                self.c["mt_rows"].up(v.tensor_tensor(mt[32:36, :], TA[1][0:4, 0:T], mt[0:4, :].bitcast(F32), ALU.subtract))

            def dve_normalise(self, v, b, g):
                b, g = self.norm(b, g)
                if not exists(b):
                    return
                w = self.dv + 1
                self.wait(v, "pv", b, g, 4)
                o8 = OB[:, 0:8 * w].rearrange("p (r w) -> p r w", w=w)
                self.c["recip"].up(v.reciprocal(rz[:], o8[:, :, self.dv]))
                self.wait(v, "recip", b, g, 1)
                if g == 0:
                    self.c["onT"].wait(v, b, 0)
                o4 = OB[:, 0:8 * w].rearrange("p (j q w) -> p q j w", q=NT, j=4)
                dst = on[:, :, g * 4 * self.dv:(g + 1) * 4 * self.dv].rearrange("p q (j d) -> p q j d", j=4)
                rzb = rz[:].rearrange("p (j q) -> p q j", q=NT).unsqueeze(3).broadcast_to([P, NT, 4, self.dv])
                self.c["norm"].up(v.tensor_tensor(dst, o4[:, :, :, 0:self.dv], rzb, ALU.mult))

            def dve_max(self, v, b, g, i):
                b, g = self.norm(b, g)
                if not exists(b):
                    return
                qt, pr = i // 2, i % 2
                self.wait(v, "s_mm", b, g, i + 1)
                if i == 0:
                    self.wait(v, "mT", b, g - 2, 1)
                self.c["row_max"].up(v.tensor_reduce(nm[:, g % 2, qt, 2 * pr:2 * pr + 2],
                                                     SA[i % 2][:].rearrange("p (j t) -> p j t", j=2), AX.X, ALU.max,
                                                     negate=True))

            def dve_shift(self, v, b, g):
                b, g = self.norm(b, g)
                if self.kind == 0 or not exists(b):
                    return
                cs = cst[:, b, :, 4 * g:4 * g + 4]
                self.wait(v, "row_max", b, g, 4)
                if isinstance(b, int) or True:
                    cst_c.wait(v, b, 1)
                self.c["shift"].up(v.tensor_tensor(msum[:], cs, nm[:, g % 2], ALU.subtract))
                self.wait(v, "shift", b, g, 1)
                self.c["shift"].up(v.tensor_tensor(shift[:, g % 2], cs, msum[:], ALU.subtract))

            def dve_add_out(self, v, b):
                if not exists(b):
                    return
                self.c["out_mm"].wait(v, b, 1)
                self.c["x_add"].wait(v, b, 1)
                xb = x[:, b, :, :].rearrange("p t d -> p (t d)")
                x_done.up(v.tensor_tensor(xb, xb, bank[7][:, 0:T], ALU.add))

            def dve_prep_a(self, v, b):
                if not exists(b):
                    return
                ln_stats(v, b, self.ph)

            def dve_prep_b(self, v, b):
                if not exists(b):
                    return
                if self.kind == 0:
                    x_xn_c.wait(v, b, 0)
                    xh_c.wait(v, b, 0)
                else:
                    xT_c.at(B * self.ph).wait(v, b, 0)
                ln_xn(v, b, self.ph)

            def dve_prep_h(self, v, b, part):
                if self.kind == 1 or not exists(b):
                    return
                if part == 0:
                    xn_c.at(B * self.ph).wait(v, b, NT)
                    for t in range(NT):
                        stats2_c.up(v.bn_stats(st2[:, t, :], xn[:, t, :]))
                    for t in range(NT):
                        if t == 0:
                            hold(v, b, (stats2_c, NT))
                        mv2_c.up(v.bn_aggr(mv2[:, t, :], st2[:, t, :]))
                    return
                rstd2_c.wait(v, b, 1)
                xT_c.at(B * self.ph).wait(v, b, 0)
                for t in range(NT):
                    xh_c.up(v.tensor_scalar(xh[:, t, :], xn[:, t, :], mv2[:, t, 0:1], rstd2[:, t:t + 1],
                                            ALU.subtract, ALU.mult))

            def dve_prep_keys(self, v, b):
                if self.kind == 0 or not exists(b):
                    return
                kk_hi_c.wait(v, b, 1)
                cq_c.wait(v, b, 1)
                cqs_c.wait(v, b, 1)
                kk_lo_c.up(v.scalar_tensor_tensor(k1[:, b, 1, :], bank[7][:, 0:T], bkk[:, 0:1],
                                                  k1[:, b, 0, :].bitcast(F32), ALU.add, ALU.subtract))

            def dve_prep_values(self, v, b):
                if not exists(b):
                    return
                self.c["v_mm"].wait(v, b, 1)
                if self.kind == 0:
                    for t in range(NT):
                        ins = v.tensor_tensor(v0[:, b, t, :, 0:DH0],
                                              bank[7][:, t * P:(t + 1) * P].rearrange("p (h d) -> p h d", h=H0),
                                              bvr[:].rearrange("p (h d) -> p h d", h=H0), ALU.add)
                    self.c["v_ev"].up(ins)
                else:
                    self.c["v_ev"].up(v.tensor_tensor(v1[:, b, :, 0:DC],
                                                      bank[7][:, 0:NT * DC].rearrange("p (t d) -> p t d", t=NT),
                                                      bdkvr[:].unsqueeze(1).broadcast_to([P, NT, DC]), ALU.add))
                    cst_c.up(v.tensor_copy(cst[:, b, :, :],
                                           bank[7][:, P:P + NT * H1].rearrange("p (t h) -> p t h", t=NT)))

            def dve(self, v):
                v.wait_ge(x_done.sem, B * self.ph)
                for g in range(2):
                    for half in range(2):
                        self.dve_split(v, 0, g, half)
                for i in range(4):
                    self.dve_max(v, 0, 0, i)
                self.dve_shift(v, 0, 0)

                last = self.ng - 1

                def body(b):
                    route = []
                    if is_batch(b, B - 1):
                        route = (route0 if self.kind == 0 else route1)(v, 0, self.next[1])
                    share = -(-len(route) // (2 * (self.ng - 1) or 2))

                    def routed():
                        for _ in range(min(share, len(route))):
                            route.pop(0)()

                    for g in range(self.ng):
                        self.dve_rows(v, b, g)
                        self.dve_normalise(v, b, g - 1)
                        self.dve_max(v, b, g + 1, 0)
                        if self.kind == 0:
                            self.dve_split(v, b, g + 2, 0)
                            if g == 2:
                                self.dve_prep_h(v, b + 2, 1)
                        routed()
                        self.dve_max(v, b, g + 1, 1)
                        if self.kind == 0:
                            self.dve_split(v, b, g + 2, 1)
                        if g == 0 and self.kind == 1:
                            self.dve_prep_values(v, b + 1)
                        self.dve_max(v, b, g + 1, 2)
                        if self.kind == 1:
                            self.dve_split(v, b, g + 2, 0)
                        routed()
                        if g == 0:
                            self.dve_prep_a(v, b + 2)
                            self.dve_next_stats(v, b + 2)
                        if g == 1 and self.kind == 0:
                            self.dve_prep_b(v, b + 2)
                            self.dve_next_normal(v, b + 2)
                        self.dve_max(v, b, g + 1, 3)
                        self.dve_shift(v, b, g + 1)
                        if self.kind == 1:
                            self.dve_split(v, b, g + 2, 1)
                        if g == 0:
                            self.dve_add_out(v, b - 1)
                            if self.kind == 1:
                                self.dve_prep_b(v, b + 2)
                                self.dve_next_normal(v, b + 2)
                        if g == 1:
                            self.dve_prep_h(v, b + 2, 0)
                        if g == last:
                            if self.kind == 1:
                                self.dve_prep_keys(v, b + 2)
                            else:
                                self.dve_prep_values(v, b + 2)

                batches(v, body, self.lead)
                self.dve_normalise(v, B, -1)
                self.dve_add_out(v, B - 1)

            def pool_prep(self, g_, b):
                if not exists(b):
                    return
                ln_rstd(g_, b, self.ph)
                if self.kind == 0:
                    xn_c.at(B * self.ph).wait(g_, b, NT)
                    mv2_c.wait(g_, b, NT)
                    xh_c.wait(g_, b, 0)
                    veps2_c.up(nc.gpsimd.tensor_tensor(veps2[:], mv2[:, :, 1], eps2[:], ALU.add))
                    veps2_c.wait(g_, b, 1)
                    rstd2_c.up(nc.gpsimd.tensor_tensor(rstd2[:], veps2[:], neghalf[:], ALU.pow))
                    x_xn_c.up(nc.gpsimd.tensor_tensor(x[:, b], x[:, b], xn[:], ALU.add))
                    hold_pool(g_, b, x_xn_c, 1)
                else:
                    hold_pool(g_, b, xn_c.at(B * self.ph), NT)
                bias = bo0 if self.kind == 0 else bo1
                self.c["x_add"].up(nc.gpsimd.tensor_tensor(x[:, b], x[:, b], bias[:].unsqueeze(1).broadcast_to([P, NT, D]),
                                                           ALU.add))

            def pool_keys(self, g_, b, g):
                b, g = self.norm(b, g)
                if self.kind == 0 or not exists(b):
                    return
                kk_lo_c.wait(g_, b, 1)
                self.wait(g_, "k_mask", b, g, 0)
                hold_pool(g_, b, self.c["t_mm"], (g - 2) * 4 + 4, 1)
                self.c["k_mask"].up(nc.gpsimd.tensor_copy(k1s[:, g % 2], k1[:, b].bitcast(F32)))

            def pool(self, g_):
                for b in range(self.lead):
                    self.pool_prep(g_, b)
                g_.wait_ge(x_done.sem, B * self.ph)
                self.pool_keys(g_, 0, 0)
                self.pool_keys(g_, 0, 1)

                def body(b):
                    for g in range(self.ng):
                        self.pool_keys(g_, b, g + 2)
                        if g == 0:
                            self.pool_prep(g_, b + self.lead)
                            if self.next_exists(b + 2):
                                ln_rstd(g_, b + 2 - B, self.next[0])

                batches(g_, body, self.lead)

        if True:
            A1C["k_mask"].per = 2
        att0, att1 = Att(0), Att(1)

        row = lambda ap, n: ap.rearrange("(a n) -> a n", a=1).partition_broadcast(P) if False else ap.partition_broadcast(P)
        col = lambda ap: ap.rearrange("(p a) -> p a", a=1)

        N_X, N_W0, N_ATT0, N_PRE1, N_MOE = 2, 8, 16, 18, 6

        @block.sync
        def _(sp):
            def load(dst, src, s, scattered=False):
                sp.dma_start(dst, src, allow_slow_non_contiguous=scattered).then_inc(s, 16)

            xin = I["L0_attn_x"].rearrange("b (t p) d -> p (b t) d", p=P)
            xf = x[:].rearrange("p b t d -> p (b t) d")
            load(xf[:, 0:4], xin[:, 0:4], x_in)
            load(xf[:, 4:], xin[:, 4:], x_in)
            load(wr0[:], I["L0_ffn_Wr"], w0_in)
            load(rb0[:], I["L0_ffn_router_bias"].partition_broadcast(P), w0_in)
            load(wg0[:], I["L0_ffn_Wg"].rearrange("e h i -> h e i"), w0_in)
            load(wu0[:], I["L0_ffn_Wu"].rearrange("e h i -> h e i"), w0_in)
            load(cw0[:], I["L0_ffn_conv_w"].rearrange("k a h -> h (k a)"), w0_in, True)
            load(cb0[:], col(I["L0_ffn_conv_b"]), w0_in)
            for e in range(2):
                load(wd0[e * IM0:(e + 1) * IM0], I["L0_ffn_Wd"].rearrange("(j e) i h -> e i j h", e=2)[e], w0_in)
            load(wqkv[:], I["L0_attn_w_qkv"], att0_in)
            load(gam[:], col(I["L0_attn_ln_gamma"]), att0_in)
            load(bet[:], col(I["L0_attn_ln_beta"]), att0_in)
            bqkv = I["L0_attn_b_qkv"].rearrange("(s g r) -> s r g", s=3, g=4)
            for c in range(4):
                load(bq4[32 * c:32 * c + 32], bqkv[0], att0_in, True)
                load(bk4[32 * c:32 * c + 32], bqkv[1], att0_in, True)
            load(bvr[:], I["L0_attn_b_qkv"][2 * D:3 * D].partition_broadcast(P), att0_in)
            load(wo0[:], I["L0_attn_w_out"], att0_in)
            load(bo0[:], I["L0_attn_b_out"].partition_broadcast(P), att0_in)
            load(wr1t[:], I["L1_ffn_router_w"], att0_in)
            load(cb1[:], I["L1_ffn_correction_bias"].partition_broadcast(P), att0_in)
            for dst, w, bias in ((uq, "W_UQ", "b_UQ"), (uk, "W_UK", "b_UK"), (uv, "W_UV", "b_UV")):
                load(dst[0:DC], I[f"L1_attn_{w}"], pre1_in)
                load(dst[DC:DC + 1], I[f"L1_attn_{bias}"].rearrange("(a n) -> a n", a=1), pre1_in)
            load(qr[0:DC], I["L1_attn_W_QR"].rearrange("c (h r) -> c h r", h=H1), pre1_in)
            load(qr[DC:DC + 1], I["L1_attn_b_QR"].rearrange("(a h r) -> a h r", a=1, h=H1), pre1_in)
            load(wo1[:], I["L1_attn_W_O"].rearrange("(h d) n -> d h n", h=H1), pre1_in)
            load(wdq[:], I["L1_attn_W_DQ"], pre1_in)
            load(bdq[:], col(I["L1_attn_b_DQ"]), pre1_in)
            for c in range(2):
                load(wkk[:, c, 0:DC], I["L1_attn_W_DKV"], pre1_in)
                load(wkk[:, c, DC:], I["L1_attn_W_KR"], pre1_in)
                load(bkk[64 * c:64 * c + DC], col(I["L1_attn_b_DKV"]), pre1_in)
                load(bkk[64 * c + DC:64 * c + 64], col(I["L1_attn_b_KR"]), pre1_in)
            load(bdkvr[:], I["L1_attn_b_DKV"].partition_broadcast(P), pre1_in)
            load(bo1r[:], I["L1_attn_b_O"].partition_broadcast(P), pre1_in)
            load(wup[:], I["L1_ffn_up_w"].rearrange("e h i -> h e i"), moe_in)
            for e in range(2):
                load(wdn[e * IM1:(e + 1) * IM1], I["L1_ffn_down_w"].rearrange("(j e) i h -> e i j h", e=2)[e], moe_in)
            load(wsu[:], I["L1_ffn_shared_up_w"], moe_in)
            load(wsd[:], I["L1_ffn_shared_down_w"].rearrange("(s p) h -> p s h", p=P), moe_in)
            outv = out.rearrange("b (t p) d -> b p t d", p=P)
            with sp.Fori(0, B) as b:
                sp.wait_ge(x_done.sem, b + (B * (LAST_STAGE - 1) + 1))
                sp.dma_start(outv[b], x[:, b]).then_inc(stored, 16)
            sp.wait_ge(stored, 16 * B)

        LOADS = {"w0": 8, "att0": 3 + 8 + 5, "pre1": 6 + 2 + 3 + 8 + 2, "moe": 5}

        @block.gpsimd
        def _(g):
            g.memset(ident[:], 0.0).then_inc(const_pool, 1)
            g.wait_ge(const_pool, 1)
            g.affine_select(out=ident[:], in_=ident[:], compare_op=ALU.not_equal, fill=1.0, base=0,
                            pattern=[[-1, P]], channel_multiplier=1).then_inc(const_pool, 1)
            g.memset(neghalf[:], -0.5).then_inc(const_pool, 1)
            g.memset(eps2[:], LN_EPS).then_inc(const_pool, 1)
            g.wait_ge(const_pool, 4)

            def rstd_loop(ph, first=0):
                for b in range(first, 2):
                    ln_rstd(g, b, ph)
                with g.Fori(2, B) as b:
                    ln_rstd(g, b, ph)

            def one_row():
                rstd_c.at(B * 3).wait(g, B - 1, 1)
                g.memset(cq[DC:DC + 1], 1.0).then_inc(cq_one, 1)
                g.wait_ge(cq_one, 1)

            stages = [lambda: rstd_loop(0),
                      lambda: (g.wait_ge(att0_in, 16 * LOADS["att0"]), att0.pool(g)), lambda: rstd_loop(2, 2), lambda: (rstd_loop(3), one_row()),
                      lambda: (g.wait_ge(pre_done, 1), att1.pool(g)), lambda: rstd_loop(5, 1)]
            for stage in stages[:LAST_STAGE]:
                stage()

        @block.tensor
        def _(pe):
            pe.wait_ge(ready0, 1)
            pe.wait_ge(w0_in, 16 * LOADS["w0"])

            def attention_weights():
                pe.wait_ge(x_done.sem, B)
                pe.wait_ge(pre1_in, 16 * LOADS["pre1"])
                pe.wait_ge(att0_in, 16 * LOADS["att0"])
                for i, w in enumerate((uq, uk, uv)):
                    for h in range(H1):
                        ins = pe.transpose(bank[i][:, h * (DC + 1):(h + 1) * (DC + 1)], w[:, h * DK:(h + 1) * DK],
                                           ident[0:DC + 1, 0:DC + 1])
                    ins.then_inc(pre_tr, 1)
                pe.transpose(bank[6][:, 0:E1], wr1t[:], ident[0:E1, 0:E1]).then_inc(pre_tr, 1)
                pe.wait_ge(pre_ev, 4)
                for h in range(H1):
                    ins = pe.matmul(bank[3][0:DC + 1, h * (DC + 1):(h + 1) * (DC + 1)], uqt[:, h, :], ukt[:, h, :],
                                    start=True, stop=True)
                ins.then_inc(pre_mm, 1)
                for h in range(H1):
                    blk, j = h // 4, h % 4
                    ins = pe.matmul(bank[4][32 * j:32 * j + 32, blk * D:(blk + 1) * D], uvt[:, h, 0:DC], wo1[:, h, :],
                                    start=True, stop=True, tile_position=(0, 32 * j))
                ins.then_inc(pre_mm, 1)
                for h in range(H1):
                    ins = pe.matmul(bank[5][:, 0:D], bvb[:, h, :], wo1[:, h, :], start=(h == 0), stop=(h == H1 - 1))
                ins.then_inc(pre_mm, 1)
                pe.wait_ge(pre_done, 1)

            stages = [lambda: f0_pe(pe, 0, 0, att0), lambda: (attention_weights(), att0.pe(pe)), lambda: f0_pe(pe, 2, 1, F1),
                      lambda: (pe.wait_ge(moe_in, 16 * LOADS["moe"]), f1_pe(pe, 3, 0, att1)),
                      lambda: att1.pe(pe), lambda: f1_pe(pe, 5, 1, None)]
            for stage in stages[:LAST_STAGE]:
                stage()

        @block.scalar
        def _(a):
            a.wait_ge(ready0, 1)
            stages = [lambda: f0_act(a, 0, 0, att0), lambda: (a.wait_ge(pre_done, 1), att0.act(a)), lambda: f0_act(a, 2, 1, F1), lambda: f1_act(a, 3, 0, att1),
                      lambda: att1.act(a), lambda: f1_act(a, 5, 1, None)]
            for stage in stages[:LAST_STAGE]:
                stage()

        @block.vector
        def _(v):
            v.memset(xt[:, :, 0:TAPS - 1], 0.0).then_inc(const_dve, 1)
            v.memset(pad16[:], PAD_LOW).then_inc(const_dve, 1)
            v.memset(want8[:], PAD_LOW).then_inc(const_dve, 1)
            v.memset(want8g[:], PAD_LOW).then_inc(const_dve, 1)
            v.memset(cc[:].bitcast(F32), 0.0).then_inc(const_dve, 1)
            v.memset(mt[:].bitcast(F32), 0.0).then_inc(const_dve, 1)
            v.memset(a1[:], 0.0).then_inc(const_dve, 1)
            v.memset(acol[:], 0.0).then_inc(const_dve, 1)
            v.memset(v0[:, :, :, :, DH0:], 1.0).then_inc(const_dve, 1)
            v.memset(v1[:, :, :, DC:], 1.0).then_inc(const_dve, 1)
            v.memset(cqs[:], 0.0).then_inc(const_dve, 1)
            v.wait_ge(const_pool, 4)
            v.tensor_tensor(sel_small[:], ident[:, 0:64], ident[:, 64:128], ALU.add).then_inc(const_dve, 1)
            v.wait_ge(const_dve, 12)
            v.memset(cqs[DC:DC + 1], 1.0).then_inc(const_dve, 1)
            v.tensor_copy(sel_exp[:], sel_small[:].unsqueeze(2).broadcast_to([P, 64, 64])).then_inc(const_dve, 1)
            v.wait_ge(w0_in, 16 * LOADS["w0"])
            v.wait_ge(x_in, 32)
            v.wait_ge(const_dve, 14)
            v.memset(rz[:], 0.0).then_inc(ready0, 1)
            v.wait_ge(ready0, 1)

            def attention_weights():
                v.wait_ge(x_done.sem, B)
                v.tensor_reduce(head_mask[:], ident[:].rearrange("p (c j d) -> p j c d", c=4, j=4), AX.XY,
                                ALU.add).then_inc(const_dve, 1)
                v.tensor_tensor(rz[:, 0:4], ident[:, 0:4], ident[:, 32:36], ALU.add).then_inc(const_dve, 1)
                v.wait_ge(const_dve, 16)
                v.tensor_copy(sel_row[:], rz[:, 0:4].unsqueeze(2).broadcast_to([P, 4, P])).then_inc(const_dve, 1)
                v.wait_ge(att0_in, 16 * LOADS["att0"])
                for dst, o in ((wq4, 0), (wk4, D)):
                    v.tensor_copy(dst[:], wqkv[:, o:o + D].rearrange("p (g r) -> p g r", g=4).unsqueeze(2)
                                  .broadcast_to([P, 4, 4, 32])).then_inc(const_dve, 1)
                v.wait_ge(pre1_in, 16 * LOADS["pre1"])
                v.wait_ge(pre_tr, 4)
                for i, dst in enumerate((uqt, ukt, uvt)):
                    v.tensor_copy(dst[:], bank[i][:, 0:H1 * (DC + 1)].rearrange("p (h c) -> p h c",
                                                                                h=H1)).then_inc(const_dve, 1)
                v.tensor_copy(wr1[:], bank[6][:, 0:E1]).then_inc(const_dve, 1)
                v.wait_ge(const_dve, 23)
                v.tensor_copy(bvb, uvt[:, :, DC:DC + 1].broadcast_to([P, H1, P])).then_inc(pre_ev, 4)
                v.wait_ge(pre_mm, 1)
                m = bank[3][0:DC + 1, 0:H1 * (DC + 1)].rearrange("p (h c) -> p h c", h=H1)
                for c in range(2):
                    v.tensor_copy(a1[0:DC + 1, :, c, 0:DC], m[:, :, 0:DC]).then_inc(const_dve, 1)
                    v.tensor_copy(a1[0:DC + 1, :, c, DC:], qr[:]).then_inc(const_dve, 1)
                v.tensor_copy(acol[0:DC + 1, :], m[:, :, DC]).then_inc(const_dve, 1)
                v.wait_ge(pre_mm, 2)
                v.tensor_copy(vo1[:], bank[4][:, 0:2 * D].rearrange("p (b n) -> p b n", b=2)).then_inc(const_dve, 1)
                v.wait_ge(pre_mm, 3)
                v.tensor_tensor(bo1[:], bank[5][:, 0:D], bo1r[:], ALU.add).then_inc(const_dve, 1)
                v.wait_ge(const_dve, 30)
                v.memset(rz[:], 0.0).then_inc(pre_done, 1)
                v.wait_ge(pre_done, 1)

            stages = [lambda: f0_dve(v, 0, 0, att0), lambda: (attention_weights(), att0.dve(v)), lambda: f0_dve(v, 2, 1, F1), lambda: f1_dve(v, 3, 0, att1),
                      lambda: att1.dve(v), lambda: f1_dve(v, 5, 1, None)]
            for stage in stages[:LAST_STAGE]:
                stage()


_INS = ['L0_attn_x', 'L0_attn_ln_gamma', 'L0_attn_ln_beta', 'L0_attn_w_qkv', 'L0_attn_b_qkv', 'L0_attn_w_out',
        'L0_attn_b_out', 'L0_ffn_Wr', 'L0_ffn_router_bias', 'L0_ffn_Wg', 'L0_ffn_Wu', 'L0_ffn_Wd', 'L0_ffn_conv_w',
        'L0_ffn_conv_b', 'L1_attn_W_DQ', 'L1_attn_b_DQ', 'L1_attn_W_UQ', 'L1_attn_b_UQ', 'L1_attn_W_DKV',
        'L1_attn_b_DKV', 'L1_attn_W_UK', 'L1_attn_b_UK', 'L1_attn_W_UV', 'L1_attn_b_UV', 'L1_attn_W_QR',
        'L1_attn_b_QR', 'L1_attn_W_KR', 'L1_attn_b_KR', 'L1_attn_W_O', 'L1_attn_b_O', 'L1_ffn_router_w',
        'L1_ffn_correction_bias', 'L1_ffn_up_w', 'L1_ffn_down_w', 'L1_ffn_shared_up_w', 'L1_ffn_shared_down_w']


def kernel(**inputs):
    import numpy as _np
    import concourse.bacc as _bacc
    from concourse import mybir as _mybir
    from concourse.bass_utils import run_bass_kernel_spmd as _run

    nc = _bacc.Bacc("TRN2", target_bir_lowering=False, num_devices=1)
    arrays, aps = {}, {}
    for name in _INS:
        a = _np.ascontiguousarray(inputs[name])
        arrays[f"in_{name}"] = a
        aps[name] = nc.dram_tensor(f"in_{name}", a.shape, _mybir.dt.from_np(a.dtype), kind="ExternalInput").ap()
    shape = inputs["L0_attn_x"].shape
    out = nc.dram_tensor("out_0", shape, _mybir.dt.from_np(_np.dtype("float32")), kind="ExternalOutput").ap()
    macaron_kernel(nc, aps, out)
    r = _run(nc, [arrays], core_ids=[0])
    return r.results[0]["out_0"]
```

```python
from contextlib import ExitStack

import concourse.bass as bass
from concourse import mybir

ALU = mybir.AluOpType
ACT = mybir.ActivationFunctionType
AX = mybir.AxisListType
F32 = mybir.dt.float32
F32R = mybir.dt.float32r

P = 128
D = 128
LN_EPS = 1e-5
PAD_LOW = -3e38
TAKEN = -2e38
LOW = -1e30


class Count:

    def __init__(self, sem, per, base=0):
        self.sem, self.per, self.base = sem, per, base

    def at(self, base):
        return Count(self.sem, self.per, base)

    def wait(self, eng, b, k):
        k = k + self.base * self.per
        if isinstance(b, int):
            if b * self.per + k > 0:
                eng.wait_ge(self.sem, b * self.per + k)
        else:
            assert self.per + k > 0
            eng.wait_ge(self.sem, b * self.per + k)

    def up(self, ins):
        return ins.then_inc(self.sem, 1)


def macaron_kernel(nc, I, out):
    B, T, _ = I["L0_attn_x"].shape
    NT = T // P
    E0, IM0 = I["L0_ffn_Wg"].shape[0], I["L0_ffn_Wg"].shape[2]
    R0 = I["L0_ffn_Wr"].shape[1]
    TAPS = I["L0_ffn_conv_w"].shape[0]
    NC0 = E0 * IM0 // P
    E1, _, IM1 = I["L1_ffn_up_w"].shape
    NG1, TOPG = 8, 4
    NC1 = E1 * IM1 // P
    NSH = I["L1_ffn_shared_up_w"].shape[1] // P
    PAIRS = NC1 // 2
    SLOTS = PAIRS + NSH
    H0, DH0 = 16, 8
    H1, DC, DR = 8, 32, 32
    DK = 128
    assert T == 256 and NT == 2 and SLOTS % 6 == 0 and H0 * DH0 == D and NC0 == 2 and TAPS == 4

    with ExitStack() as ctx:
        def sb(name, shape, dt=F32):
            return ctx.enter_context(nc.sbuf_tensor(name, shape, dt))

        def sem(name):
            return ctx.enter_context(nc.semaphore(name))

        def count(name, per=1):
            return Count(sem(name), per)

        bank = [ctx.enter_context(nc.psum_tensor(f"bank{i}", [P, 512], F32)) for i in range(8)]

        ident = sb("ident", [P, P])
        neghalf = sb("neghalf", [P, NT])
        eps2 = sb("eps2", [P, NT])
        cell = sb("cell", [P, 2])
        cell_pool = sb("cell_pool", [P, 2, NT])
        head_mask = sb("head_mask", [P, 4])
        sel_small = sb("sel_small", [P, 64])
        sel_exp = sb("sel_exp", [P, 64, 64], F32R)
        sel_row = sb("sel_row", [P, 4, P], F32R)

        x = sb("x", [P, B, NT, D])
        xt = sb("xt", [P, B, TAPS - 1 + T])
        xts = sb("xts", [P, T])
        xn = sb("xn", [P, NT, D])
        xh = sb("xh", [P, NT, D])
        st = sb("st", [P, NT, 6])
        mv = sb("mv", [P, NT, 2])
        veps = sb("veps", [P, NT])
        rstd = sb("rstd", [P, NT])
        st2 = sb("st2", [P, NT, 6])
        mv2 = sb("mv2", [P, NT, 2])
        veps2 = sb("veps2", [P, NT])
        rstd2 = sb("rstd2", [P, NT])

        area = sb("area", [P, 4096])

        def part(at, *shape, rows=P):
            n = 1
            for k in shape:
                n *= k
            names = "abcd"[:len(shape)]
            return area[0:rows, at:at + n].rearrange(f"p ({' '.join(names)}) -> p {' '.join(names)}",
                                                     **dict(zip(names, shape)))

        wr0 = sb("wr0", [P, R0])
        rb0 = sb("rb0", [P, R0])
        wg0 = sb("wg0", [P, E0, IM0])
        wu0 = sb("wu0", [P, E0, IM0])
        wd0 = sb("wd0", [P, NC0, D])
        cw0 = sb("cw0", [P, TAPS])
        cb0 = sb("cb0", [P, 1])
        gam = sb("gam", [P, 1])
        bet = sb("bet", [P, 1])
        wqkv = sb("wqkv", [P, 3 * D])
        wq4 = sb("wq4", [P, 4, 4, 32])
        wk4 = sb("wk4", [P, 4, 4, 32])
        bq4 = sb("bq4", [P, 4])
        bk4 = sb("bk4", [P, 4])
        bvr = sb("bvr", [P, D])
        wo0 = sb("wo0", [P, D])
        bo0 = sb("bo0", [P, D])
        wr1 = sb("wr1", [P, E1])
        wr1t = sb("wr1t", [E1, D])
        cb1 = sb("cb1", [P, E1])
        wdn = sb("wdn", [P, NC1, D])
        wup_hi = sb("wup_hi", [P, E1 * IM1], F32R)
        wup_lo = sb("wup_lo", [P, E1 * IM1], F32R)
        wsu_hi = sb("wsu_hi", [P, NSH * P], F32R)
        wsu_lo = sb("wsu_lo", [P, NSH * P], F32R)
        wsd = sb("wsd", [P, NSH, D])
        wup = wdn[:].rearrange("p j d -> p (j d)").rearrange("p (e i) -> p e i", e=E1)
        wsu = wsd[:].rearrange("p j d -> p (j d)")
        uq, uk, uv = (part(i * H1 * DK, H1 * DK, rows=DC + 1) for i in range(3))
        qr = sb("qr", [DC + 1, H1, DR])
        uqt = sb("uqt", [P, H1, DC + 1])
        ukt = sb("ukt", [P, H1, DC + 1])
        uvt = sb("uvt", [P, H1, DC + 1])
        wo1 = sb("wo1", [P, H1, D])
        wdq = sb("wdq", [P, DC])
        bdq = sb("bdq", [DC, 1])
        wkk = sb("wkk", [P, 2, DC + DR])
        bkk = sb("bkk", [P, 1])
        bdkvr = sb("bdkvr", [P, DC])
        bo1r = sb("bo1r", [P, D])
        a1 = sb("a1", [P, H1, 2, DC + DR])
        acol = sb("acol", [P, H1])
        vo1 = sb("vo1", [P, 2, D])
        bvb = part(3 * H1 * DK, H1, P)
        bo1 = sb("bo1", [P, D])

        k0m = sb("k0m", [P, 2, 4, T], F32R)
        xt_hi = k0m[:].rearrange("p g j t -> p (g j t)").rearrange("p (b t) -> p b t", b=B)
        cq = sb("cq", [P, B, T])
        xn_all = cq[:].rearrange("p b (t d) -> p b t d", t=NT)
        sc = sb("sc", [P, NT, E1])
        sfc = sb("sfc", [P, NT, E1])
        pad16 = sb("pad16", [P, NT, 16])
        top8 = sb("top8", [P, NT, 8])
        want8 = sb("want8", [P, NT, 8])
        want8g = sb("want8g", [P, NT, 8])
        hit16 = sb("hit16", [P, NT, 16])
        wsel = sb("wsel", [P, NT, E1])
        wsum = sb("wsum", [P, NT])
        wrec = sb("wrec", [P, NT])
        cwt = sb("cwt", [P, NT, E1])
        cc = sb("cc", [P, NT, P], F32R)
        k1 = sb("k1", [P, B, 2, T], F32R)
        ct = k1[:, :, 0, :]
        xt_lo = k1[:, :, 1, :]
        s46 = sb("s46", [P, NT])
        s46h = sb("s46h", [P, NT])
        c7h = sb("c7h", [P, NT])
        skip_u = sb("skip_u", [P, NT, D])
        skip_v = sb("skip_v", [P, NT, D])
        g_max = sb("g_max", [P, NT * NG1])
        g_eq = sb("g_eq", [P, NT, E1])
        g_cnt = sb("g_cnt", [P, NT * NG1])
        g_rest = sb("g_rest", [P, NT, E1])
        g_m2 = sb("g_m2", [P, NT * NG1])
        g_d = sb("g_d", [P, NT * NG1])
        g_d2 = sb("g_d2", [P, NT * NG1])
        g_m2b = sb("g_m2b", [P, NT * NG1])
        gmask = sb("gmask", [P, NT, NG1])
        masked = sb("masked", [P, NT, E1])
        hit64 = sb("hit64", [P, NT, E1])
        relu_h = part(0, 3, 512)
        hid = part(1536, 3, 512)
        relu_c = part(3072, 2, 512)
        outT = sb("outT", [P, T])
        conv = part(3072, 2, T)
        hid0 = part(3584, 512)

        q0 = sb("q0", [P, 4, T], F32R)
        k0 = sb("k0", [P, T], F32R)
        v0 = sb("v0", [P, B, NT, H0, DH0 + 1])
        q1 = sb("q1", [P, 2, 4, T], F32R)
        k1s = sb("k1s", [P, 2, 2, T], F32R)
        cqs = sb("cqs", [P, T])
        v1 = sb("v1", [P, B, NT, DC + 1])
        cst = sb("cst", [P, B, NT, H1])
        nm = sb("nm", [P, 2, NT, 4])
        msum = sb("msum", [P, NT, 4])
        shift = sb("shift", [P, 2, NT, 4])
        mt = sb("mt", [P, T], F32R)
        probs = part(0, 4, 512)
        rz = sb("rz", [P, 8])
        on = sb("on", [P, NT, H1 * DC])
        ots = sb("ots", [P, 512])
        gu = on[:].rearrange("p q c -> p (q c)")
        silu_g = ots

        x_in, w0_in, att0_in, pre1_in, moe_in, down_in = (sem(n) for n in ("x_in", "w0_in", "att0_in", "pre1_in", "moe_in",
                                                                         "down_in"))
        stored = sem("stored")
        cq_one = sem("cq_one")
        const_pool, const_dve = sem("const_pool"), sem("const_dve")
        pre_tr, pre_ev, pre_mm, pre_done = sem("pre_tr"), sem("pre_ev"), sem("pre_mm"), sem("pre_done")
        ready0 = sem("ready0")
        wsu_split = sem("wsu_split")
        stats_c = count("stats", NT)
        mv_c = count("mean_var", NT)
        veps_c = count("var_eps")
        rstd_c = count("rstd")
        xn_c = count("xn", NT)
        xT_c = count("xT_psum")
        xts_c = count("xT_stage")
        xt_c = count("xT_all")
        x_done = count("x_done")
        logit_c = count("logits")
        score_c = count("scores")
        R_OPS0, R_OPS1 = 21, 29
        route0_c = count("route0", R_OPS0)
        route1_c = count("route1", R_OPS1)
        ccT_c = count("ccT_psum")
        ct_c = count("ct_all")
        xn_kept_c = count("xn_kept")
        xt_low_c = count("xT_low")
        up_split_c = count("up_weights_split", 2)
        gate_c, up0_c, cb0_c = count("gate_psum"), count("up_psum"), count("comb0_psum")
        silu_c, gu_c, hid0_c = count("silu"), count("gate_up"), count("hid0")
        conv_c = count("conv", 4)
        down0_c, outT0_c, back0_c = count("down0_psum"), count("outT0"), count("back0_psum")
        up1_c = count("up1_psum", SLOTS)
        cb1_c = count("comb1_psum", PAIRS)
        relu_c_ = count("relu1", SLOTS)
        rc_c = count("relu_comb", PAIRS)
        hid1_c = count("hid1", SLOTS)
        down1_c = count("down1_psum", SLOTS)
        outT1_c, back1_c = count("outT1"), count("back1_psum")

        def make_attention_counts(tag, ng):
            c = {}
            for name, per in (("q_mm", 1), ("k_mm", 1), ("q_hi", 1), ("q_hi2", 1), ("k_hi", 1), ("q_lo", 1), ("q_lo2", 1),
                              ("k_lo", 2), ("k_mask", 4), ("s_mm", 4), ("row_max", 4), ("shift", 2), ("mT", 1),
                              ("mt_rows", 2), ("t_mm", 4), ("exp", 4), ("pv", 4), ("recip", 1), ("norm", 1)):
                c[name] = count(f"{tag}_{name}", per * ng)
            return c

        A0C = make_attention_counts("a0", 4)
        A1C = make_attention_counts("a1", 2)
        A1C["k_mask"].per = 2
        for c, tag in ((A0C, "a0"), (A1C, "a1")):
            for name in ("v_mm", "v_ev", "onT", "ots", "out_mm", "x_add"):
                c[name] = count(f"{tag}_{name}")
        stats2_c = count("stats2", NT)
        mv2_c = count("mean_var2", NT)
        veps2_c = count("var_eps2")
        rstd2_c = count("rstd2")
        xh_c = count("xh", NT)
        x_xn_c = count("x_plus_xn")
        kk_mm_c, kk_hi_c, kk_lo_c, cq_c, cqs_c = (count(n) for n in ("kk_mm", "kk_hi", "kk_lo", "cq_ev", "cq_stage"))
        cst_c = count("cst_ev")

        block = ctx.enter_context(nc.Block())

        def batches(eng, body, lead):
            body(0)
            with eng.Fori(1, B - lead) as b:
                body(b)
            for b in range(B - lead, B):
                body(b)

        def hold(v, b, *waits, which=0):
            for c, k in waits:
                c.wait(v, b, k)
            if not isinstance(b, int):
                v.memset(cell[:, which:which + 1], 0.0)

        def hold_pool(g, b, c, k, which=0):
            c.wait(g, b, k)
            if not isinstance(b, int):
                nc.gpsimd.tensor_tensor(cell_pool[:, which], neghalf[:], eps2[:], ALU.add)

        def is_batch(b, k):
            return isinstance(b, int) and b == k

        def exists(b):
            return not isinstance(b, int) or 0 <= b < B

        def ln_stats(v, b, ph):
            if ph and isinstance(b, int):
                x_done.at(B * (ph - 1)).wait(v, b, 1)
            for t in range(NT):
                stats_c.up(v.bn_stats(st[:, t, :], x[:, b, t, :]))
            for t in range(NT):
                if t == 0:
                    hold(v, b, (stats_c.at(B * ph), NT), (rstd_c.at(B * ph), 0))
                mv_c.up(v.bn_aggr(mv[:, t, :], st[:, t, :]))

        def ln_rstd(g, b, ph):
            mv_c.at(B * ph).wait(g, b, NT)
            xn_c.at(B * ph).wait(g, b, 0)
            veps_c.up(nc.gpsimd.tensor_tensor(veps[:], mv[:, :, 1], eps2[:], ALU.add))
            veps_c.at(B * ph).wait(g, b, 1)
            rstd_c.up(nc.gpsimd.tensor_tensor(rstd[:], veps[:], neghalf[:], ALU.pow))

        def ln_xn(v, b, ph):
            rstd_c.at(B * ph).wait(v, b, 1)
            for t in range(NT):
                xn_c.up(v.tensor_scalar(xn[:, t, :], x[:, b, t, :], mv[:, t, 0:1], rstd[:, t:t + 1],
                                        ALU.subtract, ALU.mult))

        def x_transpose(pe, b, ph, src, ready):
            ready(pe, b)
            for t in range(NT):
                ins = pe.transpose(bank[7][:, t * P:(t + 1) * P], src[:, t, :], ident[:])
            xT_c.up(ins)

        def x_evacuate(a, b, ph, **affine):
            xT_c.at(B * ph).wait(a, b, 1)
            fn = ACT.Identity if affine else ACT.Copy
            xts_c.up(nc.scalar.activation(xts[:], bank[7][:, 0:T], fn, **affine))
            xt_c.up(nc.scalar.activation(xt[:, b, TAPS - 1:], bank[7][:, 0:T], fn, **affine))

        def ffn_pe_xT(pe, b, ph, fo, shared_bank=True):
            if shared_bank:
                ct_c.at(B * fo).wait(pe, b, 0)
            else:
                xt_c.at(B * ph).wait(pe, b, 0)
            x_transpose(pe, b, ph, xn, lambda e, i: xn_c.at(B * ph).wait(e, i, NT))

        def ffn_pe_router(pe, b, ph, fo, w, ne, bk=None):
            xts_c.at(B * ph).wait(pe, b, 1)
            xt_c.at(B * ph).wait(pe, b, 1)
            if bk is not None:
                score_c.at(B * fo).wait(pe, b, 0)
            o = bank[7] if bk is None else bk
            for t in range(NT):
                ins = pe.matmul(o[:, T + t * E1:T + t * E1 + ne], xts[:, t * P:(t + 1) * P], w[:, 0:ne],
                                start=True, stop=True)
            logit_c.up(ins)

        def ffn_pe_ccT(pe, b, fo, route, n_route, bk=None):
            route.wait(pe, b, n_route)
            if bk is not None:
                ct_c.at(B * fo).wait(pe, b, 0)
            o = bank[7] if bk is None else bk
            for t in range(NT):
                ins = pe.transpose(o[:, t * P:(t + 1) * P], cc[:, t, :].bitcast(F32), ident[:])
            ccT_c.up(ins)

        def ffn_act_xT(a, b, ph, fo):
            logit_c.at(B * fo).wait(a, b, 0)
            if fo < F1_FIRST:
                x_evacuate(a, b, ph)
                return
            xT_c.at(B * ph).wait(a, b, 1)
            xt_low_c.at(B * (fo - F1_FIRST)).wait(a, b, 0)
            xts_c.up(nc.scalar.activation(xts[:], bank[7][:, 0:T], ACT.Copy))
            xt_c.up(nc.scalar.activation(xt_hi[:, b, :], bank[7][:, 0:T], ACT.Copy))

        def f1_dve_low(v, b, ph, fo):
            xts_c.at(B * ph).wait(v, b, 1)
            xt_c.at(B * ph).wait(v, b, 1)
            xt_low_c.at(B * fo).up(v.tensor_tensor(xt_lo[:, b, :], xts[:], xt_hi[:, b, :].bitcast(F32), ALU.subtract))

        def ffn_act_scores(a, b, fo, ne, route, n_route, bk=None):
            logit_c.at(B * fo).wait(a, b, 1)
            route.wait(a, b, n_route)
            o = bank[7] if bk is None else bk
            lg = o[:, T:T + NT * E1].rearrange("p (t e) -> p t e", t=NT)[:, :, 0:ne]
            score_c.up(nc.scalar.activation(sc[:, :, 0:ne], lg, ACT.Sigmoid))

        def ffn_act_ct(a, b, fo, bk=None):
            ccT_c.at(B * fo).wait(a, b, 1)
            o = bank[7] if bk is None else bk
            ct_c.up(nc.scalar.activation(ct[:, b, :], o[:, 0:T], ACT.Copy))

        def chain(v, c, b):
            k = [0]

            def do(make, lone=False, free=0):
                if k[0] > free:
                    if lone and not free:
                        hold(v, b, (c, k[0]), which=1)
                    elif not lone:
                        c.wait(v, b, k[0] - free)
                k[0] += 1
                c.up(make())
            return do, k

        def route0(v, b, fo):
            do, k = chain(v, route0_c.at(B * fo), b)
            score_c.at(B * FO_ALL[("f0", fo)]).wait(v, b, 1)
            do(lambda: v.tensor_tensor(pad16[:, :, 0:R0], sc[:, :, 0:R0],
                                       rb0[:].unsqueeze(1).broadcast_to([P, NT, R0]), ALU.add))
            yield
            for t in range(NT):
                do(lambda: v.max(top8[:, t, :], pad16[:, t, :]), True, t)
                yield
            do(lambda: v.tensor_copy(want8[:, :, 0:2], top8[:, :, 0:2]))
            yield
            for t in range(NT):
                do(lambda: v.match_replace(hit16[:, t, :], want8[:, t, :], pad16[:, t, :], TAKEN), True, t)
                yield
            do(lambda: v.scalar_tensor_tensor(wsel[:, :, 0:R0], hit16[:, :, 0:R0], TAKEN, sc[:, :, 0:R0],
                                               ALU.is_equal, ALU.mult))
            yield
            do(lambda: v.reduce_sum(wsum[:], wsel[:, :, 0:R0], AX.X))
            yield
            do(lambda: v.tensor_scalar(wsum[:], wsum[:], 1e-9, None, ALU.add))
            yield
            do(lambda: v.reciprocal(wrec[:], wsum[:]))
            yield
            do(lambda: v.tensor_tensor(cwt[:, :, 0:R0], wsel[:, :, 0:R0], wrec[:].unsqueeze(2).broadcast_to([P, NT, R0]),
                                        ALU.mult))
            yield
            ccT_c.at(B * FO_ALL[("f0", fo)]).wait(v, b, 0)
            do(lambda: v.tensor_copy(cc[:, :, 0:R0], cwt[:, :, 0:R0]))
            yield
            do(lambda: v.tensor_tensor(cc[:, :, 64:64 + R0], cwt[:, :, 0:R0], cc[:, :, 0:R0].bitcast(F32), ALU.subtract))
            yield
            do(lambda: v.tensor_tensor(s46[:], cwt[:, :, 4], cwt[:, :, 6], ALU.add))
            yield
            do(lambda: v.tensor_scalar(c7h[:], cwt[:, :, 7], 0.5, None, ALU.mult), False, 1)
            yield
            do(lambda: v.tensor_scalar(s46h[:], s46[:], 0.5, None, ALU.mult), False, 1)
            yield
            for t in range(NT):
                xn_kept_c.at(B * fo).wait(v, b, 1)
                do(lambda: v.tensor_scalar(skip_u[:, t, :], xn_all[:, b, t, :], 0.0, c7h[:, t:t + 1],
                                           ALU.max, ALU.mult), False, 1 + t)
                yield
            for t in range(NT):
                do(lambda: v.scalar_tensor_tensor(skip_v[:, t, :], xn_all[:, b, t, :], s46h[:, t:t + 1],
                                                       skip_u[:, t, :], ALU.mult, ALU.add), False, 1)
                yield
            do(lambda: v.tensor_tensor(x[:, b, :, :], x[:, b, :, :], skip_v[:], ALU.add))
            yield
            assert k[0] == R_OPS0, k

        def route1(v, b, fo):
            do, k = chain(v, route1_c.at(B * fo), b)
            grp = lambda a: a[:].rearrange("p t (g e) -> p (t g) e", e=E1 // NG1)
            spread = lambda a: a[:].unsqueeze(2).broadcast_to([P, NT * NG1, E1 // NG1])
            score_c.at(B * FO_ALL[("f1", fo)]).wait(v, b, 1)
            ccT_c.at(B * FO_ALL[("f1", fo)]).wait(v, b, 0)
            do(lambda: v.tensor_tensor(sfc[:], sc[:], cb1[:].unsqueeze(1).broadcast_to([P, NT, E1]), ALU.add))
            yield
            do(lambda: v.reduce_max(g_max[:], grp(sfc), AX.X))
            yield
            do(lambda: v.tensor_tensor(grp(g_eq), grp(sfc), spread(g_max), ALU.is_equal))
            yield
            do(lambda: v.reduce_sum(g_cnt[:], grp(g_eq), AX.X))
            yield
            do(lambda: v.scalar_tensor_tensor(g_rest[:], g_eq[:], LOW, sfc[:], ALU.mult, ALU.add))
            yield
            do(lambda: v.reduce_max(g_m2[:], grp(g_rest), AX.X))
            yield
            do(lambda: v.tensor_scalar(g_d[:], g_cnt[:], 1.5, LOW, ALU.is_lt, ALU.mult))
            yield
            do(lambda: v.tensor_tensor(g_d2[:], g_d[:], g_max[:], ALU.add))
            yield
            do(lambda: v.tensor_tensor(g_m2b[:], g_m2[:], g_d2[:], ALU.max))
            yield
            do(lambda: v.tensor_tensor(pad16[:, :, 0:NG1], g_max[:].rearrange("p (t g) -> p t g", t=NT),
                                        g_m2b[:].rearrange("p (t g) -> p t g", t=NT), ALU.add))
            yield
            for t in range(NT):
                do(lambda: v.max(top8[:, t, :], pad16[:, t, :]), True, t)
                yield
            do(lambda: v.tensor_copy(want8g[:, :, 0:TOPG], top8[:, :, 0:TOPG]))
            yield
            for t in range(NT):
                do(lambda: v.match_replace(hit16[:, t, :], want8g[:, t, :], pad16[:, t, :], TAKEN), True, t)
                yield
            do(lambda: v.tensor_scalar(gmask[:], hit16[:, :, 0:NG1], TAKEN, None, ALU.is_equal))
            yield
            do(lambda: v.tensor_tensor(grp(masked), grp(sfc),
                                        gmask[:].rearrange("p t g -> p (t g)").unsqueeze(2)
                                        .broadcast_to([P, NT * NG1, E1 // NG1]), ALU.mult))
            yield
            for t in range(NT):
                do(lambda: v.max(top8[:, t, :], masked[:, t, :]), True, t)
                yield
            for t in range(NT):
                do(lambda: v.match_replace(hit64[:, t, :], top8[:, t, :], masked[:, t, :], TAKEN), True, t)
                yield
            do(lambda: v.scalar_tensor_tensor(wsel[:], hit64[:], TAKEN, sc[:], ALU.is_equal, ALU.mult))
            yield
            do(lambda: v.reduce_sum(wsum[:], wsel[:], AX.X))
            yield
            do(lambda: v.tensor_scalar(wsum[:], wsum[:], 1e-20, None, ALU.add))
            yield
            do(lambda: v.reciprocal(wrec[:], wsum[:]))
            yield
            do(lambda: v.tensor_scalar(wrec[:], wrec[:], 2.5, None, ALU.mult))
            yield
            do(lambda: v.tensor_tensor(cwt[:], wsel[:], wrec[:].unsqueeze(2).broadcast_to([P, NT, E1]), ALU.mult))
            yield
            do(lambda: v.tensor_copy(cc[:, :, 0:E1], cwt[:]))
            yield
            do(lambda: v.tensor_tensor(cc[:, :, 64:64 + E1], cwt[:], cc[:, :, 0:E1].bitcast(F32), ALU.subtract))
            yield
            assert k[0] == R_OPS1, k

        FO_ALL = {("f0", 0): 0, ("f0", 1): 1, ("f1", 0): 2, ("f1", 1): 3}
        F1, F1_FIRST = "f1", FO_ALL[("f1", 0)]

        GB, UB, CB, ACC, BT = bank[0], bank[1], bank[2], bank[4], bank[5]
        TB, LB = bank[3], bank[6]
        CC_STEP, SEL_STEP = 13, 7

        def f0_pe(pe, ph, fo, nxt):
            fa = FO_ALL[("f0", fo)]
            if ph:
                pe.wait_ge(x_done.sem, B * ph)

            def project(b, bk, w, c, read):
                if not exists(b):
                    return
                xt_c.at(B * ph).wait(pe, b, 1)
                read.at(B * fo).wait(pe, b, 0)
                for j in range(NC0):
                    ins = pe.matmul(bk[:, j * T:(j + 1) * T], w[:].rearrange("p e i -> p (e i)")[:, j * P:(j + 1) * P],
                                    xt[:, b, TAPS - 1:], start=True, stop=True)
                c.up(ins)

            def gate(b):
                project(b, GB, wg0, gate_c, silu_c)

            def up(b):
                project(b, UB, wu0, up0_c, gu_c)

            def transposed(b):
                if exists(b):
                    ffn_pe_xT(pe, b, ph, fa, False)
                elif nxt is F1 and b == B:
                    ffn_pe_xT(pe, 0, ph + 1, F1_FIRST, False)

            def logits(b):
                if exists(b):
                    ffn_pe_router(pe, b, ph, fa, wr0, R0, LB)
                elif nxt is F1 and b == B:
                    ffn_pe_router(pe, 0, ph + 1, F1_FIRST, wr1, E1, LB)

            def weights_T(b):
                if exists(b):
                    ffn_pe_ccT(pe, b, fa, route0_c.at(B * fo), CC_STEP, TB)
                elif nxt is F1:
                    ffn_pe_ccT(pe, 0, F1_FIRST, route1_c, R_OPS1, TB)

            def attention_xT(b):
                if not exists(b) and nxt is not F1:
                    nxt.pe_prep_xT(pe, b - B, -1)

            def attention_values(b):
                if nxt is not F1:
                    if b == 0:
                        pe.wait_ge(att0_in, 16 * LOADS["att0"])
                    nxt.pe_prep_values(pe, b)

            def weights(b):
                if not exists(b):
                    return
                ct_c.at(B * fa).wait(pe, b, 1)
                hid0_c.at(B * fo).wait(pe, b, 0)
                for j in range(NC0):
                    ins = pe.matmul(CB[:, j * T:(j + 1) * T], sel_exp[:, 2 * j:2 * j + 2, :].rearrange("p e i -> p (e i)"),
                                    ct[:, b, :], start=True, stop=True)
                cb0_c.up(ins)

            def body(b):
                up(b + 1)
                hid0_c.at(B * fo).wait(pe, b, 1)
                outT0_c.at(B * fo).wait(pe, b, 0)
                for j in range(NC0):
                    ins = pe.matmul(ACC[:, 0:T], wd0[:, j, :], hid0[:, j * T:(j + 1) * T], start=(j == 0), stop=(j == NC0 - 1))
                down0_c.up(ins)
                if is_batch(b, B - 1):
                    attention_values(0)
                transposed(b + 2)
                logits(b + 2)
                outT0_c.at(B * fo).wait(pe, b, 1)
                x_done.at(B * ph).wait(pe, b, 0)
                for t in range(NT):
                    ins = pe.transpose(BT[:, t * P:(t + 1) * P], outT[:, t * P:(t + 1) * P], ident[:])
                back0_c.up(ins)
                attention_xT(b + 2)
                weights_T(b + 1)
                gate(b + 2)
                weights(b + 1)
                if is_batch(b, B - 1):
                    attention_values(1)

            if ph == 0:
                transposed(0)
                logits(0)
                transposed(1)
            gate(0)
            up(0)
            if ph == 0:
                logits(1)
            weights_T(0)
            gate(1)
            weights(0)
            batches(pe, body, 2)

        def f0_act_xT(a, b, ph, fo):
            ffn_act_xT(a, b, ph, FO_ALL[("f0", fo)])
            xn_c.at(B * ph).wait(a, b, NT)
            xn_kept_c.at(B * fo).up(nc.scalar.activation(xn_all[:, b], xn[:], ACT.Copy))

        def f0_dve_normal(v, b, ph, fo):
            xT_c.at(B * ph).wait(v, b, 0)
            xn_kept_c.at(B * fo).wait(v, b, 0)
            ln_xn(v, b, ph)

        def f0_act(a, ph, fo, nxt):
            fa = FO_ALL[("f0", fo)]
            if ph:
                a.wait_ge(x_done.sem, B * ph)
            r0 = route0_c.at(B * fo)

            def silu(b):
                if not exists(b):
                    return
                gate_c.at(B * fo).wait(a, b, 1)
                gu_c.at(B * fo).wait(a, b, 0)
                silu_c.up(nc.scalar.activation(silu_g[:], GB[:], ACT.Silu))

            def transposed(b):
                if exists(b):
                    f0_act_xT(a, b, ph, fo)
                elif nxt is F1 and b == B:
                    ffn_act_xT(a, 0, ph + 1, F1_FIRST)

            def scores(b):
                if exists(b):
                    ffn_act_scores(a, b, fa, R0, r0, SEL_STEP - R_OPS0, LB)
                elif nxt is F1 and b == B:
                    r0.wait(a, B - 1, SEL_STEP)
                    ffn_act_scores(a, 0, F1_FIRST, E1, route1_c, 0, LB)

            def weights(b):
                if exists(b):
                    ffn_act_ct(a, b, fa, TB)
                elif nxt is F1:
                    ffn_act_ct(a, 0, F1_FIRST, TB)

            def body(b):
                silu(b + 1)
                transposed(b + 2)
                scores(b + 2)
                if not exists(b + 2) and nxt is not F1:
                    if b + 2 == B:
                        a.wait_ge(att0_in, 16 * LOADS["att0"])
                    nxt.act_prep(a, b + 2 - B)
                weights(b + 1)

            if ph == 0:
                transposed(0)
                scores(0)
                transposed(1)
            silu(0)
            if ph == 0:
                scores(1)
            weights(0)
            batches(a, body, 2)

        def f0_dve(v, ph, fo, nxt):
            fa = FO_ALL[("f0", fo)]
            if ph:
                v.wait_ge(x_done.sem, B * ph)

            def stats(b):
                if exists(b):
                    ln_stats(v, b, ph)
                elif nxt is not F1:
                    nxt.dve_prep_a(v, b - B)
                elif b == B:
                    ln_stats(v, 0, ph + 1)

            def normal(b):
                if exists(b):
                    f0_dve_normal(v, b, ph, fo)
                elif nxt is not F1:
                    if b == B:
                        xn_kept_c.at(B * fo).wait(v, B - 1, 1)
                        xT_c.at(B * ph).wait(v, B - 1, 1)
                    nxt.dve_prep_b(v, b - B)
                    nxt.dve_prep_h(v, b - B, 0)
                elif b == B:
                    xn_kept_c.at(B * fo).wait(v, B - 1, 1)
                    xT_c.at(B * ph).wait(v, B - 1, 1)
                    ln_xn(v, 0, ph + 1)

            def convolve(b, k):
                if k == 0:
                    xt_c.at(B * ph).wait(v, b, 1)
                    outT0_c.at(B * fo).wait(v, b, 0)
                    conv_c.up(v.tensor_scalar(conv[:, 0, :], xt[:, b, 0:T], cw0[:, 0:1], cb0[:, 0:1], ALU.mult, ALU.add))
                else:
                    conv_c.at(B * fo).wait(v, b, k)
                    conv_c.up(v.scalar_tensor_tensor(conv[:, k % 2, :], xt[:, b, k:k + T], cw0[:, k:k + 1], conv[:, (k - 1) % 2, :],
                                                     ALU.mult, ALU.add))

            def gate_up(b):
                silu_c.at(B * fo).wait(v, b, 1)
                up0_c.at(B * fo).wait(v, b, 1)
                hid0_c.at(B * fo).wait(v, b, 0)
                gu_c.up(v.tensor_tensor(gu[:], silu_g[:], UB[:], ALU.mult))

            def hidden(b):
                gu_c.at(B * fo).wait(v, b, 1)
                cb0_c.at(B * fo).wait(v, b, 1)
                down0_c.at(B * fo).wait(v, b, 0)
                hid0_c.up(v.tensor_tensor(hid0[:], gu[:], CB[:], ALU.mult))

            def out_T(b):
                down0_c.at(B * fo).wait(v, b, 1)
                conv_c.at(B * fo).wait(v, b, TAPS)
                back0_c.at(B * fo).wait(v, b, 0)
                outT0_c.up(v.tensor_tensor(outT[:], conv[:, (TAPS - 1) % 2, :], ACC[:, 0:T], ALU.add))

            def add_out(b):
                back0_c.at(B * fo).wait(v, b, 1)
                route0_c.at(B * fo).wait(v, b, R_OPS0)
                x_done.up(v.scalar_tensor_tensor(x[:, b, :, :].rearrange("p t d -> p (t d)"), BT[:, 0:T], 0.5,
                                                 x[:, b, :, :].rearrange("p t d -> p (t d)"), ALU.mult, ALU.add))

            def body(b):
                route = route0(v, b + 1, fo) if exists(b + 1) else route1(v, 0, 0) if nxt is F1 else iter(())

                def routed(n):
                    for _ in range(n):
                        next(route, None)

                routed(1)
                stats(b + 2)
                routed(1)
                gate_up(b)
                routed(1)
                convolve(b, 0)
                routed(1)
                hidden(b)
                if is_batch(b, B - 1) and nxt is not F1:
                    nxt.dve_prep_values(v, 0)
                routed(1)
                normal(b + 2)
                for k in range(1, TAPS):
                    routed(1)
                    convolve(b, k)
                routed(2)
                out_T(b)
                if not exists(b + 2) and nxt is not F1:
                    nxt.dve_prep_h(v, b + 2 - B, 1)
                routed(7)
                add_out(b)
                routed(R_OPS1)
                if nxt is F1 and is_batch(b, B - 2):
                    f1_dve_low(v, 0, ph + 1, 0)
                if is_batch(b, B - 2) and nxt is not F1:
                    v.wait_ge(att0_in, 16 * LOADS["att0"])
                if is_batch(b, B - 1) and nxt is not F1:
                    nxt.dve_prep_values(v, 1)

            if ph == 0:
                stats(0)
                normal(0)
                stats(1)
                normal(1)
                for _ in route0(v, 0, fo):
                    pass
            batches(v, body, 2)

        HB, CB1 = (bank[0], bank[1]), (bank[2], bank[3])

        def up_weight(slot):
            if slot < PAIRS:
                return [[w[:, (2 * slot + c) * P:(2 * slot + c + 1) * P] for w in (wup_hi, wup_lo)] for c in range(2)]
            return [[w[:, (slot - PAIRS) * P:(slot - PAIRS + 1) * P] for w in (wsu_hi, wsu_lo)]]

        def down_weight(slot):
            if slot < PAIRS:
                return [wdn[:, 2 * slot + c, :] for c in range(2)]
            return [wsd[:, slot - PAIRS, :]]

        def width(slot):
            return 512 if slot < PAIRS else T

        def f1_pe(pe, ph, fo, nxt):
            fa = FO_ALL[("f1", fo)]
            pe.wait_ge(x_done.sem, B * ph)
            r1 = route1_c.at(B * fo)

            def down(b, s):
                if s < 0:
                    b, s = b - 1, s + SLOTS
                if not exists(b):
                    return
                hid1_c.at(B * fo).wait(pe, b, s + 1)
                if s == 0:
                    outT1_c.at(B * fo).wait(pe, b, 0)
                ws = down_weight(s)
                for c, w in enumerate(ws):
                    ins = pe.matmul(ACC[:, 0:T], w, hid[:, s % 3, c * T:(c + 1) * T], start=(s == 0 and c == 0),
                                    stop=(s == SLOTS - 1))
                down1_c.up(ins)

            def back(b):
                outT1_c.at(B * fo).wait(pe, b, 1)
                x_done.at(B * ph).wait(pe, b, 0)
                for t in range(NT):
                    ins = pe.transpose(BT[:, t * P:(t + 1) * P], outT[:, t * P:(t + 1) * P], ident[:])
                back1_c.up(ins)

            def body(b):
                xt_c.at(B * ph).wait(pe, b, 1)
                xt_low_c.at(B * fo).wait(pe, b, 1)
                ct_c.at(B * fa).wait(pe, b, 1)
                for s in range(SLOTS):
                    relu_c_.at(B * fo).wait(pe, b, s - 1)
                    for c, (hi, lo) in enumerate(up_weight(s)):
                        o = HB[s % 2][:, c * T:(c + 1) * T]
                        pe.matmul(o, hi, xt_hi[:, b, :], start=True, stop=False)
                        pe.matmul(o, hi, xt_lo[:, b, :], start=False, stop=False)
                        ins = pe.matmul(o, lo, xt_hi[:, b, :], start=False, stop=True)
                    up1_c.up(ins)
                    if s < PAIRS:
                        rc_c.at(B * fo).wait(pe, b, s - 1)
                        for c in range(2):
                            e = 4 * s + 2 * c
                            ins = pe.matmul(CB1[s % 2][:, c * T:(c + 1) * T],
                                            sel_exp[:, e:e + 2, :].rearrange("p e i -> p (e i)"), ct[:, b, :],
                                            start=True, stop=True)
                        cb1_c.up(ins)
                    down(b, s - 2)
                    if s == 3 and exists(b + 1):
                        ffn_pe_xT(pe, b + 1, ph, fa)
                    if s == 4 and exists(b - 1):
                        back(b - 1)
                    if s == 5 and exists(b + 1):
                        ffn_pe_router(pe, b + 1, ph, fa, wr1, E1)
                    if s == SLOTS - 2 and exists(b + 1):
                        ffn_pe_ccT(pe, b + 1, fa, r1, R_OPS1)
                    if not exists(b + 1) and nxt:
                        i, k = s // 9, s % 9
                        if k == 4:
                            if i == 0:
                                ct_c.at(B * fa).wait(pe, B - 1, 1)
                            nxt.pe_prep_xT(pe, i, -1)
                        if k == 6:
                            nxt.pe_prep_values(pe, i)
                        if k == 8 and i == 0:
                            nxt.pe_prep_latent(pe, 0)

            batches(pe, body, 1)
            down(B, -2)
            down(B, -1)
            back(B - 1)

        def f1_act(a, ph, fo, nxt):
            fa = FO_ALL[("f1", fo)]
            a.wait_ge(x_done.sem, B * ph)
            r1 = route1_c.at(B * fo)

            def evacuate(b):
                down1_c.at(B * fo).wait(a, b, SLOTS)
                back1_c.at(B * fo).wait(a, b, 0)
                outT1_c.up(nc.scalar.activation(outT[:], ACC[:, 0:T], ACT.Copy))

            def body(b):
                for s in range(SLOTS):
                    up1_c.at(B * fo).wait(a, b, s + 1)
                    hid1_c.at(B * fo).wait(a, b, s - 2)
                    relu_c_.up(nc.scalar.activation(relu_h[:, s % 3, 0:width(s)], HB[s % 2][:, 0:width(s)], ACT.Relu))
                    if s == 1 and exists(b - 1):
                        evacuate(b - 1)
                    if s == 3 and exists(b + 1):
                        ffn_act_xT(a, b + 1, ph, fa)
                    if s == 5 and exists(b + 1):
                        ffn_act_scores(a, b + 1, fa, E1, r1, 0)
                    if s == SLOTS - 2 and exists(b + 1):
                        ffn_act_ct(a, b + 1, fa)
                    if not exists(b + 1) and nxt:
                        if s % 9 == 4:
                            nxt.act_prep(a, s // 9)
                        if s % 9 == 6:
                            nxt.act_prep_keys(a, s // 9)

            batches(a, body, 1)
            evacuate(B - 1)

        def f1_dve(v, ph, fo, nxt):
            fa = FO_ALL[("f1", fo)]
            v.wait_ge(x_done.sem, B * ph)

            def hidden(b, s):
                if s < 0:
                    b, s = b - 1, s + SLOTS
                if not exists(b):
                    return
                down1_c.at(B * fo).wait(v, b, s - 2)
                if s < PAIRS:
                    rc_c.at(B * fo).wait(v, b, s + 1)
                    ins = v.tensor_tensor(hid[:, s % 3, :], relu_c[:, s % 2, :], relu_h[:, s % 3, :], ALU.mult)
                else:
                    relu_c_.at(B * fo).wait(v, b, s + 1)
                    ins = v.tensor_tensor(hid[:, s % 3, 0:T], relu_h[:, s % 3, 0:T], relu_h[:, s % 3, 0:T], ALU.mult)
                hid1_c.up(ins)

            def add_out(b):
                back1_c.at(B * fo).wait(v, b, 1)
                x_done.up(v.scalar_tensor_tensor(x[:, b, :, :].rearrange("p t d -> p (t d)"), BT[:, 0:T], 0.5,
                                                 x[:, b, :, :].rearrange("p t d -> p (t d)"), ALU.mult, ALU.add))

            def body(b):
                route = route1(v, b + 1, fo) if exists(b + 1) else iter(())
                for s in range(SLOTS):
                    hidden(b, s - 1)
                    if s < PAIRS:
                        relu_c_.at(B * fo).wait(v, b, s + 1)
                        cb1_c.at(B * fo).wait(v, b, s + 1)
                        hid1_c.at(B * fo).wait(v, b, s - 1)
                        rc_c.up(v.tensor_tensor(relu_c[:, s % 2, :], relu_h[:, s % 3, :], CB1[s % 2][:], ALU.mult))
                    if exists(b + 1):
                        if s == 0:
                            ln_stats(v, b + 1, ph)
                        if s == 2:
                            xT_c.at(B * ph).wait(v, b + 1, 0)
                            ln_xn(v, b + 1, ph)
                        if s == 5:
                            f1_dve_low(v, b + 1, ph, fo)
                    if s == 4 and exists(b - 1):
                        add_out(b - 1)
                    if 6 <= s <= SLOTS - 3:
                        for _ in range(-(-R_OPS1 // (SLOTS - 8))):
                            next(route, None)
                    if not exists(b + 1) and nxt:
                        i, k = s // 9, s % 9
                        if k == 0:
                            nxt.dve_prep_a(v, i)
                        if k == 2:
                            if i == 0:
                                xT_c.at(B * ph).wait(v, B - 1, 1)
                            nxt.dve_prep_b(v, i)
                        if k == 7:
                            nxt.dve_prep_keys(v, i)
                        if s == 9:
                            nxt.dve_prep_values(v, 0)

            batches(v, body, 1)
            hidden(B, -1)
            add_out(B - 1)

        SA, TA, OB, MQ, MK = (bank[0], bank[1]), (bank[2], bank[3]), bank[4], bank[5], bank[6]

        class Att:
            def __init__(self, kind):
                self.kind = kind
                self.ng = 4 if kind == 0 else 2
                self.c = A0C if kind == 0 else A1C
                self.ph = 1 if kind == 0 else 4
                self.lead = 2
                self.next = (2, 1) if kind == 0 else (5, 1)
                self.next_all = FO_ALL[("f0" if kind == 0 else "f1", 1)]
                self.dv = DH0 if kind == 0 else DC
                self.scale = float(DH0) ** -0.5 if kind == 0 else float(DK + DR) ** -0.5

            def norm(self, b, g):
                return (b + 1, g - self.ng) if g >= self.ng else (b - 1, g + self.ng) if g < 0 else (b, g)

            def wait(self, eng, name, b, g, k):
                per = self.c[name].per // self.ng
                self.c[name].wait(eng, b, g * per + k)

            def pe_project(self, pe, b, g, half):
                b, g = self.norm(b, g)
                if not exists(b):
                    return
                bk, lo, mm = ((MQ, "q_lo", "q_mm"), (MK, "k_lo" if self.kind == 0 else "q_lo2", "k_mm"))[half]
                self.wait(pe, lo, b, g, 0)
                if self.kind == 0:
                    xt_c.at(B * self.ph).wait(pe, b, 1)
                    ins = pe.matmul(bk[:, 0:T], (wq4, wk4)[half][:, g].rearrange("p c r -> p (c r)"), xt[:, b, TAPS - 1:],
                                    start=True, stop=True)
                else:
                    if isinstance(b, int):
                        pe.wait_ge(cq_one, 1)
                    cq_c.wait(pe, b, 1)
                    for i in range(2):
                        ins = pe.matmul(bk[:, i * T:(i + 1) * T], a1[:, 4 * g + 2 * half + i].rearrange("p c r -> p (c r)"),
                                        cq[:, b, :], start=True, stop=True)
                self.c[mm].up(ins)

            def pe_scores(self, pe, b, g, i):
                b, g = self.norm(b, g)
                if not exists(b):
                    return
                par, qt, pr = g % 2, i // 2, i % 2
                if i == 0:
                    self.wait(pe, "q_lo", b, g, 1)
                    if self.kind == 1:
                        kk_lo_c.wait(pe, b, 1)
                if self.kind == 0 and i < 2:
                    self.wait(pe, "k_mask", b, g, 2 * pr + 2)
                if self.kind == 1 and i == 1:
                    self.wait(pe, "q_lo2", b, g, 1)
                self.wait(pe, "row_max", b, g, i - 1)
                bk = SA[i % 2]
                if self.kind == 0:
                    ins = pe.matmul(bk[:], q0[:, g, qt * P:(qt + 1) * P],
                                    k0m[:, par, 2 * pr:2 * pr + 2, :].rearrange("p j t -> p (j t)"), start=True, stop=True)
                else:
                    for j in range(2):
                        for part in range(2):
                            ins = pe.matmul(bk[:, j * T:(j + 1) * T], q1[:, par, 2 * pr + j, qt * P:(qt + 1) * P],
                                            k1[:, b, part, :], start=(part == 0), stop=(part == 1))
                self.c["s_mm"].up(ins)

            def pe_max_transpose(self, pe, b, g):
                src, name, n = (nm, "row_max", 4) if self.kind == 0 else (shift, "shift", 2)
                self.wait(pe, name, b, g, n)
                self.wait(pe, "exp", b, g, 0)
                for qt in range(NT):
                    ins = pe.transpose(TA[1][0:4, qt * P:(qt + 1) * P], src[:, g % 2, qt, :], ident[:])
                self.c["mT"].up(ins)

            def pe_probs(self, pe, b, g, j):
                par = g % 2
                if j == 0:
                    self.wait(pe, "mt_rows", b, g, 2)
                if self.kind == 1 and j == 0:
                    self.wait(pe, "k_mask", b, g, 1)
                self.wait(pe, "exp", b, g, j - 1)
                bk = TA[j % 2]
                pe.matmul(bk[:].rearrange("p (k t) -> p k t", k=2), sel_row[:, j, :],
                          mt[:].unsqueeze(1).broadcast_to([P, 2, T]), start=True, stop=False)
                for kt in range(NT):
                    o = bk[:, kt * T:(kt + 1) * T]
                    if self.kind == 0:
                        ins = pe.matmul(o, k0m[:, par, j, kt * P:(kt + 1) * P], q0[:, g, :], start=False, stop=(kt == 1))
                    else:
                        for part in range(2):
                            ins = pe.matmul(o, k1s[:, par, part, kt * P:(kt + 1) * P], q1[:, par, j, :], start=False,
                                            stop=(kt == 1 and part == 1))
                self.c["t_mm"].up(ins)

            def pe_values(self, pe, b, g, j):
                b, g = self.norm(b, g)
                if not exists(b):
                    return
                w = self.dv + 1
                self.wait(pe, "exp", b, g, j + 1)
                if j == 0:
                    self.wait(pe, "norm", b, g, 0)
                for qt in range(NT):
                    for kt in range(NT):
                        rhs = v0[:, b, kt, 4 * g + j, :] if self.kind == 0 else v1[:, b, kt, :]
                        o = (j * NT + qt) * w
                        ins = pe.matmul(OB[:, o:o + w], probs[:, j, kt * T + qt * P:kt * T + (qt + 1) * P], rhs,
                                        start=(kt == 0), stop=(kt == 1))
                self.c["pv"].up(ins)

            def pe_out_transpose(self, pe, b):
                if not exists(b):
                    return
                self.wait(pe, "norm", b, self.ng - 1, 1)
                if exists(b + 2):
                    (self.c["v_ev"] if self.kind == 0 else cst_c).wait(pe, b, 3)
                elif is_batch(b, B - 2):
                    score_c.at(B * self.next_all).wait(pe, 0, 1)
                nb = H0 * DH0 // P if self.kind == 0 else H1 * DC // P
                for blk in range(nb):
                    for qt in range(NT):
                        ins = pe.transpose(bank[7][:, (blk * NT + qt) * P:(blk * NT + qt + 1) * P],
                                           on[:, qt, blk * P:(blk + 1) * P], ident[:])
                self.c["onT"].up(ins)

            def pe_out(self, pe, b):
                if not exists(b):
                    return
                self.c["ots"].wait(pe, b, 1)
                nb = 1 if self.kind == 0 else 2
                for qt in range(NT):
                    for blk in range(nb):
                        w = wo0[:] if self.kind == 0 else vo1[:, blk, :]
                        ins = pe.matmul(bank[7][:, qt * P:(qt + 1) * P], ots[:, (blk * NT + qt) * P:(blk * NT + qt + 1) * P],
                                        w, start=(blk == 0), stop=(blk == nb - 1))
                self.c["out_mm"].up(ins)

            def pe_prep_xT(self, pe, b, prev):
                if not exists(b):
                    return
                if exists(prev):
                    x_done.at(B * self.ph).wait(pe, prev, 1)
                ready = ((lambda e, i: xh_c.wait(e, i, NT)) if self.kind == 0 else
                         (lambda e, i: xn_c.at(B * self.ph).wait(e, i, NT)))
                (self.c["v_ev"] if self.kind == 0 else cst_c).wait(pe, b, 0)
                x_transpose(pe, b, self.ph, xh if self.kind == 0 else xn, ready)

            def pe_prep_values(self, pe, b):
                if not exists(b):
                    return
                xts_c.at(B * self.ph).wait(pe, b, 1)
                xt_c.at(B * self.ph).wait(pe, b, 1)
                if self.kind == 0:
                    for t in range(NT):
                        ins = pe.matmul(bank[7][:, t * P:(t + 1) * P], xts[:, t * P:(t + 1) * P], wqkv[:, 2 * D:3 * D],
                                        start=True, stop=True)
                    self.c["v_mm"].up(ins)
                    return
                pe.matmul(bank[7][:, 0:T], wkk[:].rearrange("p c r -> p (c r)"), xt[:, b, TAPS - 1:], start=True, stop=True)
                kk_mm_c.up(pe.matmul(bank[7][0:DC, T:2 * T], wdq[:], xt[:, b, TAPS - 1:], start=True, stop=True))

            def pe_prep_latent(self, pe, b):
                if self.kind == 0 or not exists(b):
                    return
                kk_lo_c.wait(pe, b, 1)
                for t in range(NT):
                    pe.matmul(bank[7][:, t * DC:(t + 1) * DC], xts[:, t * P:(t + 1) * P], wkk[:, 0, 0:DC], start=True, stop=True)
                cqs_c.wait(pe, b, 1)
                for t in range(NT):
                    ins = pe.matmul(bank[7][:, P + t * H1:P + (t + 1) * H1], cqs[:, t * P:(t + 1) * P], acol[:],
                                    start=True, stop=True)
                self.c["v_mm"].up(ins)

            def next_exists(self, b):
                return isinstance(b, int) and b >= B and (self.kind == 0 or b == B)

            def pe_next_xT(self, pe, b):
                if self.next_exists(b):
                    x_done.at(B * self.ph).wait(pe, b - 3, 1)
                    if b > B:
                        score_c.at(B * self.next_all).wait(pe, b - B, 0)
                    ffn_pe_xT(pe, b - B, self.next[0], self.next_all, b == B)

            def pe_next_logits(self, pe, b):
                if self.next_exists(b):
                    w, ne = (wr0, R0) if self.kind == 0 else (wr1, E1)
                    ffn_pe_router(pe, b - B, self.next[0], self.next_all, w, ne)

            def pe_next_ccT(self, pe, b):
                if self.kind == 1 and is_batch(b, B - 1):
                    x_done.at(B * self.ph).wait(pe, B - 2, 1)
                    ffn_pe_ccT(pe, 0, self.next_all, route1_c.at(B * self.next[1]), R_OPS1)

            def act_next_xT(self, a, b):
                if self.next_exists(b):
                    if self.kind == 0:
                        f0_act_xT(a, b - B, *self.next)
                    else:
                        ffn_act_xT(a, 0, self.next[0], self.next_all)

            def act_next_scores(self, a, b):
                if self.next_exists(b):
                    if self.kind == 0:
                        ffn_act_scores(a, b - B, self.next_all, R0, route0_c.at(B * self.next[1]), SEL_STEP - R_OPS0)
                    else:
                        ffn_act_scores(a, 0, self.next_all, E1, route1_c.at(B * self.next[1]), 0)

            def dve_next_stats(self, v, b):
                if self.next_exists(b):
                    ln_stats(v, b - B, self.next[0])

            def dve_next_normal(self, v, b):
                if self.next_exists(b):
                    if self.kind == 0:
                        f0_dve_normal(v, b - B, *self.next)
                    else:
                        ln_xn(v, 0, self.next[0])

            def pe(self, pe):
                pe.wait_ge(x_done.sem, B * self.ph)
                for g in range(2):
                    for half in range(2):
                        self.pe_project(pe, 0, g, half)
                for i in range(4):
                    self.pe_scores(pe, 0, 0, i)

                last = self.ng - 1

                def body(b):
                    for g in range(self.ng):
                        self.pe_max_transpose(pe, b, g)
                        self.pe_project(pe, b, g + 2, 0)
                        self.pe_values(pe, b, g - 1, 3)
                        self.pe_scores(pe, b, g + 1, 0)
                        if self.kind == 0:
                            self.pe_project(pe, b, g + 2, 1)
                        self.pe_scores(pe, b, g + 1, 1)
                        if self.kind == 1:
                            self.pe_project(pe, b, g + 2, 1)
                        self.pe_probs(pe, b, g, 0)
                        self.pe_scores(pe, b, g + 1, 2)
                        self.pe_probs(pe, b, g, 1)
                        if g == 0:
                            self.pe_prep_latent(pe, b + 1)
                        if g == last and self.kind == 1:
                            self.pe_prep_xT(pe, b + 2, b - 1)
                            self.pe_next_xT(pe, b + 2)
                            self.pe_next_ccT(pe, b)
                        if g == last and self.kind == 0:
                            self.pe_prep_values(pe, b + 2)
                            self.pe_next_logits(pe, b + 2)
                        self.pe_values(pe, b, g, 0)
                        self.pe_scores(pe, b, g + 1, 3)
                        self.pe_probs(pe, b, g, 2)
                        if g == 0:
                            self.pe_out_transpose(pe, b - 1)
                        self.pe_values(pe, b, g, 1)
                        self.pe_probs(pe, b, g, 3)
                        if g == last and self.kind == 1:
                            self.pe_prep_values(pe, b + 2)
                            self.pe_next_logits(pe, b + 2)
                        if g == 2:
                            self.pe_prep_xT(pe, b + 2, b - 1)
                            self.pe_next_xT(pe, b + 2)
                        self.pe_values(pe, b, g, 2)
                        if g == 0:
                            self.pe_out(pe, b - 1)

                batches(pe, body, self.lead)
                self.pe_values(pe, B - 1, last, 3)
                if self.kind == 0:
                    score_c.at(B * self.next_all).wait(pe, 1, 1)
                else:
                    ct_c.at(B * self.next_all).wait(pe, 0, 1)
                self.pe_out_transpose(pe, B - 1)
                self.pe_out(pe, B - 1)

            def act_split(self, a, b, g, half):
                b, g = self.norm(b, g)
                if not exists(b):
                    return
                c = self.c
                self.wait(a, ("q_mm", "k_mm")[half], b, g, 1)
                if self.kind == 1:
                    self.wait(a, "t_mm", b, g - 2, 2 * half + 2)
                    c[("q_hi", "q_hi2")[half]].up(nc.scalar.activation(
                        q1[:, g % 2, 2 * half:2 * half + 2, :].rearrange("p j t -> p (j t)"), (MQ, MK)[half][:], ACT.Copy))
                elif half == 0:
                    self.wait(a, "t_mm", b, g - 4, 4)
                    c["q_hi"].up(nc.scalar.activation(q0[:, g, :], MQ[:, 0:T], ACT.Identity, bias=bq4[:, g:g + 1]))
                else:
                    self.wait(a, "k_mask", b, g, 0)
                    c["k_hi"].up(nc.scalar.activation(k0[:], MK[:, 0:T], ACT.Identity, bias=bk4[:, g:g + 1]))

            def act_mask(self, a, b, g, j):
                b, g = self.norm(b, g)
                if not exists(b):
                    return
                self.wait(a, "k_lo", b, g, 2)
                self.wait(a, "t_mm", b, g - 2, j + 1)
                self.c["k_mask"].up(nc.scalar.activation(k0m[:, g % 2, j, :], k0[:].bitcast(F32), ACT.Copy,
                                                         scale=head_mask[:, j:j + 1]))

            def act_exp(self, a, b, g, j):
                self.wait(a, "t_mm", b, g, j + 1)
                self.wait(a, "pv", b, g, j + 1 - 4)
                self.c["exp"].up(nc.scalar.activation(probs[:, j, :], TA[j % 2][:], ACT.Exp, scale=self.scale))

            def act_out(self, a, b):
                if not exists(b):
                    return
                self.c["onT"].wait(a, b, 1)
                self.c["out_mm"].wait(a, b, 0)
                n = T if self.kind == 0 else 2 * T
                self.c["ots"].up(nc.scalar.activation(ots[:, 0:n], bank[7][:, 0:n], ACT.Copy))

            def act_prep(self, a, b):
                if not exists(b):
                    return
                self.c["v_mm"].wait(a, b, 0)
                if self.kind == 0:
                    x_evacuate(a, b, self.ph, bias=bet[:, 0:1], scale=gam[:, 0:1])
                else:
                    x_evacuate(a, b, self.ph)

            def act_prep_keys(self, a, b):
                if self.kind == 0 or not exists(b):
                    return
                kk_mm_c.wait(a, b, 1)
                kk_hi_c.up(nc.scalar.activation(k1[:, b, 0, :], bank[7][:, 0:T], ACT.Identity, bias=bkk[:, 0:1]))
                cq_c.up(nc.scalar.activation(cq[0:DC, b, :], bank[7][0:DC, T:2 * T], ACT.Identity, bias=bdq[:, 0:1]))
                cqs_c.up(nc.scalar.activation(cqs[0:DC, :], bank[7][0:DC, T:2 * T], ACT.Identity, bias=bdq[:, 0:1]))

            def act(self, a):
                a.wait_ge(x_done.sem, B * self.ph)
                for g in range(2):
                    for half in range(2):
                        self.act_split(a, 0, g, half)
                    if self.kind == 0:
                        for j in range(4):
                            self.act_mask(a, 0, g, j)

                last = self.ng - 1

                def body(b):
                    for g in range(self.ng):
                        if self.kind == 0:
                            self.act_split(a, b, g + 2, 0)
                            self.act_split(a, b, g + 2, 1)
                            self.act_exp(a, b, g, 0)
                            self.act_exp(a, b, g, 1)
                            self.act_mask(a, b, g + 2, 0)
                            self.act_exp(a, b, g, 2)
                            self.act_mask(a, b, g + 2, 1)
                            if g == 0:
                                self.act_out(a, b - 1)
                            self.act_exp(a, b, g, 3)
                            self.act_mask(a, b, g + 2, 2)
                            self.act_mask(a, b, g + 2, 3)
                            if g == 2:
                                self.act_prep(a, b + 2)
                                self.act_next_xT(a, b + 2)
                            if g == 3:
                                self.act_next_scores(a, b + 2)
                        else:
                            self.act_exp(a, b, g, 0)
                            self.act_exp(a, b, g, 1)
                            self.act_split(a, b, g + 2, 0)
                            if g == 1:
                                self.act_prep(a, b + 2)
                                self.act_next_xT(a, b + 2)
                                if self.kind == 1 and is_batch(b, B - 1):
                                    ffn_act_ct(a, 0, self.next_all)
                            self.act_exp(a, b, g, 2)
                            if g == 0:
                                self.act_out(a, b - 1)
                            self.act_exp(a, b, g, 3)
                            self.act_split(a, b, g + 2, 1)
                            if g == 1:
                                self.act_prep_keys(a, b + 2)
                                self.act_next_scores(a, b + 2)

                batches(a, body, self.lead)
                self.act_out(a, B - 1)

            def dve_split(self, v, b, g, half):
                b, g = self.norm(b, g)
                if not exists(b):
                    return
                c, hi = self.c, slice(64, P)
                if self.kind == 1:
                    bk, name, src = ((MQ, "q_lo", "q_hi"), (MK, "q_lo2", "q_hi2"))[half]
                    self.wait(v, src, b, g, 1)
                    q = q1[hi, g % 2, 2 * half:2 * half + 2, :].rearrange("p j t -> p (j t)")
                    c[name].up(v.tensor_tensor(q, bk[hi, :], q.bitcast(F32), ALU.subtract))
                elif half == 0:
                    self.wait(v, "q_hi", b, g, 1)
                    c["q_lo"].up(v.scalar_tensor_tensor(q0[hi, g, :], MQ[hi, 0:T], bq4[hi, g:g + 1],
                                                        q0[hi, g, :].bitcast(F32), ALU.add, ALU.subtract))
                else:
                    self.wait(v, "k_hi", b, g, 1)
                    for r in (slice(32, 64), slice(96, 128)):
                        c["k_lo"].up(v.scalar_tensor_tensor(k0[r, :], MK[r, 0:T], bk4[r, g:g + 1], k0[r, :].bitcast(F32),
                                                            ALU.add, ALU.subtract))

            def dve_rows(self, v, b, g):
                self.wait(v, "mT", b, g, 1)
                self.wait(v, "t_mm", b, g, 0)
                self.c["mt_rows"].up(v.tensor_copy(mt[0:4, :], TA[1][0:4, 0:T]))
                self.wait(v, "mt_rows", b, g, 1)
                self.c["mt_rows"].up(v.tensor_tensor(mt[32:36, :], TA[1][0:4, 0:T], mt[0:4, :].bitcast(F32), ALU.subtract))

            def dve_normalise(self, v, b, g):
                b, g = self.norm(b, g)
                if not exists(b):
                    return
                w = self.dv + 1
                self.wait(v, "pv", b, g, 4)
                o8 = OB[:, 0:8 * w].rearrange("p (r w) -> p r w", w=w)
                self.c["recip"].up(v.reciprocal(rz[:], o8[:, :, self.dv]))
                self.wait(v, "recip", b, g, 1)
                if g == 0:
                    self.c["onT"].wait(v, b, 0)
                o4 = OB[:, 0:8 * w].rearrange("p (j q w) -> p q j w", q=NT, j=4)
                dst = on[:, :, g * 4 * self.dv:(g + 1) * 4 * self.dv].rearrange("p q (j d) -> p q j d", j=4)
                rzb = rz[:].rearrange("p (j q) -> p q j", q=NT).unsqueeze(3).broadcast_to([P, NT, 4, self.dv])
                self.c["norm"].up(v.tensor_tensor(dst, o4[:, :, :, 0:self.dv], rzb, ALU.mult))

            def dve_max(self, v, b, g, i):
                b, g = self.norm(b, g)
                if not exists(b):
                    return
                qt, pr = i // 2, i % 2
                self.wait(v, "s_mm", b, g, i + 1)
                if i == 0:
                    self.wait(v, "mT", b, g - 2, 1)
                self.c["row_max"].up(v.tensor_reduce(nm[:, g % 2, qt, 2 * pr:2 * pr + 2],
                                                     SA[i % 2][:].rearrange("p (j t) -> p j t", j=2), AX.X, ALU.max,
                                                     negate=True))

            def dve_shift(self, v, b, g):
                b, g = self.norm(b, g)
                if self.kind == 0 or not exists(b):
                    return
                cs = cst[:, b, :, 4 * g:4 * g + 4]
                self.wait(v, "row_max", b, g, 4)
                cst_c.wait(v, b, 1)
                self.c["shift"].up(v.tensor_tensor(msum[:], cs, nm[:, g % 2], ALU.subtract))
                self.wait(v, "shift", b, g, 1)
                self.c["shift"].up(v.tensor_tensor(shift[:, g % 2], cs, msum[:], ALU.subtract))

            def dve_add_out(self, v, b):
                if not exists(b):
                    return
                self.c["out_mm"].wait(v, b, 1)
                self.c["x_add"].wait(v, b, 1)
                xb = x[:, b, :, :].rearrange("p t d -> p (t d)")
                x_done.up(v.tensor_tensor(xb, xb, bank[7][:, 0:T], ALU.add))

            def dve_prep_a(self, v, b):
                if not exists(b):
                    return
                ln_stats(v, b, self.ph)

            def dve_prep_b(self, v, b):
                if not exists(b):
                    return
                if self.kind == 0:
                    x_xn_c.wait(v, b, 0)
                    xh_c.wait(v, b, 0)
                else:
                    xT_c.at(B * self.ph).wait(v, b, 0)
                ln_xn(v, b, self.ph)

            def dve_prep_h(self, v, b, part):
                if self.kind == 1 or not exists(b):
                    return
                if part == 0:
                    xn_c.at(B * self.ph).wait(v, b, NT)
                    for t in range(NT):
                        stats2_c.up(v.bn_stats(st2[:, t, :], xn[:, t, :]))
                    for t in range(NT):
                        if t == 0:
                            hold(v, b, (stats2_c, NT))
                        mv2_c.up(v.bn_aggr(mv2[:, t, :], st2[:, t, :]))
                    return
                rstd2_c.wait(v, b, 1)
                xT_c.at(B * self.ph).wait(v, b, 0)
                for t in range(NT):
                    xh_c.up(v.tensor_scalar(xh[:, t, :], xn[:, t, :], mv2[:, t, 0:1], rstd2[:, t:t + 1],
                                            ALU.subtract, ALU.mult))

            def dve_prep_keys(self, v, b):
                if self.kind == 0 or not exists(b):
                    return
                kk_hi_c.wait(v, b, 1)
                cq_c.wait(v, b, 1)
                cqs_c.wait(v, b, 1)
                kk_lo_c.up(v.scalar_tensor_tensor(k1[:, b, 1, :], bank[7][:, 0:T], bkk[:, 0:1],
                                                  k1[:, b, 0, :].bitcast(F32), ALU.add, ALU.subtract))

            def dve_prep_values(self, v, b):
                if not exists(b):
                    return
                self.c["v_mm"].wait(v, b, 1)
                if self.kind == 0:
                    for t in range(NT):
                        ins = v.tensor_tensor(v0[:, b, t, :, 0:DH0],
                                              bank[7][:, t * P:(t + 1) * P].rearrange("p (h d) -> p h d", h=H0),
                                              bvr[:].rearrange("p (h d) -> p h d", h=H0), ALU.add)
                    self.c["v_ev"].up(ins)
                else:
                    self.c["v_ev"].up(v.tensor_tensor(v1[:, b, :, 0:DC],
                                                      bank[7][:, 0:NT * DC].rearrange("p (t d) -> p t d", t=NT),
                                                      bdkvr[:].unsqueeze(1).broadcast_to([P, NT, DC]), ALU.add))
                    cst_c.up(v.tensor_copy(cst[:, b, :, :],
                                           bank[7][:, P:P + NT * H1].rearrange("p (t h) -> p t h", t=NT)))

            def dve(self, v):
                v.wait_ge(x_done.sem, B * self.ph)
                for g in range(2):
                    for half in range(2):
                        self.dve_split(v, 0, g, half)
                for i in range(4):
                    self.dve_max(v, 0, 0, i)
                self.dve_shift(v, 0, 0)

                last = self.ng - 1

                def body(b):
                    route = iter(())
                    if is_batch(b, B - 1):
                        route = (route0 if self.kind == 0 else route1)(v, 0, self.next[1])
                    share = -(-(R_OPS0 if self.kind == 0 else R_OPS1) // (2 * (self.ng - 1)))

                    def routed():
                        for _ in range(share):
                            next(route, None)

                    for g in range(self.ng):
                        self.dve_rows(v, b, g)
                        self.dve_normalise(v, b, g - 1)
                        self.dve_max(v, b, g + 1, 0)
                        if self.kind == 0:
                            self.dve_split(v, b, g + 2, 0)
                            if g == 2:
                                self.dve_prep_h(v, b + 2, 1)
                        routed()
                        self.dve_max(v, b, g + 1, 1)
                        if self.kind == 0:
                            self.dve_split(v, b, g + 2, 1)
                        if g == 0 and self.kind == 1:
                            self.dve_prep_values(v, b + 1)
                        self.dve_max(v, b, g + 1, 2)
                        if self.kind == 1:
                            self.dve_split(v, b, g + 2, 0)
                        routed()
                        if g == 0:
                            self.dve_prep_a(v, b + 2)
                            self.dve_next_stats(v, b + 2)
                        if g == 1 and self.kind == 0:
                            self.dve_prep_b(v, b + 2)
                            self.dve_next_normal(v, b + 2)
                        self.dve_max(v, b, g + 1, 3)
                        self.dve_shift(v, b, g + 1)
                        if self.kind == 1:
                            self.dve_split(v, b, g + 2, 1)
                        if g == 0:
                            self.dve_add_out(v, b - 1)
                            if self.kind == 1:
                                self.dve_prep_b(v, b + 2)
                                self.dve_next_normal(v, b + 2)
                        if g == 1:
                            self.dve_prep_h(v, b + 2, 0)
                        if g == last:
                            if self.kind == 1:
                                self.dve_prep_keys(v, b + 2)
                                if self.next_exists(b + 2):
                                    f1_dve_low(v, 0, *self.next)
                            else:
                                self.dve_prep_values(v, b + 2)

                batches(v, body, self.lead)
                self.dve_normalise(v, B, -1)
                self.dve_add_out(v, B - 1)

            def pool_prep(self, g_, b):
                if not exists(b):
                    return
                ln_rstd(g_, b, self.ph)
                if self.kind == 0:
                    xn_c.at(B * self.ph).wait(g_, b, NT)
                    mv2_c.wait(g_, b, NT)
                    xh_c.wait(g_, b, 0)
                    veps2_c.up(nc.gpsimd.tensor_tensor(veps2[:], mv2[:, :, 1], eps2[:], ALU.add))
                    veps2_c.wait(g_, b, 1)
                    rstd2_c.up(nc.gpsimd.tensor_tensor(rstd2[:], veps2[:], neghalf[:], ALU.pow))
                    x_xn_c.up(nc.gpsimd.tensor_tensor(x[:, b], x[:, b], xn[:], ALU.add))
                    hold_pool(g_, b, x_xn_c, 1)
                else:
                    hold_pool(g_, b, xn_c.at(B * self.ph), NT)
                bias = bo0 if self.kind == 0 else bo1
                self.c["x_add"].up(nc.gpsimd.tensor_tensor(x[:, b], x[:, b], bias[:].unsqueeze(1).broadcast_to([P, NT, D]),
                                                           ALU.add))

            def pool_keys(self, g_, b, g):
                b, g = self.norm(b, g)
                if self.kind == 0 or not exists(b):
                    return
                kk_lo_c.wait(g_, b, 1)
                self.wait(g_, "k_mask", b, g, 0)
                hold_pool(g_, b, self.c["t_mm"], (g - 2) * 4 + 4, 1)
                self.c["k_mask"].up(nc.gpsimd.tensor_copy(k1s[:, g % 2], k1[:, b].bitcast(F32)))

            def pool_split_up(self, g_, b):
                w = wup.rearrange("p (b e) i -> p b (e i)", b=B)[:, b, :]
                hi, lo = (d[:].rearrange("p (b n) -> p b n", b=B)[:, b, :] for d in (wup_hi, wup_lo))
                if self.next_exists(b + 2):
                    rstd_c.at(B * self.next[0]).wait(g_, b + 2 - B, 1)
                elif exists(b + 2):
                    hold_pool(g_, b, self.c["x_add"], 3, 1)
                up_split_c.up(nc.gpsimd.tensor_copy(hi, w))
                hold_pool(g_, b, up_split_c, 1, 1)
                up_split_c.up(nc.gpsimd.tensor_tensor(lo, w, hi.bitcast(F32), ALU.subtract))
                up_split_c.wait(g_, b, 2)

            def pool(self, g_):
                for b in range(self.lead):
                    self.pool_prep(g_, b)
                g_.wait_ge(x_done.sem, B * self.ph)
                self.pool_keys(g_, 0, 0)
                self.pool_keys(g_, 0, 1)

                def body(b):
                    for g in range(self.ng):
                        if g == 0:
                            self.pool_prep(g_, b + self.lead)
                            if self.next_exists(b + 2):
                                ln_rstd(g_, b + 2 - B, self.next[0])
                        self.pool_keys(g_, b, g + 2)
                        if g == 1 and self.kind == 0:
                            self.pool_split_up(g_, b)

                batches(g_, body, self.lead)

        att0, att1 = Att(0), Att(1)

        col = lambda ap: ap.rearrange("(p a) -> p a", a=1)

        @block.sync
        def _(sp):
            def load(dst, src, s, scattered=False):
                sp.dma_start(dst, src, allow_slow_non_contiguous=scattered).then_inc(s, 16)

            xin = I["L0_attn_x"].rearrange("b (t p) d -> p (b t) d", p=P)
            xf = x[:].rearrange("p b t d -> p (b t) d")
            load(xf[:, 0:4], xin[:, 0:4], x_in)
            load(xf[:, 4:], xin[:, 4:], x_in)
            load(wr0[:], I["L0_ffn_Wr"], w0_in)
            load(rb0[:], I["L0_ffn_router_bias"].partition_broadcast(P), w0_in)
            load(wg0[:], I["L0_ffn_Wg"].rearrange("e h i -> h e i"), w0_in)
            load(wu0[:], I["L0_ffn_Wu"].rearrange("e h i -> h e i"), w0_in)
            load(cw0[:], I["L0_ffn_conv_w"].rearrange("k a h -> h (k a)"), w0_in, True)
            load(cb0[:], col(I["L0_ffn_conv_b"]), w0_in)
            for e in range(2):
                load(wd0[e * IM0:(e + 1) * IM0], I["L0_ffn_Wd"].rearrange("(j e) i h -> e i j h", e=2)[e], w0_in)
            load(wqkv[:], I["L0_attn_w_qkv"], att0_in)
            load(gam[:], col(I["L0_attn_ln_gamma"]), att0_in)
            load(bet[:], col(I["L0_attn_ln_beta"]), att0_in)
            bqkv = I["L0_attn_b_qkv"].rearrange("(s g r) -> s r g", s=3, g=4)
            for c in range(4):
                load(bq4[32 * c:32 * c + 32], bqkv[0], att0_in, True)
                load(bk4[32 * c:32 * c + 32], bqkv[1], att0_in, True)
            load(bvr[:], I["L0_attn_b_qkv"][2 * D:3 * D].partition_broadcast(P), att0_in)
            load(wo0[:], I["L0_attn_w_out"], att0_in)
            load(bo0[:], I["L0_attn_b_out"].partition_broadcast(P), att0_in)
            load(wr1t[:], I["L1_ffn_router_w"], att0_in)
            load(cb1[:], I["L1_ffn_correction_bias"].partition_broadcast(P), att0_in)
            for dst, w, bias in ((uq, "W_UQ", "b_UQ"), (uk, "W_UK", "b_UK"), (uv, "W_UV", "b_UV")):
                load(dst[0:DC], I[f"L1_attn_{w}"], pre1_in)
                load(dst[DC:DC + 1], I[f"L1_attn_{bias}"].rearrange("(a n) -> a n", a=1), pre1_in)
            load(qr[0:DC], I["L1_attn_W_QR"].rearrange("c (h r) -> c h r", h=H1), pre1_in)
            load(qr[DC:DC + 1], I["L1_attn_b_QR"].rearrange("(a h r) -> a h r", a=1, h=H1), pre1_in)
            load(wo1[:], I["L1_attn_W_O"].rearrange("(h d) n -> d h n", h=H1), pre1_in)
            load(wdq[:], I["L1_attn_W_DQ"], pre1_in)
            load(bdq[:], col(I["L1_attn_b_DQ"]), pre1_in)
            for c in range(2):
                load(wkk[:, c, 0:DC], I["L1_attn_W_DKV"], pre1_in)
                load(wkk[:, c, DC:], I["L1_attn_W_KR"], pre1_in)
                load(bkk[64 * c:64 * c + DC], col(I["L1_attn_b_DKV"]), pre1_in)
                load(bkk[64 * c + DC:64 * c + 64], col(I["L1_attn_b_KR"]), pre1_in)
            load(bdkvr[:], I["L1_attn_b_DKV"].partition_broadcast(P), pre1_in)
            load(bo1r[:], I["L1_attn_b_O"].partition_broadcast(P), pre1_in)
            load(wup, I["L1_ffn_up_w"].rearrange("e h i -> h e i"), moe_in)
            load(wsu, I["L1_ffn_shared_up_w"], moe_in)
            sp.wait_ge(wsu_split, 2)
            load(wsd[:], I["L1_ffn_shared_down_w"].rearrange("(s p) h -> p s h", p=P), down_in)
            sp.wait_ge(up_split_c.sem, 2 * B)
            for e in range(2):
                load(wdn[e * IM1:(e + 1) * IM1], I["L1_ffn_down_w"].rearrange("(j e) i h -> e i j h", e=2)[e], down_in)
            outv = out.rearrange("b (t p) d -> b p t d", p=P)
            with sp.Fori(0, B) as b:
                sp.wait_ge(x_done.sem, b + (B * 5 + 1))
                sp.dma_start(outv[b], x[:, b]).then_inc(stored, 16)
            sp.wait_ge(stored, 16 * B)

        LOADS = {"w0": 8, "att0": 3 + 8 + 5, "pre1": 6 + 2 + 3 + 8 + 2, "moe": 2, "down": 3}

        @block.gpsimd
        def _(g):
            g.memset(ident[:], 0.0).then_inc(const_pool, 1)
            g.wait_ge(const_pool, 1)
            g.affine_select(out=ident[:], in_=ident[:], compare_op=ALU.not_equal, fill=1.0, base=0,
                            pattern=[[-1, P]], channel_multiplier=1).then_inc(const_pool, 1)
            g.memset(neghalf[:], -0.5).then_inc(const_pool, 1)
            g.memset(eps2[:], LN_EPS).then_inc(const_pool, 1)
            g.wait_ge(const_pool, 4)

            def rstd_loop(ph, first=0):
                for b in range(first, 2):
                    ln_rstd(g, b, ph)
                with g.Fori(2, B) as b:
                    ln_rstd(g, b, ph)

            def one_row():
                rstd_c.at(B * 3).wait(g, B - 1, 1)
                g.memset(cq[DC:DC + 1], 1.0).then_inc(cq_one, 1)
                g.wait_ge(cq_one, 1)

            rstd_loop(0)
            g.wait_ge(att0_in, 16 * LOADS["att0"])
            g.wait_ge(moe_in, 16 * LOADS["moe"])
            att0.pool(g)
            rstd_loop(2, 2)
            rstd_loop(3)
            one_row()
            g.wait_ge(pre_done, 1)
            att1.pool(g)
            rstd_loop(5, 1)

        @block.tensor
        def _(pe):
            pe.wait_ge(ready0, 1)
            pe.wait_ge(w0_in, 16 * LOADS["w0"])

            def attention_weights():
                pe.wait_ge(x_done.sem, B)
                pe.wait_ge(pre1_in, 16 * LOADS["pre1"])
                pe.wait_ge(att0_in, 16 * LOADS["att0"])
                for i, w in enumerate((uq, uk, uv)):
                    for h in range(H1):
                        ins = pe.transpose(bank[i][:, h * (DC + 1):(h + 1) * (DC + 1)], w[:, h * DK:(h + 1) * DK],
                                           ident[0:DC + 1, 0:DC + 1])
                    ins.then_inc(pre_tr, 1)
                pe.transpose(bank[6][:, 0:E1], wr1t[:], ident[0:E1, 0:E1]).then_inc(pre_tr, 1)
                pe.wait_ge(pre_ev, 4)
                for h in range(H1):
                    ins = pe.matmul(bank[3][0:DC + 1, h * (DC + 1):(h + 1) * (DC + 1)], uqt[:, h, :], ukt[:, h, :],
                                    start=True, stop=True)
                ins.then_inc(pre_mm, 1)
                for h in range(H1):
                    blk, j = h // 4, h % 4
                    ins = pe.matmul(bank[4][32 * j:32 * j + 32, blk * D:(blk + 1) * D], uvt[:, h, 0:DC], wo1[:, h, :],
                                    start=True, stop=True, tile_position=(0, 32 * j))
                ins.then_inc(pre_mm, 1)
                for h in range(H1):
                    ins = pe.matmul(bank[5][:, 0:D], bvb[:, h, :], wo1[:, h, :], start=(h == 0), stop=(h == H1 - 1))
                ins.then_inc(pre_mm, 1)
                pe.wait_ge(pre_done, 1)

            f0_pe(pe, 0, 0, att0)
            attention_weights()
            att0.pe(pe)
            f0_pe(pe, 2, 1, F1)
            pe.wait_ge(down_in, 16 * LOADS["down"])
            pe.wait_ge(up_split_c.sem, 2 * B)
            f1_pe(pe, 3, 0, att1)
            att1.pe(pe)
            f1_pe(pe, 5, 1, None)

        @block.scalar
        def _(a):
            a.wait_ge(ready0, 1)
            f0_act(a, 0, 0, att0)
            a.wait_ge(pre_done, 1)
            att0.act(a)
            f0_act(a, 2, 1, F1)
            f1_act(a, 3, 0, att1)
            att1.act(a)
            f1_act(a, 5, 1, None)

        @block.vector
        def _(v):
            v.memset(xt[:, :, 0:TAPS - 1], 0.0).then_inc(const_dve, 1)
            v.memset(pad16[:], PAD_LOW).then_inc(const_dve, 1)
            v.memset(want8[:], PAD_LOW).then_inc(const_dve, 1)
            v.memset(want8g[:], PAD_LOW).then_inc(const_dve, 1)
            v.memset(cc[:].bitcast(F32), 0.0).then_inc(const_dve, 1)
            v.memset(mt[:].bitcast(F32), 0.0).then_inc(const_dve, 1)
            v.memset(a1[:], 0.0).then_inc(const_dve, 1)
            v.memset(acol[:], 0.0).then_inc(const_dve, 1)
            v.memset(v0[:, :, :, :, DH0:], 1.0).then_inc(const_dve, 1)
            v.memset(v1[:, :, :, DC:], 1.0).then_inc(const_dve, 1)
            v.memset(cqs[:], 0.0).then_inc(const_dve, 1)
            v.wait_ge(const_pool, 4)
            v.tensor_tensor(sel_small[:], ident[:, 0:64], ident[:, 64:128], ALU.add).then_inc(const_dve, 1)
            v.wait_ge(const_dve, 12)
            v.memset(cqs[DC:DC + 1], 1.0).then_inc(const_dve, 1)
            v.tensor_copy(sel_exp[:], sel_small[:].unsqueeze(2).broadcast_to([P, 64, 64])).then_inc(const_dve, 1)
            v.wait_ge(w0_in, 16 * LOADS["w0"])
            v.wait_ge(x_in, 32)
            v.wait_ge(const_dve, 14)
            v.memset(rz[:], 0.0).then_inc(ready0, 1)
            v.wait_ge(ready0, 1)

            def attention_weights():
                v.wait_ge(x_done.sem, B)
                v.tensor_reduce(head_mask[:], ident[:].rearrange("p (c j d) -> p j c d", c=4, j=4), AX.XY,
                                ALU.add).then_inc(const_dve, 1)
                v.tensor_tensor(rz[:, 0:4], ident[:, 0:4], ident[:, 32:36], ALU.add).then_inc(const_dve, 1)
                v.wait_ge(const_dve, 16)
                v.tensor_copy(sel_row[:], rz[:, 0:4].unsqueeze(2).broadcast_to([P, 4, P])).then_inc(const_dve, 1)
                v.wait_ge(att0_in, 16 * LOADS["att0"])
                for dst, o in ((wq4, 0), (wk4, D)):
                    v.tensor_copy(dst[:], wqkv[:, o:o + D].rearrange("p (g r) -> p g r", g=4).unsqueeze(2)
                                  .broadcast_to([P, 4, 4, 32])).then_inc(const_dve, 1)
                v.wait_ge(pre1_in, 16 * LOADS["pre1"])
                v.wait_ge(pre_tr, 4)
                for i, dst in enumerate((uqt, ukt, uvt)):
                    v.tensor_copy(dst[:], bank[i][:, 0:H1 * (DC + 1)].rearrange("p (h c) -> p h c",
                                                                                h=H1)).then_inc(const_dve, 1)
                v.tensor_copy(wr1[:], bank[6][:, 0:E1]).then_inc(const_dve, 1)
                v.wait_ge(moe_in, 16 * LOADS["moe"])
                v.tensor_copy(wsu_hi[:], wsu).then_inc(wsu_split, 1)
                v.wait_ge(wsu_split, 1)
                v.tensor_tensor(wsu_lo[:], wsu, wsu_hi[:].bitcast(F32), ALU.subtract).then_inc(wsu_split, 1)
                v.wait_ge(const_dve, 23)
                v.tensor_copy(bvb, uvt[:, :, DC:DC + 1].broadcast_to([P, H1, P])).then_inc(pre_ev, 4)
                v.wait_ge(pre_mm, 1)
                m = bank[3][0:DC + 1, 0:H1 * (DC + 1)].rearrange("p (h c) -> p h c", h=H1)
                for c in range(2):
                    v.tensor_copy(a1[0:DC + 1, :, c, 0:DC], m[:, :, 0:DC]).then_inc(const_dve, 1)
                    v.tensor_copy(a1[0:DC + 1, :, c, DC:], qr[:]).then_inc(const_dve, 1)
                v.tensor_copy(acol[0:DC + 1, :], m[:, :, DC]).then_inc(const_dve, 1)
                v.wait_ge(pre_mm, 2)
                v.tensor_copy(vo1[:], bank[4][:, 0:2 * D].rearrange("p (b n) -> p b n", b=2)).then_inc(const_dve, 1)
                v.wait_ge(pre_mm, 3)
                v.tensor_tensor(bo1[:], bank[5][:, 0:D], bo1r[:], ALU.add).then_inc(const_dve, 1)
                v.wait_ge(const_dve, 30)
                v.wait_ge(wsu_split, 2)
                v.memset(rz[:], 0.0).then_inc(pre_done, 1)
                v.wait_ge(pre_done, 1)

            f0_dve(v, 0, 0, att0)
            attention_weights()
            att0.dve(v)
            f0_dve(v, 2, 1, F1)
            f1_dve(v, 3, 0, att1)
            att1.dve(v)
            f1_dve(v, 5, 1, None)


_INS = ['L0_attn_x', 'L0_attn_ln_gamma', 'L0_attn_ln_beta', 'L0_attn_w_qkv', 'L0_attn_b_qkv', 'L0_attn_w_out',
        'L0_attn_b_out', 'L0_ffn_Wr', 'L0_ffn_router_bias', 'L0_ffn_Wg', 'L0_ffn_Wu', 'L0_ffn_Wd', 'L0_ffn_conv_w',
        'L0_ffn_conv_b', 'L1_attn_W_DQ', 'L1_attn_b_DQ', 'L1_attn_W_UQ', 'L1_attn_b_UQ', 'L1_attn_W_DKV',
        'L1_attn_b_DKV', 'L1_attn_W_UK', 'L1_attn_b_UK', 'L1_attn_W_UV', 'L1_attn_b_UV', 'L1_attn_W_QR',
        'L1_attn_b_QR', 'L1_attn_W_KR', 'L1_attn_b_KR', 'L1_attn_W_O', 'L1_attn_b_O', 'L1_ffn_router_w',
        'L1_ffn_correction_bias', 'L1_ffn_up_w', 'L1_ffn_down_w', 'L1_ffn_shared_up_w', 'L1_ffn_shared_down_w']


def kernel(**inputs):
    import numpy as _np
    import concourse.bacc as _bacc
    from concourse import mybir as _mybir
    from concourse.bass_utils import run_bass_kernel_spmd as _run

    nc = _bacc.Bacc("TRN2", target_bir_lowering=False, num_devices=1)
    arrays, aps = {}, {}
    for name in _INS:
        a = _np.ascontiguousarray(inputs[name])
        arrays[f"in_{name}"] = a
        aps[name] = nc.dram_tensor(f"in_{name}", a.shape, _mybir.dt.from_np(a.dtype), kind="ExternalInput").ap()
    shape = inputs["L0_attn_x"].shape
    out = nc.dram_tensor("out_0", shape, _mybir.dt.from_np(_np.dtype("float32")), kind="ExternalOutput").ap()
    macaron_kernel(nc, aps, out)
    r = _run(nc, [arrays], core_ids=[0])
    return r.results[0]["out_0"]
```
